# Optimizing a Trainium2 kernel written in Bass

```python
import numpy as np
import jax
import jax.numpy as jnp

def _softmax(x, axis=-1):
    return jax.nn.softmax(x, axis=axis)

def _gelu(x):
    return jax.nn.gelu(x, approximate=True)

def _silu(x):
    return jax.nn.silu(x)

def _sigmoid(x):
    return jax.nn.sigmoid(x)

def _layernorm(x, axis=-1, eps=1e-05):
    m = jnp.mean(x, axis=axis, keepdims=True)
    v = jnp.var(x, axis=axis, keepdims=True)
    return (x - m) / jnp.sqrt(v + eps)

def _scatter_add(tgt, idx, src, axis=0):
    return tgt.at[idx].add(src)

def _segment_sum(src, seg, n):
    return jax.ops.segment_sum(src, seg, n)
kernel_name = 'mk_seq_preln_d2_jaxref_r8_6f1332'

def setup_inputs(seed: int=0):
    np.random.seed(seed)
    _w = jnp.asarray

    def _L0_attn_setup():
        import jax, jax.numpy as jnp
        import numpy as np
        N_HEADS = 1
        LATENT_DIM = 128
        SCALE = 1.0 / float(np.sqrt(LATENT_DIM * N_HEADS))
        key = jax.random.key(seed)
        kx, kq, ko = jax.random.split(key, 3)
        B, S, D = (4, 512, 128)
        x = jax.random.normal(kx, (B, S, D), dtype=jnp.float32)
        w_qkv = jax.random.normal(kq, (3 * N_HEADS * (LATENT_DIM // N_HEADS), D), dtype=jnp.float32) * 0.02
        w_o = jax.random.normal(ko, (LATENT_DIM, N_HEADS * (LATENT_DIM // N_HEADS)), dtype=jnp.float32) * 0.02
        return {'x': x, 'w_qkv': w_qkv, 'w_o': w_o}
    _L0_attn_in = _L0_attn_setup()

    def _L0_ffn_setup():
        import jax, jax.numpy as jnp
        import numpy as np
        from jax import lax
        T, B, I, M, O = (32, 64, 128, 128, 128)

        def _xavier(key, shape):
            fan_out, fan_in = shape
            limit = float(np.sqrt(6.0 / (fan_in + fan_out)))
            return jax.random.uniform(key, shape, jnp.float32, -limit, limit)
        key = jax.random.key(seed)
        ks = jax.random.split(key, 9)
        x = jax.random.normal(ks[0], (T, B, I), jnp.float32)
        return {'x': x, 'wf': _xavier(ks[1], (M, I)), 'uf': _xavier(ks[2], (M, M)), 'bf': jnp.zeros((M,), jnp.float32), 'wi': _xavier(ks[3], (M, I)), 'ui': _xavier(ks[4], (M, M)), 'bi': jnp.zeros((M,), jnp.float32), 'wc': _xavier(ks[5], (M, I)), 'uc': _xavier(ks[6], (M, M)), 'bc': jnp.zeros((M,), jnp.float32), 'wo': _xavier(ks[7], (O, I)), 'uo': _xavier(ks[8], (O, M)), 'bo': jnp.zeros((O,), jnp.float32), 'in_c': jnp.zeros((M,), jnp.float32)}
    _L0_ffn_in = _L0_ffn_setup()

    def _L1_attn_setup():
        import jax, jax.numpy as jnp
        import numpy as np
        EPS = float(np.finfo(np.float32).eps)
        SEQ_LEN = 256
        NUM_HEADS = 16
        DIM_EMB = 128
        DIM_HEAD = DIM_EMB // NUM_HEADS
        DIM_K = DIM_EMB
        BATCH = 2

        def cosine_positional_encoding(seq_len, dim):
            idx = jnp.arange(seq_len, dtype=jnp.float32)
            scale = 1.0 / (10000.0 ** (jnp.arange(0, dim, 2, dtype=jnp.float32) / dim) + EPS)
            ang = idx[:, None] * scale[None, :]
            return jnp.stack([jnp.sin(ang), jnp.cos(ang)], axis=-1).reshape(seq_len, dim)
        key = jax.random.key(seed)
        ks = jax.random.split(key, 5)
        s = DIM_EMB ** (-0.5)
        return {'x': jax.random.normal(ks[0], (BATCH, SEQ_LEN, DIM_EMB), dtype=jnp.float32), 'Wq': jax.random.normal(ks[1], (DIM_EMB, DIM_EMB), dtype=jnp.float32) * s, 'Wk': jax.random.normal(ks[2], (DIM_EMB, DIM_EMB), dtype=jnp.float32) * s, 'Wv': jax.random.normal(ks[3], (DIM_EMB, DIM_EMB), dtype=jnp.float32) * s, 'Wo': jax.random.normal(ks[4], (DIM_EMB, DIM_EMB), dtype=jnp.float32) * s}
    _L1_attn_in = _L1_attn_setup()

    def _L1_ffn_setup():
        import jax, jax.numpy as jnp
        import numpy as np
        B, S, H = (2, 256, 128)
        E, F, K = (64, 64, 8)
        G, TG = (8, 4)
        SCALE = 2.5
        F_SH = 64

        def _gate(x, gate_w, gate_bias):
            scores = jax.nn.sigmoid(x @ gate_w.T)
            sc = scores + gate_bias[None, :]
            T = x.shape[0]
            group_scores = jax.lax.top_k(sc.reshape(T, G, E // G), 2)[0].sum(-1)
            _, gidx = jax.lax.top_k(group_scores, TG)
            gmask = jnp.zeros((T, G), sc.dtype).at[jnp.arange(T)[:, None], gidx].set(1.0)
            smask = jnp.repeat(gmask, E // G, axis=1)
            masked = jnp.where(smask > 0, sc, -jnp.inf)
            _, tidx = jax.lax.top_k(masked, K)
            tw = jnp.take_along_axis(scores, tidx, axis=1)
            tw = tw / (tw.sum(-1, keepdims=True) + 1e-20)
            return (tidx, tw * SCALE)
        key = jax.random.key(seed)
        ks = jax.random.split(key, 9)

        def w(k, shape, fan_in):
            return jax.random.normal(k, shape, jnp.float32) / np.float32(np.sqrt(fan_in))
        return {'hidden_states': jax.random.normal(ks[0], (B, S, H), jnp.float32), 'gate_w': w(ks[1], (E, H), H), 'gate_bias': jax.random.normal(ks[2], (E,), jnp.float32) * 0.01, 'We_gate': w(ks[3], (E, H, F), H), 'We_up': w(ks[4], (E, H, F), H), 'We_down': w(ks[5], (E, F, H), F), 'Ws_gate': w(ks[6], (H, F_SH), H), 'Ws_up': w(ks[7], (H, F_SH), H), 'Ws_down': w(ks[8], (F_SH, H), F_SH)}
    _L1_ffn_in = _L1_ffn_setup()
    _d = {'L0_attn_x': _L0_attn_in['x'], 'L0_attn_w_qkv': _L0_attn_in['w_qkv'], 'L0_attn_w_o': _L0_attn_in['w_o'], 'L0_ffn_wf': _L0_ffn_in['wf'], 'L0_ffn_uf': _L0_ffn_in['uf'], 'L0_ffn_bf': _L0_ffn_in['bf'], 'L0_ffn_wi': _L0_ffn_in['wi'], 'L0_ffn_ui': _L0_ffn_in['ui'], 'L0_ffn_bi': _L0_ffn_in['bi'], 'L0_ffn_wc': _L0_ffn_in['wc'], 'L0_ffn_uc': _L0_ffn_in['uc'], 'L0_ffn_bc': _L0_ffn_in['bc'], 'L0_ffn_wo': _L0_ffn_in['wo'], 'L0_ffn_uo': _L0_ffn_in['uo'], 'L0_ffn_bo': _L0_ffn_in['bo'], 'L0_ffn_in_c': _L0_ffn_in['in_c'], 'L1_attn_Wq': _L1_attn_in['Wq'], 'L1_attn_Wk': _L1_attn_in['Wk'], 'L1_attn_Wv': _L1_attn_in['Wv'], 'L1_attn_Wo': _L1_attn_in['Wo'], 'L1_ffn_gate_w': _L1_ffn_in['gate_w'], 'L1_ffn_gate_bias': _L1_ffn_in['gate_bias'], 'L1_ffn_We_gate': _L1_ffn_in['We_gate'], 'L1_ffn_We_up': _L1_ffn_in['We_up'], 'L1_ffn_We_down': _L1_ffn_in['We_down'], 'L1_ffn_Ws_gate': _L1_ffn_in['Ws_gate'], 'L1_ffn_Ws_up': _L1_ffn_in['Ws_up'], 'L1_ffn_Ws_down': _L1_ffn_in['Ws_down']}
    _x0 = _d['L0_attn_x']
    _d['L0_attn_x'] = jax.random.normal(jax.random.fold_in(jax.random.key(seed), 1), (16, 256, 128), dtype=_x0.dtype)
    del _x0
    return _d

def reference(L0_attn_x, L0_attn_w_qkv, L0_attn_w_o, L0_ffn_wf, L0_ffn_uf, L0_ffn_bf, L0_ffn_wi, L0_ffn_ui, L0_ffn_bi, L0_ffn_wc, L0_ffn_uc, L0_ffn_bc, L0_ffn_wo, L0_ffn_uo, L0_ffn_bo, L0_ffn_in_c, L1_attn_Wq, L1_attn_Wk, L1_attn_Wv, L1_attn_Wo, L1_ffn_gate_w, L1_ffn_gate_bias, L1_ffn_We_gate, L1_ffn_We_up, L1_ffn_We_down, L1_ffn_Ws_gate, L1_ffn_Ws_up, L1_ffn_Ws_down):

    def _L0_attn_ref(x, w_qkv, w_o):
        import jax, jax.numpy as jnp
        import numpy as np
        N_HEADS = 1
        LATENT_DIM = 128
        SCALE = 1.0 / float(np.sqrt(LATENT_DIM * N_HEADS))
        B, S, _ = x.shape
        qkv = jnp.einsum('bsd,fd->bsf', x, w_qkv)
        qkv = qkv.reshape(B, S, N_HEADS, 3 * LATENT_DIM).transpose(0, 2, 1, 3)
        q, k, v = jnp.split(qkv, 3, axis=-1)
        attn_logits = jnp.einsum('bhqd,bhkd->bhqk', q, k) * SCALE
        attention = jax.nn.softmax(attn_logits, axis=1)
        values = jnp.einsum('bhqk,bhkd->bhqd', attention, v)
        values = values.transpose(0, 2, 1, 3).reshape(B, S, N_HEADS * LATENT_DIM)
        return jnp.einsum('bsf,of->bso', values, w_o)

    def _L0_ffn_ref(x, wf, uf, bf, wi, ui, bi, wc, uc, bc, wo, uo, bo, in_c):
        import jax, jax.numpy as jnp
        import numpy as np
        from jax import lax
        T, B, I, M, O = (32, 64, 128, 128, 128)

        def _xavier(key, shape):
            fan_out, fan_in = shape
            limit = float(np.sqrt(6.0 / (fan_in + fan_out)))
            return jax.random.uniform(key, shape, jnp.float32, -limit, limit)
        batch = x.shape[1]
        c0 = jnp.broadcast_to(in_c, (batch, in_c.shape[0]))

        def step(c, xt):
            ft = jax.nn.sigmoid(xt @ wf.T + c @ uf.T + bf)
            it = jax.nn.sigmoid(xt @ wi.T + c @ ui.T + bi)
            gt = jnp.tanh(xt @ wc.T + c @ uc.T + bc)
            c = ft * c + it * gt
            return (c, None)
        c_final, _ = lax.scan(step, c0, x)
        h = jnp.tanh(jnp.einsum('tbi,oi->tbo', x, wo) + c_final @ uo.T + bo)
        return h

    def _L1_attn_ref(x, Wq, Wk, Wv, Wo):
        import jax, jax.numpy as jnp
        import numpy as np
        EPS = float(np.finfo(np.float32).eps)
        SEQ_LEN = 256
        NUM_HEADS = 16
        DIM_EMB = 128
        DIM_HEAD = DIM_EMB // NUM_HEADS
        DIM_K = DIM_EMB
        BATCH = 2

        def cosine_positional_encoding(seq_len, dim):
            idx = jnp.arange(seq_len, dtype=jnp.float32)
            scale = 1.0 / (10000.0 ** (jnp.arange(0, dim, 2, dtype=jnp.float32) / dim) + EPS)
            ang = idx[:, None] * scale[None, :]
            return jnp.stack([jnp.sin(ang), jnp.cos(ang)], axis=-1).reshape(seq_len, dim)
        B, S, E = x.shape
        pos = cosine_positional_encoding(S, DIM_HEAD)

        def split_heads(t):
            return t.reshape(B, S, NUM_HEADS, DIM_HEAD).transpose(0, 2, 1, 3)
        q = split_heads(x @ Wq) + pos[None, None]
        k = split_heads(x @ Wk) + pos[None, None]
        v = split_heads(x @ Wv)
        scores = jnp.einsum('bhqd,bhkd->bhqk', q, k) * DIM_K ** (-0.5)
        causal_mask = jnp.triu(jnp.ones((S, S), dtype=bool), k=1)
        m_inf = -jnp.finfo(scores.dtype).max
        scores = jnp.where(causal_mask[None, None], m_inf, scores)
        attn = jax.nn.softmax(scores, axis=-1)
        out = jnp.einsum('bhqk,bhkd->bhqd', attn, v)
        out = out.transpose(0, 2, 1, 3).reshape(B, S, E)
        return out @ Wo

    def _L1_ffn_ref(hidden_states, gate_w, gate_bias, We_gate, We_up, We_down, Ws_gate, Ws_up, Ws_down):
        import jax, jax.numpy as jnp
        import numpy as np
        B, S, H = (2, 256, 128)
        E, F, K = (64, 64, 8)
        G, TG = (8, 4)
        SCALE = 2.5
        F_SH = 64

        def _gate(x, gate_w, gate_bias):
            scores = jax.nn.sigmoid(x @ gate_w.T)
            sc = scores + gate_bias[None, :]
            T = x.shape[0]
            group_scores = jax.lax.top_k(sc.reshape(T, G, E // G), 2)[0].sum(-1)
            _, gidx = jax.lax.top_k(group_scores, TG)
            gmask = jnp.zeros((T, G), sc.dtype).at[jnp.arange(T)[:, None], gidx].set(1.0)
            smask = jnp.repeat(gmask, E // G, axis=1)
            masked = jnp.where(smask > 0, sc, -jnp.inf)
            _, tidx = jax.lax.top_k(masked, K)
            tw = jnp.take_along_axis(scores, tidx, axis=1)
            tw = tw / (tw.sum(-1, keepdims=True) + 1e-20)
            return (tidx, tw * SCALE)
        b, s, h = hidden_states.shape
        x = hidden_states.reshape(-1, h).astype(jnp.float32)
        tidx, tw = _gate(x, gate_w, gate_bias)
        T = x.shape[0]
        w_dense = jnp.zeros((T, E), tw.dtype).at[jnp.arange(T)[:, None], tidx].add(tw)

        def body(acc, ws):
            wg, wu, wdn, cw = ws
            hmid = jax.nn.silu(x @ wg) * (x @ wu)
            return (acc + cw[:, None] * (hmid @ wdn), None)
        y, _ = jax.lax.scan(body, jnp.zeros_like(x), (We_gate, We_up, We_down, w_dense.T))
        y = y.reshape(b, s, h)
        shared = jax.nn.silu(hidden_states @ Ws_gate) * (hidden_states @ Ws_up) @ Ws_down
        return y + shared
    x = L0_attn_x
    x = x + _L0_attn_ref(_layernorm(x, axis=-1), L0_attn_w_qkv, L0_attn_w_o)
    x = x + _L0_ffn_ref(_layernorm(x, axis=-1), L0_ffn_wf, L0_ffn_uf, L0_ffn_bf, L0_ffn_wi, L0_ffn_ui, L0_ffn_bi, L0_ffn_wc, L0_ffn_uc, L0_ffn_bc, L0_ffn_wo, L0_ffn_uo, L0_ffn_bo, L0_ffn_in_c)
    x = x + _L1_attn_ref(_layernorm(x, axis=-1), L1_attn_Wq, L1_attn_Wk, L1_attn_Wv, L1_attn_Wo)
    x = x + _L1_ffn_ref(_layernorm(x, axis=-1), L1_ffn_gate_w, L1_ffn_gate_bias, L1_ffn_We_gate, L1_ffn_We_up, L1_ffn_We_down, L1_ffn_Ws_gate, L1_ffn_Ws_up, L1_ffn_Ws_down)
    return x

_drawn_inputs = setup_inputs


def setup_inputs(seed=0):
    import zlib

    import numpy as np

    out = dict(_drawn_inputs(seed))
    spreads = {'L0_ffn_bf': (0.0, 0.1),
     'L0_ffn_bi': (0.0, 0.1),
     'L0_ffn_bc': (0.0, 0.1),
     'L0_ffn_bo': (0.0, 0.1),
     'L0_ffn_in_c': (0.0, 0.519)}
    factors = {}
    for name, (base, spread) in spreads.items():
        noise = np.random.default_rng([zlib.crc32(name.encode()), seed]).standard_normal(out[name].shape)
        drawn = base * np.exp(spread * noise) if base else spread * noise
        out[name] = jnp.asarray(drawn.astype(out[name].dtype))
    for name, factor in factors.items():
        out[name] = (out[name] * factor).astype(out[name].dtype)
    return out
```

```python
import concourse.bass as bass
from concourse import mybir
from concourse.alu_op_type import AluOpType as ALU
from contextlib import ExitStack

F32 = mybir.dt.float32
F32R = mybir.dt.float32r
BF16 = mybir.dt.bfloat16
F16 = mybir.dt.float16
ACT = mybir.ActivationFunctionType
AX = mybir.AxisListType

P = 128
B, S, D = 16, 256, 128
TILES = B * S // P
HEADS, HD = 16, 8
GROUPS = 4
NE, FF = 64, 64
PAIRS = NE // 2
UNITS = PAIRS + 1
STAGE_UNITS = 3
CHUNK = 512
CHUNKS = B * S // CHUNK
EPS = 1e-5
STATS = TILES + 6
BIG = 3e38
SCALE = float(D) ** -0.5
ROUTED_SCALE = 2.5
LOW = 4096.0

WF, WI, WC, WO, WV1, GW, WV0, WO0, UF, UI, UC, UO, WO1, WQ, WK = range(15)
SPLIT = 6
C_ID, C_POS, C_QLO, C_KLO, C_TRI, C_END = 0, 128, 640, 641, 642, 706


def begins(b):
    return isinstance(b, int) and b == 0


class Chain:

    def __init__(self, eng, sem):
        self.eng, self.sem, self.base, self.n = eng, sem, 0, 0

    def at(self, base):
        self.base, self.n = base, 0

    def did(self, ins):
        ins.then_inc(self.sem, 1)
        self.n += 1

    def settle(self, back=0):
        self.eng.wait_ge(self.sem, self.base + self.n - back)


def two_layers(nc, x, small, vec, gate_bias, gu, wd, cf32, cbf, cf16, out):
    ctx = ExitStack()
    with ctx:
        def sb(name, shape, dt=F32):
            return ctx.enter_context(nc.sbuf_tensor(name, shape, dt))

        def sem(name):
            return ctx.enter_context(nc.semaphore(name))

        X = sb("X", [P, TILES * D])
        YHI = sb("YHI", [P, B * S], F32R)
        YLO = sb("YLO", [P, B * S], F32R)
        GUH = sb("GUH", [P, UNITS * 256], F32R)
        GUL = sb("GUL", [P, UNITS * 256], F32R)
        WD = sb("WD", [P, UNITS * 128])
        W = sb("W", [P, 15 * 128])
        WH = sb("WH", [P, SPLIT * 128], F32R)
        WL = sb("WL", [P, SPLIT * 128], F32R)
        WQK = [[sb(f"W{m}S{part}", [P, HEADS * 32], F32R) for part in "hl"] for m in "qk"]
        VEC = sb("VEC", [P, 5])
        BIAS = sb("BIAS", [P, NE])
        CF = sb("CF", [P, C_END])
        CB = sb("CB", [P, 256], BF16)
        SEL = sb("SEL", [P, PAIRS * 128 + 128], F16)
        CWT = sb("CWT", [P, B * S], F16)
        IDR = sb("IDR", [P, P], F32R)
        ONES = sb("ONES", [P, P])
        EPST = sb("EPST", [P, TILES])
        MV = sb("MV", [P, TILES * 2])
        RS = sb("RS", [P, TILES])
        BN = sb("BN", [P, TILES * 6])
        NMR = sb("NMR", [P, TILES])
        COLS = sb("COLS", [P, 3 * B])
        BUF = sb("BUF", [P, 3072])
        ROT = sb("ROT", [P, 1024])
        VP = sb("VP", [P, 2 * 2 * HEADS * 32])
        US = sb("US", [P, S])
        OH2 = sb("OH2", [P, 2 * D])
        OHS = sb("OHS", [P, 2 * 2 * D])
        OT = sb("OT", [P, S])
        RD = sb("RD", [P, 2 * 4])
        NOTE = sb("NOTE", [P, 1])
        MX = sb("MX", [P, 2 * 4])

        ident = CF[:, C_ID:C_ID + 128]
        pos = CF[:, C_POS:C_POS + 512]
        ident_bf = CB[:, 0:128]
        causal = CB[:, 128:256]
        ident_h = SEL[:, PAIRS * 128:PAIRS * 128 + 128]

        def w(n):
            return W[:, n * 128:(n + 1) * 128]

        def wh(n):
            return WH[:, n * 128:(n + 1) * 128]

        def wl(n):
            return WL[:, n * 128:(n + 1) * 128]

        PA = ctx.enter_context(nc.psum_tensor("PA", [P, 512], F32))
        PS = ctx.enter_context(nc.psum_tensor("PS", [P, 1536], F32))
        PT = ctx.enter_context(nc.psum_tensor("PT", [P, 1536], F32))
        PB = ctx.enter_context(nc.psum_tensor("PB", [P, 512], F32))

        ld_x, ld_w, ld_vec, ld_bias, ld_cf, ld_cb, ld_sel, ld_wd = (
            sem(n) for n in ("ld_x", "ld_w", "ld_vec", "ld_bias", "ld_cf", "ld_cb", "ld_sel", "ld_wd"))
        ld_gu = [sem(f"ld_gu{p}") for p in range(2)]
        gu_split = sem("gu_split")
        consts = sem("consts")
        ident_r = sem("ident_r")
        small_split = sem("small_split")
        qk_split = sem("qk_split")
        stats = [sem(f"stats{n}") for n in "abcd"]
        rstd = [sem(f"rstd{n}") for n in "abcd"]
        rs_add = sem("rs_add")
        a_rows = sem("a_rows")
        a_mm = sem("a_mm")
        a_cp = sem("a_cp")
        x1_done = sem("x1_done")
        norm = [sem(f"norm{n}") for n in "bd"]
        tr = [sem(f"tr{n}") for n in "bd"]
        hi = [sem(f"hi{n}") for n in "bd"]
        lo = [[sem(f"lo{n}{p}") for p in range(2)] for n in "bd"]
        gates = [sem(f"gates{h}") for h in range(2)]
        acts = [sem(f"acts{h}") for h in range(2)]
        cell = [sem(f"cell{h}") for h in range(2)]
        c_init = sem("c_init")
        cu_mm = sem("cu_mm")
        cu_cp = sem("cu_cp")
        ro_mm, ro_add, ro_tanh, ro_tr, ro_x = (sem(n) for n in ("ro_mm", "ro_add", "ro_tanh", "ro_tr", "ro_x"))
        t_norm, t_tr, t_hi, t_lo, v_mm, v_cp = (sem(n) for n in ("t_norm", "t_tr", "t_hi", "t_lo", "v_mm", "v_cp"))
        zeroed = sem("zeroed")
        qk_mm, qk_pos, qk_hi, stack, s_mm, s_max, m_neg, m_tr, q_shift = (
            sem(n) for n in ("qk_mm", "qk_pos", "qk_hi", "stack", "s_mm", "s_max", "m_neg", "m_tr", "q_shift"))
        st_mm, prob, masked, pv_mm, u_cp, u_tr, u_rec, o_norm = (
            sem(n) for n in ("st_mm", "prob", "masked", "pv_mm", "u_cp", "u_tr", "u_rec", "o_norm"))
        o_tr, o_cp, o_mm, x3_done = (sem(n) for n in ("o_tr", "o_cp", "o_mm", "x3_done"))
        g_mm, g_exp, g_tr, g_use, g_chain, g_cw, g_cwtr, g_cwt = (
            sem(n) for n in ("g_mm", "g_exp", "g_tr", "g_use", "g_chain", "g_cw", "g_cwtr", "g_cwt"))
        e_gate, e_up, e_cw, e_silu, e_act, e_prod, e_down = (
            sem(n) for n in ("e_gate", "e_up", "e_cw", "e_silu", "e_act", "e_prod", "e_down"))
        y_cp, y_tr, x4_done, stored = (sem(n) for n in ("y_cp", "y_tr", "x4_done", "stored"))

        KM = [YLO[:, g * 1024:(g + 1) * 1024] for g in range(GROUPS)]
        QS = [YHI[:, g * 256:(g + 1) * 256] for g in range(GROUPS)]
        Q2 = [YHI[:, 1024 + p * 256:1280 + p * 256] for p in range(2)]
        HM = [YHI[:, 1536 + p * 512:2048 + p * 512] for p in range(2)]
        TH = YHI[:, 2560:2816]
        TL = YHI[:, 2816:3072]
        M2 = YHI[:, 3072:3328]
        QKF = [ROT[:, p * 512:(p + 1) * 512] for p in range(2)]
        PR = [BUF[:, p * 1536:(p + 1) * 1536] for p in range(2)]
        VPB = [VP[:, p * 1024:(p + 1) * 1024].rearrange("p (t h c) -> p t h c", t=2, c=32) for p in range(2)]
        YN = [ROT[:, p * 512:(p + 1) * 512] for p in range(2)]
        PAB = [PA, PB]
        OH = [OHS[:, p * 256:(p + 1) * 256] for p in range(2)]
        CST = [COLS[:, n * B:(n + 1) * B] for n in range(3)]
        XV = X[:, :].rearrange("p (t d) -> p t d", d=D)

        GATE = [PS[:, 0:512], PS[:, 512:1024]], [PS[:, 1024:1536], PT[:, 0:512]]
        SG = [VP[:, h * 640:h * 640 + 384] for h in range(2)]
        C = [VP[:, h * 640 + 384:h * 640 + 512] for h in range(2)]
        TMP = [VP[:, h * 640 + 512:h * 640 + 640] for h in range(2)]
        CU = VP[:, 1280:1536]
        CWS = US[:, :].bitcast(F16)
        PTH = PT[:, 0:256].bitcast(F16)
        SIL = [BUF[:, p * 512:(p + 1) * 512] for p in range(2)]
        PRD = [BUF[:, 1024 + p * 512:1536 + p * 512] for p in range(3)]
        ACTV = BUF[:, 2560:3072]
        EG = [PS[:, 0:512], PS[:, 512:1024]]
        EU = [PS[:, 1024:1536], PT[:, 0:512]]
        EC = [PT[:, 512:1024], PT[:, 1024:1536]]
        PY = PB[:, :]

        block = ctx.enter_context(nc.Block())

        def ncols(i, n):
            return bass.ds(i * n, n)

        def normalise_and_lo(dve, k):
            def normalise(G, p):
                for t in range(4):
                    at = 4 * G + t
                    nc.vector.tensor_scalar(YN[p][:, t * 128:(t + 1) * 128], X[:, bass.ds(at * D, D)],
                                            MV[:, bass.ds(at * 2, 1)], RS[:, bass.ds(at, 1)],
                                            ALU.subtract, ALU.mult).then_inc(norm[k], 1)

            def low_part(G, p):
                dve.wait_ge(hi[k], G + 1)
                nc.vector.tensor_tensor(YLO[:, ncols(G, CHUNK)], PAB[p][:, :], YHI[:, ncols(G, CHUNK)],
                                        ALU.subtract).then_inc(lo[k][p], 1)

            normalise(0, 0)
            with dve.Fori(0, CHUNKS // 2 - 1) as i:
                normalise(2 * i + 1, 1)
                low_part(2 * i, 0)
                normalise(2 * i + 2, 0)
                low_part(2 * i + 1, 1)
            normalise(CHUNKS - 1, 1)
            low_part(CHUNKS - 2, 0)
            low_part(CHUNKS - 1, 1)

        def transpose_tiles(pe, k):
            with pe.Fori(0, CHUNKS // 2) as i:
                for p in range(2):
                    pe.wait_ge(lo[k][p], i)
                    pe.wait_ge(norm[k], 4 * (2 * i + p + 1))
                    for t in range(4):
                        ins = nc.tensor.transpose(PAB[p][:, t * 128:(t + 1) * 128], YN[p][:, t * 128:(t + 1) * 128],
                                                  ident)
                    ins.then_inc(tr[k], 1)

        def split_hi(act, k):
            with act.Fori(0, CHUNKS // 2) as i:
                for p in range(2):
                    act.wait_ge(tr[k], 2 * i + p + 1)
                    nc.scalar.activation(YHI[:, ncols(2 * i + p, CHUNK)], PAB[p][:, :], ACT.Copy).then_inc(hi[k], 1)

        @block.sync
        def _(sp):
            sp.dma_start(X[:, :].rearrange("p (b h d) -> p b h d", h=2, d=D),
                         x.rearrange("b (h p) d -> p b h d", p=P)).then_inc(ld_x, 16)
            sp.dma_start(W[:, :], small.rearrange("p k m -> p (k m)")).then_inc(ld_w, 16)
            sp.dma_start(CF[:, :], cf32).then_inc(ld_cf, 16)
            sp.dma_start(VEC[:, :], vec).then_inc(ld_vec, 16)
            sp.dma_start(BIAS[:, :], gate_bias.partition_broadcast(P)).then_inc(ld_bias, 16)
            sp.dma_start(CB[:, :], cbf).then_inc(ld_cb, 16)
            for n in range(UNITS // STAGE_UNITS):
                if n >= 2:
                    sp.wait_ge(gu_split, 2 * (n - 1))
                sp.dma_start(BUF[:, (n % 2) * 1536:(n % 2) * 1536 + STAGE_UNITS * 256],
                             gu[:, n * STAGE_UNITS:(n + 1) * STAGE_UNITS, :].rearrange("p k m -> p (k m)")
                             ).then_inc(ld_gu[n % 2], 16)
            sp.dma_start(SEL[:, :], cf16).then_inc(ld_sel, 16)
            sp.dma_start(WD[:, :], wd.rearrange("p k m -> p (k m)")).then_inc(ld_wd, 16)
            with sp.Fori(0, CHUNKS) as c:
                sp.wait_ge(x4_done, c + 1)
                sp.dma_start(out[bass.ds(c * 2, 2), :, :].rearrange("b (h p) d -> p b h d", p=P),
                             X[:, bass.ds(c * CHUNK, CHUNK)].rearrange("p (b h d) -> p b h d", h=2, d=D)
                             ).then_inc(stored, 16)
            sp.wait_ge(stored, 16 * CHUNKS)

        @block.gpsimd
        def _(pool):
            g = nc.gpsimd
            g.memset(EPST[:, :], -0.5).then_inc(consts, 1)
            g.memset(ONES[:, :], 1.0).then_inc(consts, 1)
            for m in range(2):
                for part in range(2):
                    g.memset(WQK[m][part][:, :].bitcast(F32), 0.0).then_inc(consts, 1)
            pool.wait_ge(ld_w, 16)
            g.tensor_copy(WH[:, :], W[:, 0:SPLIT * 128]).then_inc(small_split, 1)
            pool.wait_ge(small_split, 1)
            g.tensor_tensor(WL[:, :], W[:, 0:SPLIT * 128], WH[:, :], ALU.subtract).then_inc(small_split, 1)

            def rstd_all(k):
                pool.wait_ge(stats[k], STATS)
                g.tensor_scalar(RS[:, :], MV[:, 1:2 * TILES:2], EPS, None, ALU.add).then_inc(rs_add, 1)
                pool.wait_ge(rs_add, k + 1)
                g.tensor_tensor(RS[:, :], RS[:, :], EPST[:, :], ALU.pow).then_inc(rstd[k], 1)

            pool.wait_ge(consts, 6)
            rstd_all(0)
            for m, src in enumerate((WQ, WK)):
                raw = w(src).rearrange("p (h d) -> p h d", d=HD)
                wide = [WQK[m][part][:, :].rearrange("p (h s d) -> p h s d", s=4, d=HD) for part in range(2)]
                for s in (1, 2, 3):
                    g.tensor_copy(wide[0][:, :, s, :], raw).then_inc(qk_split, 1)
                pool.wait_ge(qk_split, 6 * m + 3)
                for s in (1, 2, 3):
                    g.tensor_tensor(wide[1][:, :, s, :], raw, wide[0][:, :, s, :], ALU.subtract).then_inc(qk_split, 1)
            rstd_all(1)
            for n in range(UNITS // STAGE_UNITS):
                cols = slice(n * STAGE_UNITS * 256, (n + 1) * STAGE_UNITS * 256)
                raw = BUF[:, (n % 2) * 1536:(n % 2) * 1536 + STAGE_UNITS * 256]
                pool.wait_ge(ld_gu[n % 2], 16 * (n // 2 + 1))
                g.tensor_copy(GUH[:, cols], raw).then_inc(gu_split, 1)
                pool.wait_ge(gu_split, 2 * n + 1)
                g.tensor_tensor(GUL[:, cols], raw, GUH[:, cols], ALU.subtract).then_inc(gu_split, 1)

            pool.wait_ge(ro_mm, CHUNKS)
            for gr in range(GROUPS):
                g.memset(KM[gr].bitcast(F32), 0.0).then_inc(zeroed, 1)
            g.memset(M2.bitcast(F32), 0.0).then_inc(zeroed, 1)
            pool.wait_ge(ro_add, CHUNKS)
            g.memset(VP[:, :], 0.0).then_inc(zeroed, 1)
            pool.wait_ge(zeroed, 6)
            for p in range(2):
                g.memset(VPB[p][:, :, :, HD:HD + 1], 1.0).then_inc(zeroed, 1)
            rstd_all(2)

            def q_k_stack(b, gr):
                n = b * GROUPS + gr
                pool.wait_ge(qk_hi, 2 * n + 2)
                if not begins(b):
                    pool.wait_ge(st_mm, n - GROUPS + 1)
                    pool.wait_ge(q_shift, n - GROUPS + 1)
                g.tensor_tensor(QS[gr], QKF[gr % 2][:, 0:256], HM[gr % 2][:, 0:256], ALU.subtract).then_inc(stack, 1)
                for j in range(4):
                    rows = slice(32 * j, 32 * j + 32)
                    pool.wait_ge(stack, 5 * n + 1 + j)
                    g.tensor_tensor(KM[gr][rows, j * 256:(j + 1) * 256], QKF[gr % 2][rows, 256:512],
                                    HM[gr % 2][rows, 256:512], ALU.subtract).then_inc(stack, 1)
                pool.wait_ge(stack, 5 * n + 5)

            def causal_select(b, gr):
                n = b * GROUPS + gr
                pool.wait_ge(prob, n + 1)
                first = PR[gr % 2][:, 0:1024].rearrange("p (j q) -> p j q", q=256)[:, :, 0:128]
                second = PR[gr % 2][:, 1024:1536].rearrange("p (j q) -> p j q", q=128)
                pool.wait_ge(masked, 2 * n)
                g.tensor_tensor(NOTE[:, :], ONES[:, 0:1], ONES[:, 0:1], ALU.mult)
                for part in (first, second):
                    g.affine_select(out=part, in_=part, compare_op=ALU.is_ge, fill=0.0, base=0,
                                    pattern=[[0, 4], [1, 128]], channel_multiplier=-1).then_inc(masked, 1)

            def sequence(b, last):
                for gr in range(GROUPS):
                    causal_select(b, gr)
                    if gr == 0:
                        q_k_stack(b, 3)
                    elif not last:
                        q_k_stack(b + 1, gr - 1)

            for gr in range(3):
                q_k_stack(0, gr)
            sequence(0, False)
            with pool.Fori(0, 7) as k:
                sequence(2 * k + 1, False)
                sequence(2 * k + 2, False)
            sequence(15, True)

            rstd_all(3)

        @block.scalar
        def _(act):
            s = nc.scalar
            act.wait_ge(ld_cf, 16)
            s.activation(IDR[:, :], ident, ACT.Copy).then_inc(ident_r, 1)
            act.wait_ge(a_mm, 1)
            s.activation(CST[1], PA[:, 0:B], ACT.Copy).then_inc(a_cp, 1)
            act.wait_ge(a_mm, 2)
            s.activation(CST[2], PB[:, 0:B], ACT.Copy).then_inc(a_cp, 1)
            split_hi(act, 0)

            def scan_step(t, par):
                for h in range(2):
                    act.wait_ge(gates[h], t + 1)
                    for k, (f, bias) in enumerate(((ACT.Tanh, 2), (ACT.Sigmoid, 1), (ACT.Sigmoid, 0))):
                        col = (2, 1, 0)[k] * 128
                        s.activation(SG[h][:, col:col + 128], GATE[h][par][:, col:col + 128], f,
                                     bias=VEC[:, bias:bias + 1]).then_inc(acts[h], 1)

            act.wait_ge(ld_vec, 16)
            with act.Fori(0, B // 2) as k:
                scan_step(2 * k, 0)
                scan_step(2 * k + 1, 1)
            act.wait_ge(cu_mm, 1)
            s.activation(CU, PB[:, 0:256], ACT.Copy).then_inc(cu_cp, 1)
            with act.Fori(0, CHUNKS) as i:
                act.wait_ge(ro_add, i + 1)
                act.wait_ge(ro_tr, i)
                s.activation(ROT[:, 512:1024], ROT[:, 0:512], ACT.Tanh, bias=VEC[:, 3:4]).then_inc(ro_tanh, 1)

            def split_sequence(b):
                act.wait_ge(t_tr, b + 1)
                if not begins(b):
                    act.wait_ge(qk_mm, GROUPS * b)
                s.activation(TH, PB[:, 0:256], ACT.Copy).then_inc(t_hi, 1)

            def values(b, par):
                act.wait_ge(v_mm, b + 1)
                s.activation(VPB[par][:, :, :, 0:HD],
                             PB[:, 0:256].rearrange("p (t h d) -> p t h d", t=2, d=HD), ACT.Copy).then_inc(v_cp, 1)

            def hi_slots(b, gr):
                n = b * GROUPS + gr
                act.wait_ge(qk_pos, n + 1)
                s.activation(HM[gr % 2][:, 0:256], QKF[gr % 2][:, 0:256], ACT.Copy,
                             scale=CF[:, C_QLO:C_QLO + 1]).then_inc(qk_hi, 1)
                s.activation(HM[gr % 2][:, 256:512], QKF[gr % 2][:, 256:512], ACT.Copy,
                             scale=CF[:, C_KLO:C_KLO + 1]).then_inc(qk_hi, 1)

            def u_copy(b, gr):
                n = b * GROUPS + gr
                act.wait_ge(pv_mm, n + 1)
                s.activation(US[:, :], PB[:, 0:256], ACT.Copy).then_inc(u_cp, 1)

            def o_copy(b):
                act.wait_ge(o_tr, b + 1)
                s.activation(OT[:, :], PB[:, 0:256], ACT.Copy).then_inc(o_cp, 1)

            def exps(b, gr):
                n = b * GROUPS + gr
                act.wait_ge(st_mm, n + 1)
                if not begins(b) or gr >= 2:
                    act.wait_ge(pv_mm, n - 1)
                s.activation(PR[gr % 2], PT[:, :], ACT.Exp, scale=SCALE).then_inc(prob, 1)

            def sequence(b, par, first, last):
                for gr in range(GROUPS):
                    if gr >= 2:
                        u_copy(b, gr - 2)
                    elif not first:
                        u_copy(b - 1, gr + 2)
                    if gr == 2 and not first:
                        o_copy(b - 1)
                    exps(b, gr)
                    if gr == 0:
                        hi_slots(b, 3)
                        if not last:
                            split_sequence(b + 1)
                    elif not last:
                        if gr == 1:
                            values(b + 1, 1 - par)
                        hi_slots(b + 1, gr - 1)

            act.wait_ge(zeroed, 8)
            split_sequence(0)
            values(0, 0)
            for gr in range(3):
                hi_slots(0, gr)
            sequence(0, 0, True, False)
            with act.Fori(0, 7) as k:
                sequence(2 * k + 1, 1, False, False)
                sequence(2 * k + 2, 0, False, False)
            sequence(15, 1, False, True)
            u_copy(15, 2)
            u_copy(15, 3)
            o_copy(15)

            split_hi(act, 1)
            with act.Fori(0, CHUNKS) as c:
                act.wait_ge(g_mm, c + 1)
                act.wait_ge(g_tr, c)
                s.activation(ROT[:, 512:1024], PA[:, :], ACT.Exp, scale=-1.0).then_inc(g_exp, 1)
                act.wait_ge(g_cwtr, c + 1)
                s.activation(CWT[:, ncols(c, CHUNK)], PTH[:, 0:CHUNK], ACT.Copy).then_inc(g_cwt, 1)

            with act.Fori(0, CHUNKS) as c:
                for u in range(UNITS):
                    n = c * UNITS + u
                    act.wait_ge(e_gate, n + 1)
                    if u >= 2:
                        act.wait_ge(e_act, c * PAIRS + u - 1)
                    else:
                        act.wait_ge(e_prod, c * UNITS)
                    s.activation(SIL[u % 2], EG[u % 2], ACT.Silu).then_inc(e_silu, 1)
                act.wait_ge(e_down, (c + 1) * UNITS)
                s.activation(ROT[:, 512:1024], PY, ACT.Copy).then_inc(y_cp, 1)

        @block.tensor
        def _(pe):
            mm = nc.tensor.matmul

            def three(out_, wn_h, wn_l, y_h, y_l, start, stop=False, skip=True):
                mm(out_, wn_h, y_h, start=start, stop=False, skip_group_check=skip)
                mm(out_, wn_h, y_l, start=False, stop=False, skip_group_check=skip)
                return mm(out_, wn_l, y_h, start=False, stop=stop, skip_group_check=skip)

            pe.wait_ge(consts, 6)
            pe.wait_ge(ident_r, 1)
            pe.wait_ge(ld_w, 16)
            pe.wait_ge(a_rows, 2)
            mm(PA[:, 0:B], ONES[:, :], CST[0], start=True, stop=False, skip_group_check=True)
            for T in range(TILES):
                ins = mm(PA[:, T // 2:T // 2 + 1], X[:, T * D:(T + 1) * D], RS[:, T:T + 1], start=False,
                         stop=(T == TILES - 1), skip_group_check=True)
            ins.then_inc(a_mm, 1)
            pe.wait_ge(a_cp, 1)
            mm(PB[:, 0:B], w(WV0), CST[1], start=True, stop=True).then_inc(a_mm, 1)
            pe.wait_ge(a_cp, 2)
            for b in range(B):
                bank = PS[:, b // 4 * 512:b // 4 * 512 + 512] if b < 12 else PT[:, 0:512]
                ins = mm(bank[:, b % 4 * 128:b % 4 * 128 + 128], CST[2][:, b:b + 1].broadcast_to([P, P]), w(WO0),
                         start=True, stop=True)
                if b % 4 == 3:
                    ins.then_inc(a_mm, 1)

            transpose_tiles(pe, 0)

            def inputs_part(t, h, par):
                bank = GATE[h][par]
                cols = bass.ds(t * S + h * 128, 128)
                for k, n in enumerate((WF, WI, WC)):
                    three(bank[:, k * 128:(k + 1) * 128], wh(n), wl(n), YHI[:, cols], YLO[:, cols], start=(k == 0))

            def cell_part(t, h, par):
                pe.wait_ge(cell[h], 3 * t)
                bank = GATE[h][par]
                for k, n in ((2, UC), (1, UI), (0, UF)):
                    ins = mm(bank[:, k * 128:(k + 1) * 128], w(n), C[h], start=False, stop=True, skip_group_check=True)
                ins.then_inc(gates[h], 1)

            def scan_step(t, par, more=True):
                for h in range(2):
                    cell_part(t, h, par)
                    if more:
                        inputs_part(t + 1, h, 1 - par)

            pe.wait_ge(small_split, 2)
            pe.wait_ge(c_init, 2)
            for p in range(2):
                pe.wait_ge(lo[0][p], CHUNKS // 2)
            pe.wait_ge(x1_done, 4)
            for h in range(2):
                inputs_part(0, h, 0)
            with pe.Fori(0, B // 2 - 1) as k:
                scan_step(2 * k, 0)
                scan_step(2 * k + 1, 1)
            scan_step(B - 2, 0)
            scan_step(B - 1, 1, more=False)

            for h in range(2):
                pe.wait_ge(cell[h], 3 * B)
                ins = mm(PB[:, h * 128:(h + 1) * 128], w(UO), C[h], start=(h == 0), stop=True, skip_group_check=True)
            ins.then_inc(cu_mm, 1)
            with pe.Fori(0, CHUNKS) as i:
                pe.wait_ge(ro_add, i)
                cols = ncols(i, CHUNK)
                three(PA[:, :], wh(WO), wl(WO), YHI[:, cols], YLO[:, cols], start=True, stop=True).then_inc(ro_mm, 1)
                pe.wait_ge(ro_tanh, i + 1)
                pe.wait_ge(ro_x, i)
                for t in range(4):
                    ins = nc.tensor.transpose(PS[:, t * 128:(t + 1) * 128], ROT[:, 512 + t * 128:640 + t * 128], ident)
                ins.then_inc(ro_tr, 1)

            def transpose_sequence(b):
                pe.wait_ge(t_norm, 2 * b + 2)
                for t in range(2):
                    ins = nc.tensor.transpose(PB[:, t * 128:(t + 1) * 128], OH2[:, t * 128:(t + 1) * 128], ident)
                ins.then_inc(t_tr, 1)

            def values(b):
                pe.wait_ge(t_hi, b + 1)
                pe.wait_ge(t_lo, b + 1)
                for t in range(2):
                    rows = slice(t * 128, (t + 1) * 128)
                    dst = PB[:, rows]
                    mm(dst, TH[:, rows], wh(WV1), start=True, stop=False)
                    mm(dst, TH[:, rows], wl(WV1), start=False, stop=False)
                    ins = mm(dst, TL[:, rows], wh(WV1), start=False, stop=True)
                ins.then_inc(v_mm, 1)

            def q_k(b, gr):
                n = b * GROUPS + gr
                if not begins(b) or gr > 0:
                    pe.wait_ge(qk_pos, n)
                if not begins(b) or gr == 3:
                    pe.wait_ge(q_shift, n - 2)
                cols = slice(gr * 128, (gr + 1) * 128)
                for m in range(2):
                    ins = three(PA[:, m * 256:(m + 1) * 256], WQK[m][0][:, cols], WQK[m][1][:, cols], TH, TL,
                                start=True, stop=True, skip=False)
                ins.then_inc(qk_mm, 1)

            def scores(b, gr):
                n = b * GROUPS + gr
                pe.wait_ge(stack, 5 * n + 5)
                if not begins(b) or gr > 0:
                    pe.wait_ge(s_max, 2 * n)
                keys = KM[gr].rearrange("p (j k) -> p j k", k=256)
                mm(PS[:, 0:512].rearrange("p (j k) -> p j k", k=128), QS[gr][:, 0:128], keys[:, :, 0:128], start=True, stop=True,
                   skip_group_check=True)
                mm(PS[:, 0:512].rearrange("p (j k) -> p j k", k=128), ident_bf,
                   causal.unsqueeze(1).broadcast_to([P, 4, 128]), start=False, stop=True, skip_group_check=True)
                for j in (0, 2):
                    dst = PS[:, 512 + j * 256:1024 + j * 256]
                    mm(dst, QS[gr][:, 128:256], KM[gr][:, j * 256:(j + 2) * 256], start=True, stop=True,
                       skip_group_check=True)
                    ins = mm(dst.rearrange("p (j k) -> p j k", k=256)[:, :, 128:256], ident_bf,
                             causal.unsqueeze(1).broadcast_to([P, 2, 128]), start=False, stop=True,
                             skip_group_check=True)
                ins.then_inc(s_mm, 1)

            def shift_rows(b, gr, last):
                n = b * GROUPS + gr
                pe.wait_ge(m_neg, n + 1)
                if last:
                    pe.wait_ge(q_shift, n)
                    pe.wait_ge(qk_pos, min(n + 3, B * GROUPS))
                else:
                    pe.wait_ge(qk_pos, n + 3)
                for t in range(2):
                    cols = slice(t * 128, (t + 1) * 128)
                    ins = mm(PA[:, cols], M2[:, cols], IDR[:, :], start=True, stop=True)
                ins.then_inc(m_tr, 1)

            def scores_t(b, gr):
                n = b * GROUPS + gr
                pe.wait_ge(q_shift, n + 1)
                if not begins(b) or gr > 0:
                    pe.wait_ge(prob, n)
                q = Q2[gr % 2]
                for j in range(4):
                    mm(PT[:, j * 256:(j + 1) * 256], KM[gr][:, j * 256:j * 256 + 128], q, start=True, stop=True)
                for j in range(4):
                    ins = mm(PT[:, 1024 + j * 128:1152 + j * 128], KM[gr][:, j * 256 + 128:j * 256 + 256],
                             q[:, 128:256], start=True, stop=True)
                ins.then_inc(st_mm, 1)

            def probs_values(b, gr, par):
                n = b * GROUPS + gr
                pe.wait_ge(masked, 2 * n + 2)
                pe.wait_ge(v_cp, b + 1)
                for j in range(4):
                    h = GROUPS * gr + j
                    dst = PB[32 * j:32 * j + 32, 0:256]
                    mm(dst, VPB[par][:, 0, h, :], PR[gr % 2][:, j * 256:(j + 1) * 256], start=True, stop=True,
                       tile_position=(0, 32 * j), skip_group_check=True)
                for j in range(4):
                    h = GROUPS * gr + j
                    ins = mm(PB[32 * j:32 * j + 32, 128:256], VPB[par][:, 1, h, :],
                             PR[gr % 2][:, 1024 + j * 128:1152 + j * 128], start=False, stop=True,
                             tile_position=(0, 32 * j), skip_group_check=True)
                ins.then_inc(pv_mm, 1)

            def transpose_u(b, gr):
                n = b * GROUPS + gr
                pe.wait_ge(u_cp, n + 1)
                for t in range(2):
                    cols = slice(t * 128, (t + 1) * 128)
                    ins = nc.tensor.transpose(PB[:, cols], US[:, cols], ident)
                ins.then_inc(u_tr, 1)

            def transpose_o(b, par):
                pe.wait_ge(o_norm, GROUPS * b + 4)
                for t in range(2):
                    cols = slice(t * 128, (t + 1) * 128)
                    ins = nc.tensor.transpose(PB[:, cols], OH[par][:, cols], ident)
                ins.then_inc(o_tr, 1)

            def project_o(b):
                pe.wait_ge(o_cp, b + 1)
                for t in range(2):
                    cols = slice(t * 128, (t + 1) * 128)
                    ins = mm(PB[:, cols], OT[:, cols], w(WO1), start=True, stop=True)
                ins.then_inc(o_mm, 1)

            def sequence(b, par, first, last):
                for gr in range(GROUPS):
                    n = b * GROUPS + gr
                    shift_rows(b, gr, last)
                    older = (b, gr - 2, par) if gr >= 2 else (b - 1, gr + 2, 1 - par)
                    if gr >= 2 or not first:
                        if gr == 0:
                            pe.wait_ge(o_norm, n - 2)
                            if not (isinstance(b, int) and b <= 1):
                                pe.wait_ge(x3_done, b - 1)
                        elif gr == 1:
                            pe.wait_ge(o_norm, n - 2)
                            pe.wait_ge(t_hi, b + 1 if last else b + 2)
                            pe.wait_ge(t_lo, b + 1 if last else b + 2)
                        elif gr == 2:
                            if not first:
                                pe.wait_ge(o_norm, n - 2)
                            pe.wait_ge(v_cp, b + 1 if last else b + 2)
                        else:
                            pe.wait_ge(o_norm, n - 2)
                            if not first:
                                pe.wait_ge(o_cp, b)
                        probs_values(*older)
                    if gr < 3:
                        scores(b, gr + 1)
                    elif not last:
                        scores(b + 1, 0)
                    if gr >= 2 or not first:
                        transpose_u(older[0], older[1])
                    scores_t(b, gr)
                    if gr == 0:
                        q_k(b, 3)
                        if not last:
                            if first:
                                pe.wait_ge(v_cp, 1)
                            else:
                                pe.wait_ge(o_norm, n - 1)
                            transpose_sequence(b + 1)
                    elif gr == 1:
                        if not last:
                            if not first:
                                pe.wait_ge(o_norm, n - 1)
                            values(b + 1)
                            q_k(b + 1, 0)
                    elif gr == 2:
                        if not first:
                            pe.wait_ge(o_norm, n - 1)
                            transpose_o(b - 1, 1 - par)
                        if not last:
                            q_k(b + 1, 1)
                    else:
                        if not first:
                            pe.wait_ge(o_norm, n - 1)
                            project_o(b - 1)
                        if not last:
                            q_k(b + 1, 2)

            pe.wait_ge(ld_cb, 16)
            pe.wait_ge(zeroed, 8)
            pe.wait_ge(qk_split, 12)
            transpose_sequence(0)
            values(0)
            for gr in range(3):
                q_k(0, gr)
            scores(0, 0)
            sequence(0, 0, True, False)
            with pe.Fori(0, 7) as k:
                sequence(2 * k + 1, 1, False, False)
                sequence(2 * k + 2, 0, False, False)
            sequence(15, 1, False, True)
            pe.wait_ge(x3_done, 15)
            probs_values(15, 2, 1)
            transpose_u(15, 2)
            pe.wait_ge(o_norm, 4 * 15 + 3)
            probs_values(15, 3, 1)
            transpose_u(15, 3)
            transpose_o(15, 1)
            project_o(15)

            transpose_tiles(pe, 1)
            pe.wait_ge(ld_sel, 16)
            for p in range(2):
                pe.wait_ge(lo[1][p], CHUNKS // 2)
            with pe.Fori(0, CHUNKS) as c:
                cols = ncols(c, CHUNK)
                pe.wait_ge(g_exp, c)
                three(PA[:, :], wh(GW), wl(GW), YHI[:, cols], YLO[:, cols], start=True, stop=True).then_inc(g_mm, 1)
                pe.wait_ge(g_exp, c + 1)
                pe.wait_ge(g_use, c)
                for t in range(4):
                    ins = nc.tensor.transpose(PB[:, t * 128:(t + 1) * 128], ROT[:, 512 + t * 128:640 + t * 128], ident)
                ins.then_inc(g_tr, 1)
                pe.wait_ge(g_cw, c + 1)
                pe.wait_ge(g_cwt, c)
                for t in range(4):
                    ins = nc.tensor.transpose(PTH[:, t * 128:(t + 1) * 128], CWS[:, t * 128:(t + 1) * 128], ident_h)
                ins.then_inc(g_cwtr, 1)

            def down(c, u):
                n = c * UNITS + u
                pe.wait_ge(e_prod, n + 1)
                mm(PY, WD[:, u * 128:(u + 1) * 128], PRD[u % 3], start=(u == 0), stop=(u == UNITS - 1)
                   ).then_inc(e_down, 1)

            pe.wait_ge(ld_wd, 16)
            pe.wait_ge(g_cwt, CHUNKS)
            pe.wait_ge(gu_split, 2 * (UNITS // STAGE_UNITS))
            with pe.Fori(0, CHUNKS) as c:
                cols = ncols(c, CHUNK)
                pe.wait_ge(y_cp, c)
                for u in range(UNITS):
                    n = c * UNITS + u
                    at = u * 256
                    pe.wait_ge(e_silu, n - 1 if u >= 2 else c * UNITS)
                    three(EG[u % 2], GUH[:, at:at + 128], GUL[:, at:at + 128], YHI[:, cols], YLO[:, cols],
                          start=True, stop=True).then_inc(e_gate, 1)
                    if u >= 2:
                        pe.wait_ge(e_act, c * PAIRS + u - 1)
                    else:
                        pe.wait_ge(e_prod, c * UNITS)
                    three(EU[u % 2], GUH[:, at + 128:at + 256], GUL[:, at + 128:at + 256], YHI[:, cols], YLO[:, cols],
                          start=True, stop=True).then_inc(e_up, 1)
                    if u < PAIRS:
                        if u >= 2:
                            pe.wait_ge(e_prod, n - 1)
                        else:
                            pe.wait_ge(e_prod, c * UNITS)
                        mm(EC[u % 2], SEL[:, u * 128:(u + 1) * 128], CWT[:, cols], start=True, stop=True
                           ).then_inc(e_cw, 1)
                    if u >= 2:
                        down(c, u - 2)
                down(c, UNITS - 2)
                down(c, UNITS - 1)
                pe.wait_ge(y_cp, c + 1)
                for t in range(4):
                    ins = nc.tensor.transpose(PY[:, t * 128:(t + 1) * 128], ROT[:, 512 + t * 128:640 + t * 128], ident)
                ins.then_inc(y_tr, 1)
                pe.wait_ge(x4_done, c + 1)

        @block.vector
        def _(dve):
            v = nc.vector

            def row_stats(k):
                ch = Chain(dve, stats[k])
                with dve.Fori(0, TILES // 4) as i:
                    for t in range(4):
                        ch.did(v.bn_stats(BN[:, bass.ds((4 * i + t) * 6, 6)], X[:, bass.ds((4 * i + t) * D, D)]))
                ch.at(TILES)
                ch.settle()
                mean_e, m2_e, mean_o, m2_o = (BN[:, col:6 * TILES:6] for col in (1, 2, 4, 5))
                mean, var = MV[:, 0:2 * TILES:2], MV[:, 1:2 * TILES:2]
                ch.did(v.tensor_tensor(NMR[:, :], mean_e, mean_o, ALU.subtract))
                ch.did(v.tensor_tensor(mean, mean_e, mean_o, ALU.add))
                ch.did(v.tensor_tensor(var, m2_e, m2_o, ALU.add))
                ch.settle()
                ch.did(v.scalar_tensor_tensor(NMR[:, :], NMR[:, :], 0.25, NMR[:, :], ALU.mult, ALU.mult))
                ch.did(v.tensor_scalar(mean, mean, 0.5, None, ALU.mult))
                ch.settle()
                ch.did(v.scalar_tensor_tensor(var, var, 1.0 / D, NMR[:, :], ALU.mult, ALU.add))
                ch.settle()

            dve.wait_ge(ld_x, 16)
            row_stats(0)
            dve.wait_ge(rstd[0], 1)
            v.scalar_tensor_tensor(NMR[:, :], MV[:, 0:2 * TILES:2], -1.0, RS[:, :], ALU.mult, ALU.mult).then_inc(a_rows, 1)
            dve.wait_ge(a_rows, 1)
            v.tensor_tensor(CST[0], NMR[:, 0:TILES:2], NMR[:, 1:TILES:2], ALU.add).then_inc(a_rows, 1)
            for q in range(4):
                bank = PS[:, q * 512:(q + 1) * 512] if q < 3 else PT[:, 0:512]
                dve.wait_ge(a_mm, 3 + q)
                xs = X[:, q * 1024:(q + 1) * 1024].rearrange("p (b h d) -> p b h d", h=2, d=D)
                v.tensor_tensor(xs, xs, bank.rearrange("p (b d) -> p b d", d=D).unsqueeze(2).broadcast_to([P, 4, 2, D]),
                                ALU.add).then_inc(x1_done, 1)

            dve.wait_ge(x1_done, 4)
            row_stats(1)
            dve.wait_ge(rstd[1], 1)
            normalise_and_lo(dve, 0)

            dve.wait_ge(ld_vec, 16)
            for h in range(2):
                v.tensor_copy(C[h], VEC[:, 4:5].broadcast_to([P, 128])).then_inc(c_init, 1)

            def scan_step(t):
                for h in range(2):
                    f, i, gg = (SG[h][:, k * 128:(k + 1) * 128] for k in range(3))
                    dve.wait_ge(acts[h], 3 * t + 2)
                    v.tensor_tensor(TMP[h], i, gg, ALU.mult).then_inc(cell[h], 1)
                    dve.wait_ge(acts[h], 3 * t + 3)
                    dve.wait_ge(c_init, 2)
                    v.tensor_tensor(C[h], f, C[h], ALU.mult).then_inc(cell[h], 1)
                    dve.wait_ge(cell[h], 3 * t + 2)
                    v.tensor_tensor(C[h], C[h], TMP[h], ALU.add).then_inc(cell[h], 1)
                    dve.wait_ge(cell[h], 3 * t + 3)

            with dve.Fori(0, B) as t:
                scan_step(t)

            dve.wait_ge(cu_cp, 1)
            with dve.Fori(0, CHUNKS) as i:
                dve.wait_ge(ro_mm, i + 1)
                dve.wait_ge(ro_tanh, i)
                v.tensor_tensor(ROT[:, 0:512].rearrange("p (b s) -> p b s", b=2),
                                PA[:, :].rearrange("p (b s) -> p b s", b=2),
                                CU.unsqueeze(1).broadcast_to([P, 2, S]), ALU.add).then_inc(ro_add, 1)
                dve.wait_ge(ro_tr, i + 1)
                v.tensor_tensor(X[:, ncols(i, CHUNK)], X[:, ncols(i, CHUNK)], PS[:, 0:512], ALU.add).then_inc(ro_x, 1)

            dve.wait_ge(ro_x, CHUNKS)
            row_stats(2)
            dve.wait_ge(rstd[2], 1)

            def norm_sequence(b):
                if not begins(b):
                    dve.wait_ge(t_tr, b)
                for t in range(2):
                    at = 2 * b + t
                    v.tensor_scalar(OH2[:, t * 128:(t + 1) * 128], X[:, bass.ds(at * D, D)], MV[:, bass.ds(at * 2, 1)],
                                    RS[:, bass.ds(at, 1)], ALU.subtract, ALU.mult).then_inc(t_norm, 1)

            def lo_sequence(b):
                dve.wait_ge(t_hi, b + 1)
                v.tensor_tensor(TL, PB[:, 0:256], TH, ALU.subtract).then_inc(t_lo, 1)

            def positions(b, gr):
                n = b * GROUPS + gr
                dve.wait_ge(qk_mm, n + 1)
                if not begins(b) or gr >= 2:
                    dve.wait_ge(stack, 5 * n - 5)
                v.tensor_tensor(QKF[gr % 2], PA[:, :], pos, ALU.add).then_inc(qk_pos, 1)

            def shift_q(b, gr):
                n = b * GROUPS + gr
                dve.wait_ge(m_tr, n + 1)
                if not begins(b) or gr >= 2:
                    dve.wait_ge(st_mm, n - 1)
                v.tensor_tensor(Q2[gr % 2], QS[gr], PA[:, 0:256], ALU.add).then_inc(q_shift, 1)

            def maxima(b, gr):
                n = b * GROUPS + gr
                dve.wait_ge(s_mm, n + 1)
                if not begins(b) or gr > 0:
                    dve.wait_ge(m_neg, n)
                v.tensor_reduce(MX[:, 0:4], PS[:, 0:512].rearrange("p (j k) -> p j k", k=128), AX.X, ALU.max
                                ).then_inc(s_max, 1)
                v.tensor_reduce(MX[:, 4:8], PS[:, 512:1536].rearrange("p (j k) -> p j k", k=256), AX.X, ALU.max
                                ).then_inc(s_max, 1)
                dve.wait_ge(s_max, 2 * n + 2)
                if not begins(b) or gr > 0:
                    dve.wait_ge(m_tr, n)
                v.tensor_scalar(M2[:, 0:256:32], MX[:, :], -1.0, None, ALU.mult).then_inc(m_neg, 1)

            def normalise_o(b, gr, par):
                n = b * GROUPS + gr
                dve.wait_ge(u_tr, n + 1)
                if not begins(b) or gr > 0:
                    dve.wait_ge(o_norm, n)
                if not begins(b) and gr == 0:
                    dve.wait_ge(o_tr, b - 1)
                u = PB[:, 0:256].rearrange("p (t j c) -> p t j c", t=2, c=32)
                rd = RD[:, :].rearrange("p (t j) -> p t j", t=2)
                v.reciprocal(rd, u[:, :, :, HD]).then_inc(u_rec, 1)
                dve.wait_ge(u_rec, n + 1)
                o = OH[par].rearrange("p (t g j c) -> p t g j c", t=2, g=4, c=HD)[:, :, gr, :, :]
                v.tensor_tensor(o, u[:, :, :, 0:HD], rd.unsqueeze(3).broadcast_to([P, 2, 4, HD]), ALU.mult
                                ).then_inc(o_norm, 1)

            def add_o(b):
                dve.wait_ge(o_mm, b + 1)
                v.tensor_tensor(X[:, ncols(b, 256)], X[:, ncols(b, 256)], PB[:, 0:256], ALU.add).then_inc(x3_done, 1)

            def sequence(b, par, first, last):
                for gr in range(GROUPS):
                    shift_q(b, gr)
                    if gr == 0 and not last:
                        norm_sequence(b + 1)
                    if gr < 3:
                        maxima(b, gr + 1)
                    elif not last:
                        maxima(b + 1, 0)
                    if gr >= 2:
                        normalise_o(b, gr - 2, par)
                    elif not first:
                        normalise_o(b - 1, gr + 2, 1 - par)
                    if gr == 0:
                        positions(b, 3)
                        if not last:
                            lo_sequence(b + 1)
                    elif not last:
                        positions(b + 1, gr - 1)
                    if gr == 3 and not first:
                        add_o(b - 1)

            dve.wait_ge(zeroed, 8)
            dve.wait_ge(qk_split, 12)
            norm_sequence(0)
            lo_sequence(0)
            for gr in range(3):
                positions(0, gr)
            maxima(0, 0)
            sequence(0, 0, True, False)
            with dve.Fori(0, 7) as k:
                sequence(2 * k + 1, 1, False, False)
                sequence(2 * k + 2, 0, False, False)
            sequence(15, 1, False, True)
            normalise_o(15, 2, 1)
            normalise_o(15, 3, 1)
            add_o(15)

            dve.wait_ge(x3_done, B)
            row_stats(3)
            dve.wait_ge(rstd[3], 1)
            normalise_and_lo(dve, 1)

            G4 = 4 * 8

            def buf(k, shape=None):
                return VP[:, k * 256:(k + 1) * 256]

            sig, sc, t1, t2, t3, cw = (buf(k) for k in range(6))
            top, gsc, small_ = VP[:, 1536:1568], VP[:, 1568:1600], VP[:, 1600:2048]
            tot, rec = small_[:, 0:4], small_[:, 4:8]
            rank, best = small_[:, 8:40], small_[:, 40:72]
            ch = Chain(dve, g_chain)
            PER = 38

            dve.wait_ge(ld_bias, 16)
            with dve.Fori(0, CHUNKS) as c:
                ch.at(PER * c)

                def op(ins):
                    ch.did(ins)
                    ch.settle()

                dve.wait_ge(g_tr, c + 1)
                logit = PB[:, :].rearrange("p (t e) -> p t e", t=4)[:, :, 0:NE]
                ins = v.tensor_scalar(t1.rearrange("p (t e) -> p t e", t=4), logit, 1.0, None, ALU.add)
                ins.then_inc(g_use, 1)
                dve.wait_ge(g_use, c + 1)
                op(v.reciprocal(sig, t1))
                op(v.tensor_tensor(sc.rearrange("p (t e) -> p t e", t=4), sig.rearrange("p (t e) -> p t e", t=4),
                                   BIAS[:, :].unsqueeze(1).broadcast_to([P, 4, NE]), ALU.add))
                s8 = sc.rearrange("p (g k) -> p g k", k=8)
                h1 = t1[:, 0:128].rearrange("p (g k) -> p g k", k=4)
                l1 = t1[:, 128:256].rearrange("p (g k) -> p g k", k=4)
                ch.did(v.tensor_tensor(h1, s8[:, :, 0:4], s8[:, :, 4:8], ALU.max))
                op(v.tensor_tensor(l1, s8[:, :, 0:4], s8[:, :, 4:8], ALU.min))
                h2 = t2[:, 0:64].rearrange("p (g k) -> p g k", k=2)
                a2 = t2[:, 64:128].rearrange("p (g k) -> p g k", k=2)
                b2 = t2[:, 128:192].rearrange("p (g k) -> p g k", k=2)
                ch.did(v.tensor_tensor(h2, h1[:, :, 0:2], h1[:, :, 2:4], ALU.max))
                ch.did(v.tensor_tensor(a2, h1[:, :, 0:2], h1[:, :, 2:4], ALU.min))
                op(v.tensor_tensor(b2, l1[:, :, 0:2], l1[:, :, 2:4], ALU.max))
                op(v.tensor_tensor(a2, a2, b2, ALU.max))
                h3, a3, b3 = t3[:, 0:32], t3[:, 32:64], t3[:, 64:96]
                ch.did(v.tensor_tensor(h3, h2[:, :, 0], h2[:, :, 1], ALU.max))
                ch.did(v.tensor_tensor(a3, h2[:, :, 0], h2[:, :, 1], ALU.min))
                op(v.tensor_tensor(b3, a2[:, :, 0], a2[:, :, 1], ALU.max))
                op(v.tensor_tensor(a3, a3, b3, ALU.max))
                op(v.tensor_tensor(gsc, h3, a3, ALU.add))
                gs = gsc.rearrange("p (t g) -> p t g", t=4)
                other = gs.unsqueeze(2).broadcast_to([P, 4, 8, 8])
                own = gs.unsqueeze(3).broadcast_to([P, 4, 8, 8])
                gt = t1.rearrange("p (t g k) -> p t g k", t=4, k=8)
                eq = t2.rearrange("p (t g k) -> p t g k", t=4, k=8)
                ch.did(v.tensor_tensor(gt, other, own, ALU.is_gt))
                op(v.tensor_tensor(eq, other, own, ALU.is_equal))
                tri = CF[:, C_TRI:C_TRI + 64].unsqueeze(1).broadcast_to([P, 4, 64])
                op(v.tensor_tensor(t2.rearrange("p (t e) -> p t e", t=4), t2.rearrange("p (t e) -> p t e", t=4), tri,
                                   ALU.mult))
                op(v.tensor_tensor(t1, t1, t2, ALU.add))
                op(v.tensor_reduce(rank, t1.rearrange("p (g k) -> p g k", k=8), AX.X, ALU.add))
                op(v.tensor_scalar(rank, rank, 3.5, -BIG / 2, ALU.is_gt, ALU.mult))
                op(v.tensor_tensor(t3.rearrange("p (g k) -> p g k", k=8), s8, rank.unsqueeze(2).broadcast_to([P, G4, 8]),
                                   ALU.add))
                for t in range(4):
                    if t == 0:
                        ch.did(v.tensor_copy(tot, sig[:, 0:4]))
                    ch.did(v.max(best[:, t * 8:t * 8 + 8], t3[:, t * 64:(t + 1) * 64]))
                ch.settle()
                ch.did(v.tensor_copy(tot, sig[:, 0:4]))
                for t in range(4):
                    ch.did(v.match_replace(t2[:, t * 64:(t + 1) * 64], best[:, t * 8:t * 8 + 8],
                                           t3[:, t * 64:(t + 1) * 64], -BIG))
                ch.settle()
                op(v.tensor_tensor(t1, t2, t3, ALU.not_equal))
                op(v.tensor_tensor(t1, t1, sig, ALU.mult))
                op(v.tensor_reduce(tot, t1.rearrange("p (t e) -> p t e", t=4), AX.X, ALU.add))
                op(v.tensor_scalar(tot, tot, 1e-20, None, ALU.add))
                op(v.reciprocal(rec, tot))
                op(v.scalar_tensor_tensor(cw.rearrange("p (t e) -> p t e", t=4), t1.rearrange("p (t e) -> p t e", t=4),
                                          ROUTED_SCALE, rec.unsqueeze(2).broadcast_to([P, 4, NE]), ALU.mult, ALU.mult))
                parts = CWS.rearrange("p (t k e) -> p t k e", t=4, k=2)
                dve.wait_ge(g_cwtr, c)
                op(v.tensor_copy(parts[:, :, 0, :], cw.rearrange("p (t e) -> p t e", t=4)))
                op(v.tensor_tensor(t2.rearrange("p (t e) -> p t e", t=4), cw.rearrange("p (t e) -> p t e", t=4),
                                   parts[:, :, 0, :], ALU.subtract))
                ins = v.tensor_scalar(parts[:, :, 1, :], t2.rearrange("p (t e) -> p t e", t=4), LOW, None, ALU.mult)
                ins.then_inc(g_cw, 1)
                dve.wait_ge(g_cw, c + 1)
                assert ch.n == PER, ch.n

            with dve.Fori(0, CHUNKS) as c:
                for u in range(UNITS):
                    n = c * UNITS + u
                    dve.wait_ge(e_silu, n + 1)
                    dve.wait_ge(e_up, n + 1)
                    if u >= 3:
                        dve.wait_ge(e_down, n - 2)
                    if u < PAIRS:
                        v.tensor_tensor(ACTV, SIL[u % 2], EU[u % 2], ALU.mult).then_inc(e_act, 1)
                        dve.wait_ge(e_act, c * PAIRS + u + 1)
                        dve.wait_ge(e_cw, c * PAIRS + u + 1)
                        v.tensor_tensor(PRD[u % 3], ACTV, EC[u % 2], ALU.mult).then_inc(e_prod, 1)
                        dve.wait_ge(e_prod, n + 1)
                    else:
                        v.tensor_tensor(PRD[u % 3], SIL[u % 2], EU[u % 2], ALU.mult).then_inc(e_prod, 1)
                dve.wait_ge(y_tr, c + 1)
                v.tensor_tensor(X[:, ncols(c, CHUNK)], X[:, ncols(c, CHUNK)], PY, ALU.add).then_inc(x4_done, 1)


def kernel(**inputs):
    import numpy as np
    import concourse.bacc as bacc
    from concourse.bass_utils import run_bass_kernel_spmd

    a = {k: np.ascontiguousarray(v) for k, v in inputs.items()}
    f32 = np.float32

    gate = np.zeros((D, P), f32)
    gate[:, :NE] = a["L1_ffn_gate_w"].T
    mats = {
        WF: a["L0_ffn_wf"].T, WI: a["L0_ffn_wi"].T, WC: a["L0_ffn_wc"].T, WO: a["L0_ffn_wo"].T,
        WV1: a["L1_attn_Wv"], GW: gate, WV0: a["L0_attn_w_qkv"][2 * D:].T, WO0: a["L0_attn_w_o"].T,
        UF: a["L0_ffn_uf"].T, UI: a["L0_ffn_ui"].T, UC: a["L0_ffn_uc"].T, UO: a["L0_ffn_uo"].T,
        WO1: a["L1_attn_Wo"], WQ: a["L1_attn_Wq"], WK: a["L1_attn_Wk"],
    }
    small = np.ascontiguousarray(np.stack([mats[k] for k in range(15)], axis=1))
    vec = np.ascontiguousarray(np.stack([a[f"L0_ffn_{k}"] for k in ("bf", "bi", "bc", "bo", "in_c")], axis=1))
    gu = np.zeros((D, UNITS, 2, 2, FF), f32)
    wd = np.zeros((2, FF, UNITS, D), f32)
    for k, name in enumerate(("gate", "up")):
        gu[:, :PAIRS, k] = a[f"L1_ffn_We_{name}"].reshape(PAIRS, 2, D, FF).transpose(2, 0, 1, 3)
        gu[:, PAIRS, k, 0] = a[f"L1_ffn_Ws_{name}"]
    wd[:, :, :PAIRS] = a["L1_ffn_We_down"].reshape(PAIRS, 2, FF, D).transpose(1, 2, 0, 3)
    wd[0, :, PAIRS] = a["L1_ffn_Ws_down"]
    gu, wd = gu.reshape(D, UNITS, 256), wd.reshape(P, UNITS, D)

    cf = np.zeros((P, C_END), f32)
    cf[:, C_ID:C_ID + 128] = np.eye(P, dtype=f32)
    scale = 1.0 / (np.power(f32(10000.0), np.arange(0, HD, 2, dtype=f32) / f32(HD)) + np.finfo(f32).eps)
    angle = np.arange(S, dtype=f32)[:, None] * scale.astype(f32)[None, :]
    pos = np.stack([np.sin(angle), np.cos(angle)], axis=-1).reshape(S, HD).astype(f32)
    slot = np.arange(P) % 32
    for p in range(P):
        if slot[p] >= 8:
            cf[p, C_POS:C_POS + 256] = pos[:, p % 8]
            cf[p, C_POS + 256:C_POS + 512] = pos[:, p % 8]
    cf[slot == 0, C_POS + 256:C_POS + 512] = 1.0
    cf[(slot >= 16) & (slot < 24), C_QLO] = 1.0
    cf[slot >= 24, C_KLO] = 1.0
    cf[:, C_TRI:C_TRI + 64] = np.tril(np.ones((8, 8), f32), -1).reshape(1, 64)
    cb = np.zeros((P, 256), np.dtype(mybir.dt.np(BF16)))
    cb[:, :128] = np.eye(P)
    cb[:, 128:] = np.triu(np.full((P, P), -BIG, f32), 1)
    ch = np.zeros((P, PAIRS + 1, P), np.float16)
    for u in range(PAIRS):
        for k in range(2):
            ch[2 * u + k, u, k * FF:(k + 1) * FF] = 1.0
            ch[NE + 2 * u + k, u, k * FF:(k + 1) * FF] = 1.0 / LOW
    ch[:, PAIRS] = np.eye(P)
    ch = ch.reshape(P, (PAIRS + 1) * P)

    nc = bacc.Bacc("TRN2", target_bir_lowering=False, num_devices=1)
    arrays, args = {}, []
    for name, arr in (("x", a["L0_attn_x"]), ("small", small), ("vec", vec), ("gate_bias", a["L1_ffn_gate_bias"]),
                      ("gu", gu), ("wd", wd), ("cf32", cf), ("cbf", cb), ("cf16", ch)):
        arr = np.ascontiguousarray(arr)
        arrays[name] = arr
        args.append(nc.dram_tensor(name, arr.shape, mybir.dt.from_np(arr.dtype), kind="ExternalInput").ap())
    args.append(nc.dram_tensor("out", (B, S, D), F32, kind="ExternalOutput").ap())
    two_layers(nc, *args)
    r = run_bass_kernel_spmd(nc, [arrays], core_ids=[0])
    return r.results[0]["out"]
```

```python
import concourse.bass as bass
from concourse import mybir
from concourse.alu_op_type import AluOpType as ALU
from contextlib import ExitStack

F32 = mybir.dt.float32
F32R = mybir.dt.float32r
BF16 = mybir.dt.bfloat16
F16 = mybir.dt.float16
ACT = mybir.ActivationFunctionType
AX = mybir.AxisListType

P = 128
B, S, D = 16, 256, 128
TILES = B * S // P
HEADS, HD = 16, 8
GROUPS = 4
NE, FF = 64, 64
PAIRS = NE // 2
UNITS = PAIRS + 1
STAGE_UNITS = 3
CHUNK = 512
CHUNKS = B * S // CHUNK
EPS = 1e-5
STATS = TILES + 6
BIG = 3e38
SCALE = float(D) ** -0.5
ROUTED_SCALE = 2.5
LOW = 4096.0

WF, WI, WC, WO, WV1, GW, WV0, WO0, UF, UI, UC, UO, WO1, WQ, WK = range(15)
SPLIT = 6
PREP = {"stats": 4, "mean": 5, "variance": 6, "rstd": 6, "normalise": 8, "turn": 11, "low": 12, "logits": 13,
        "exp": 13, "turn_exp": 16, "sigmoid": 17, "pairs": 18, "fours": 19, "groups": 20, "compare": 21, "rank": 22,
        "reach": 23, "best": 24, "replace": 25, "chosen": 26, "sum": 27, "weights": 28, "parts": 29,
        "turn_weights": UNITS - 1}
C_ID, C_POS, C_QLO, C_KLO, C_TRI, C_END = 0, 128, 640, 641, 642, 706


def begins(b):
    return isinstance(b, int) and b == 0


class Chain:

    def __init__(self, eng, sem):
        self.eng, self.sem, self.base, self.n = eng, sem, 0, 0

    def at(self, base):
        self.base, self.n = base, 0

    def did(self, ins):
        ins.then_inc(self.sem, 1)
        self.n += 1

    def settle(self, back=0):
        self.eng.wait_ge(self.sem, self.base + self.n - back)


def two_layers(nc, x, small, vec, gate_bias, gu, wd, cf32, cbf, cf16, out):
    ctx = ExitStack()
    with ctx:
        def sb(name, shape, dt=F32):
            return ctx.enter_context(nc.sbuf_tensor(name, shape, dt))

        def sem(name):
            return ctx.enter_context(nc.semaphore(name))

        X = sb("X", [P, TILES * D])
        YHI = sb("YHI", [P, B * S], F32R)
        YLO = sb("YLO", [P, B * S], F32R)
        GUH = sb("GUH", [P, UNITS * 256], F32R)
        GUL = sb("GUL", [P, UNITS * 256], F32R)
        WH = sb("WH", [P, SPLIT * 128], F32R)
        WL = sb("WL", [P, SPLIT * 128], F32R)
        VEC = sb("VEC", [P, 5])
        BIAS = sb("BIAS", [P, NE])
        CF = sb("CF", [P, C_END])
        CB = sb("CB", [P, 256], BF16)
        SEL = sb("SEL", [P, PAIRS * 128 + 128], F16)
        CWT = sb("CWT", [P, CHUNK], F16)
        IDR = sb("IDR", [P, P], F32R)
        ONES = sb("ONES", [P, P])
        EPST = sb("EPST", [P, TILES])
        EPS4 = sb("EPS4", [P, 4])
        MV = sb("MV", [P, TILES * 2])
        RS = sb("RS", [P, TILES])
        BN = sb("BN", [P, TILES * 6])
        NMR = sb("NMR", [P, TILES])
        COLS = sb("COLS", [P, 3 * B])
        BUF = sb("BUF", [P, 3072])
        ROT = sb("ROT", [P, 1024])
        VP = sb("VP", [P, 2 * 2 * HEADS * 32])
        US = sb("US", [P, S])
        RD = sb("RD", [P, 2 * 4])
        NOTE = sb("NOTE", [P, 1])
        MX = sb("MX", [P, 2 * 4])
        PRX = sb("PRX", [P, 1024], F32R)
        LN3 = sb("LN3", [P, 40])

        with ExitStack() as early:
            def sb_early(name, shape, dt=F32):
                return early.enter_context(nc.sbuf_tensor(name, shape, dt))

            WD = sb_early("WD", [P, UNITS * 128])
            W = sb_early("W", [P, 15 * 128])
            WQK = [[sb_early(f"W{m}S{part}", [P, HEADS * 32], F32R) for part in "hl"] for m in "qk"]
            M2T = sb_early("M2T", [P, S], F32R)
            OHS, OH2, OT = sb_early("OHS", [P, 4 * D]), sb_early("OH2", [P, 2 * D]), sb_early("OT", [P, S])
        WDL = sb("WDL", [P, UNITS * 128], F32R)
        WDH = sb("WDH", [P, UNITS * 128], F32R)
        HID = sb("HID", [P, 1024], F32R)

        ident = CF[:, C_ID:C_ID + 128]
        pos = CF[:, C_POS:C_POS + 512]
        ident_bf = CB[:, 0:128]
        causal = CB[:, 128:256]
        ident_h = SEL[:, PAIRS * 128:PAIRS * 128 + 128]

        def w(n):
            return W[:, n * 128:(n + 1) * 128]

        def wh(n):
            return WH[:, n * 128:(n + 1) * 128]

        def wl(n):
            return WL[:, n * 128:(n + 1) * 128]

        PA = ctx.enter_context(nc.psum_tensor("PA", [P, 512], F32))
        PS = ctx.enter_context(nc.psum_tensor("PS", [P, 1536], F32))
        PT = ctx.enter_context(nc.psum_tensor("PT", [P, 1536], F32))
        PB = ctx.enter_context(nc.psum_tensor("PB", [P, 512], F32))

        ld_x, ld_w, ld_vec, ld_bias, ld_cf, ld_cb, ld_sel, ld_wd = (
            sem(n) for n in ("ld_x", "ld_w", "ld_vec", "ld_bias", "ld_cf", "ld_cb", "ld_sel", "ld_wd"))
        ld_gu = [sem(f"ld_gu{p}") for p in range(2)]
        gu_split = sem("gu_split")
        consts = sem("consts")
        ident_r = sem("ident_r")
        small_split = sem("small_split")
        qk_split = sem("qk_split")
        stats = [sem(f"stats{n}") for n in "abc"]
        rstd = [sem(f"rstd{n}") for n in "abc"]
        rs_add = sem("rs_add")
        a_rows = sem("a_rows")
        a_mm = sem("a_mm")
        a_cp = sem("a_cp")
        x1_done = sem("x1_done")
        norm, tr, hi = sem("norm"), sem("tr"), sem("hi")
        lo = [sem(f"lo{p}") for p in range(2)]
        gates = [sem(f"gates{h}") for h in range(2)]
        acts = [sem(f"acts{h}") for h in range(2)]
        cell = [sem(f"cell{h}") for h in range(2)]
        c_init = sem("c_init")
        cu_mm = sem("cu_mm")
        cu_cp = sem("cu_cp")
        ro_mm, ro_add, ro_tanh, ro_tr, ro_x = (sem(n) for n in ("ro_mm", "ro_add", "ro_tanh", "ro_tr", "ro_x"))
        t_norm, t_tr, t_hi, t_lo, v_mm, v_cp = (sem(n) for n in ("t_norm", "t_tr", "t_hi", "t_lo", "v_mm", "v_cp"))
        zeroed = sem("zeroed")
        km = [sem(f"km{g}") for g in range(GROUPS)]
        qk_mm, qk_pos, qk_hi, stack, s_mm, s_max, m_neg, m_tr, q_shift = (
            sem(n) for n in ("qk_mm", "qk_pos", "qk_hi", "stack", "s_mm", "s_max", "m_neg", "m_tr", "q_shift"))
        st_mm, prob, masked, pv_mm, u_cp, u_tr, u_rec, o_norm = (
            sem(n) for n in ("st_mm", "prob", "masked", "pv_mm", "u_cp", "u_tr", "u_rec", "o_norm"))
        o_tr, o_cp, o_mm, x3_done = (sem(n) for n in ("o_tr", "o_cp", "o_mm", "x3_done"))
        c_var, c_rs, c_rstd, c_norm, c_tr, c_hi, c_lo = (
            sem(n) for n in ("c_var", "c_rs", "c_rstd", "c_norm", "c_tr", "c_hi", "c_lo"))
        g_mm, g_exp, g_tr, g_use, g_chain, g_cw, g_cwtr, g_cwt = (
            sem(n) for n in ("g_mm", "g_exp", "g_tr", "g_use", "g_chain", "g_cw", "g_cwtr", "g_cwt"))
        wd_hi, wd_lo = sem("wd_hi"), sem("wd_lo")
        e_gate, e_up, e_cw, e_silu, e_act, e_prod, e_hi, e_lo, e_down = (
            sem(n) for n in ("e_gate", "e_up", "e_cw", "e_silu", "e_act", "e_prod", "e_hi", "e_lo", "e_down"))
        y_cp, y_tr, x4_done, stored = (sem(n) for n in ("y_cp", "y_tr", "x4_done", "stored"))

        KM = [YLO[:, g * 1024:(g + 1) * 1024] for g in range(GROUPS)]
        QKS = [YHI[:, g * 512:(g + 1) * 512] for g in range(GROUPS)]
        QS = [QKS[g][:, 0:256] for g in range(GROUPS)]
        Q2 = [YHI[:, 2048 + p * 256:2304 + p * 256] for p in range(2)]
        HM = [YHI[:, 2560 + p * 512:3072 + p * 512] for p in range(2)]
        TH = YHI[:, 3584:3840]
        TL = YHI[:, 3840:4096]
        MTP = PS[:, 1024:1280]
        M2 = M2T[:, :]
        QKF = [ROT[:, p * 512:(p + 1) * 512] for p in range(2)]
        PR = [BUF[:, p * 1536:(p + 1) * 1536] for p in range(2)]
        VPB = [VP[:, p * 1024:(p + 1) * 1024].rearrange("p (t h c) -> p t h c", t=2, c=32) for p in range(2)]
        YN = [ROT[:, p * 512:(p + 1) * 512] for p in range(2)]
        PBU, PAS = PB[:, 0:256], PA[:, 0:256]
        PAB = [PA, PB]
        OH = [OHS[:, p * 256:(p + 1) * 256] for p in range(2)]
        CST = [COLS[:, n * B:(n + 1) * B] for n in range(3)]
        XV = X[:, :].rearrange("p (t d) -> p t d", d=D)

        GATE = [PS[:, 0:512], PS[:, 512:1024]], [PS[:, 1024:1536], PT[:, 0:512]]
        SG = [VP[:, h * 640:h * 640 + 384] for h in range(2)]
        C = [VP[:, h * 640 + 384:h * 640 + 512] for h in range(2)]
        TMP = [VP[:, h * 640 + 512:h * 640 + 640] for h in range(2)]
        CU = VP[:, 1280:1536]
        CWS = US[:, :].bitcast(F16)
        PAH = PA[:, 0:256].bitcast(F16)
        SIL = [BUF[:, p * 512:(p + 1) * 512] for p in range(2)]
        PRF = [BUF[:, 1024 + p * 512:1536 + p * 512] for p in range(3)]
        PRH = [WH[:, 0:512], HID[:, 0:512], PRX[:, 0:512]]
        PRL = [WL[:, 0:512], HID[:, 512:1024], PRX[:, 512:1024]]
        YNC, TURN = ROT[:, 0:512], ROT[:, 512:1024]
        EG = [PS[:, 0:512], PS[:, 512:1024]]
        EU = [PS[:, 1024:1536], PT[:, 0:512]]
        EC = [PT[:, 512:1024], PT[:, 1024:1536]]
        BNC, MEAN, VAR, SPREAD, RSC = (LN3[:, a:b] for a, b in ((0, 24), (24, 28), (28, 32), (32, 36), (36, 40)))
        PY = PB[:, :]

        block = ctx.enter_context(nc.Block())

        def ncols(i, n):
            return bass.ds(i * n, n)

        def normalise_and_lo(dve):
            def normalise(G, p):
                for t in range(4):
                    at = 4 * G + t
                    nc.vector.tensor_scalar(YN[p][:, t * 128:(t + 1) * 128], X[:, bass.ds(at * D, D)],
                                            MV[:, bass.ds(at * 2, 1)], RS[:, bass.ds(at, 1)],
                                            ALU.subtract, ALU.mult).then_inc(norm, 1)

            def low_part(G, p):
                dve.wait_ge(hi, G + 1)
                nc.vector.tensor_tensor(YLO[:, ncols(G, CHUNK)], PAB[p][:, :], YHI[:, ncols(G, CHUNK)],
                                        ALU.subtract).then_inc(lo[p], 1)

            normalise(0, 0)
            with dve.Fori(0, CHUNKS // 2 - 1) as i:
                normalise(2 * i + 1, 1)
                low_part(2 * i, 0)
                normalise(2 * i + 2, 0)
                low_part(2 * i + 1, 1)
            normalise(CHUNKS - 1, 1)
            low_part(CHUNKS - 2, 0)
            low_part(CHUNKS - 1, 1)

        def transpose_tiles(pe):
            with pe.Fori(0, CHUNKS // 2) as i:
                for p in range(2):
                    pe.wait_ge(lo[p], i)
                    pe.wait_ge(norm, 4 * (2 * i + p + 1))
                    for t in range(4):
                        ins = nc.tensor.transpose(PAB[p][:, t * 128:(t + 1) * 128], YN[p][:, t * 128:(t + 1) * 128],
                                                  ident)
                    ins.then_inc(tr, 1)

        def split_hi(act):
            with act.Fori(0, CHUNKS // 2) as i:
                for p in range(2):
                    act.wait_ge(tr, 2 * i + p + 1)
                    nc.scalar.activation(YHI[:, ncols(2 * i + p, CHUNK)], PAB[p][:, :], ACT.Copy).then_inc(hi, 1)

        @block.sync
        def _(sp):
            sp.dma_start(X[:, :].rearrange("p (b h d) -> p b h d", h=2, d=D),
                         x.rearrange("b (h p) d -> p b h d", p=P)).then_inc(ld_x, 16)
            sp.dma_start(W[:, :], small.rearrange("p k m -> p (k m)")).then_inc(ld_w, 16)
            sp.dma_start(CF[:, :], cf32).then_inc(ld_cf, 16)
            sp.dma_start(VEC[:, :], vec).then_inc(ld_vec, 16)
            sp.dma_start(BIAS[:, :], gate_bias.partition_broadcast(P)).then_inc(ld_bias, 16)
            sp.dma_start(CB[:, :], cbf).then_inc(ld_cb, 16)
            for n in range(UNITS // STAGE_UNITS):
                if n >= 2:
                    sp.wait_ge(gu_split, 2 * (n - 1))
                sp.dma_start(BUF[:, (n % 2) * 1536:(n % 2) * 1536 + STAGE_UNITS * 256],
                             gu[:, n * STAGE_UNITS:(n + 1) * STAGE_UNITS, :].rearrange("p k m -> p (k m)")
                             ).then_inc(ld_gu[n % 2], 16)
            sp.dma_start(SEL[:, :], cf16).then_inc(ld_sel, 16)
            sp.dma_start(WD[:, :], wd.rearrange("p k m -> p (k m)")).then_inc(ld_wd, 16)
            def spread_k(b, gr):
                n = b * GROUPS + gr
                sp.wait_ge(stack, n + 1)
                for j in range(4):
                    rows = slice(32 * j, 32 * j + 32)
                    sp.dma_start(KM[gr][rows, j * 256:(j + 1) * 256].bitcast(F32),
                                 QKS[gr][rows, 256:512].bitcast(F32)).then_inc(km[gr], 16)

            for gr in range(GROUPS):
                spread_k(0, gr)
            with sp.Fori(1, B) as b:
                for gr in range(GROUPS):
                    spread_k(b, gr)

            with sp.Fori(0, CHUNKS) as c:
                sp.wait_ge(x4_done, c + 1)
                sp.dma_start(out[bass.ds(c * 2, 2), :, :].rearrange("b (h p) d -> p b h d", p=P),
                             X[:, bass.ds(c * CHUNK, CHUNK)].rearrange("p (b h d) -> p b h d", h=2, d=D)
                             ).then_inc(stored, 16)
            sp.wait_ge(stored, 16 * CHUNKS)

        @block.gpsimd
        def _(pool):
            g = nc.gpsimd
            g.memset(EPST[:, :], -0.5).then_inc(consts, 1)
            g.memset(ONES[:, :], 1.0).then_inc(consts, 1)
            g.memset(EPS4[:, :], EPS).then_inc(consts, 1)
            for m in range(2):
                for part in range(2):
                    g.memset(WQK[m][part][:, :].bitcast(F32), 0.0).then_inc(consts, 1)
            pool.wait_ge(ld_w, 16)
            g.tensor_copy(WH[:, :], W[:, 0:SPLIT * 128]).then_inc(small_split, 1)
            pool.wait_ge(small_split, 1)
            g.tensor_tensor(WL[:, :], W[:, 0:SPLIT * 128], WH[:, :], ALU.subtract).then_inc(small_split, 1)

            def rstd_all(k):
                pool.wait_ge(stats[k], STATS)
                g.tensor_scalar(RS[:, :], MV[:, 1:2 * TILES:2], EPS, None, ALU.add).then_inc(rs_add, 1)
                pool.wait_ge(rs_add, k + 1)
                g.tensor_tensor(RS[:, :], RS[:, :], EPST[:, :], ALU.pow).then_inc(rstd[k], 1)

            pool.wait_ge(consts, 7)
            rstd_all(0)
            for m, src in enumerate((WQ, WK)):
                raw = w(src).rearrange("p (h d) -> p h d", d=HD)
                wide = [WQK[m][part][:, :].rearrange("p (h s d) -> p h s d", s=4, d=HD) for part in range(2)]
                for s in (1, 2, 3):
                    g.tensor_copy(wide[0][:, :, s, :], raw).then_inc(qk_split, 1)
                pool.wait_ge(qk_split, 6 * m + 3)
                for s in (1, 2, 3):
                    g.tensor_tensor(wide[1][:, :, s, :], raw, wide[0][:, :, s, :], ALU.subtract).then_inc(qk_split, 1)
            rstd_all(1)
            for n in range(UNITS // STAGE_UNITS):
                cols = slice(n * STAGE_UNITS * 256, (n + 1) * STAGE_UNITS * 256)
                raw = BUF[:, (n % 2) * 1536:(n % 2) * 1536 + STAGE_UNITS * 256]
                pool.wait_ge(ld_gu[n % 2], 16 * (n // 2 + 1))
                g.tensor_copy(GUH[:, cols], raw).then_inc(gu_split, 1)
                pool.wait_ge(gu_split, 2 * n + 1)
                g.tensor_tensor(GUL[:, cols], raw, GUH[:, cols], ALU.subtract).then_inc(gu_split, 1)

            pool.wait_ge(ro_mm, CHUNKS)
            for gr in range(GROUPS):
                g.memset(KM[gr].bitcast(F32), 0.0).then_inc(zeroed, 1)
            g.memset(M2.bitcast(F32), 0.0).then_inc(zeroed, 1)
            pool.wait_ge(ro_add, CHUNKS)
            g.memset(VP[:, :], 0.0).then_inc(zeroed, 1)
            pool.wait_ge(zeroed, 6)
            for p in range(2):
                g.memset(VPB[p][:, :, :, HD:HD + 1], 1.0).then_inc(zeroed, 1)
            rstd_all(2)

            def q_k_stack(b, gr):
                n = b * GROUPS + gr
                pool.wait_ge(qk_hi, 2 * n + 2)
                if not begins(b):
                    pool.wait_ge(q_shift, n - GROUPS + 1)
                    pool.wait_ge(km[gr], 64 * b)
                g.tensor_tensor(QKS[gr], QKF[gr % 2], HM[gr % 2], ALU.subtract).then_inc(stack, 1)

            def causal_select(b, gr):
                n = b * GROUPS + gr
                pool.wait_ge(prob, n + 1)
                first = PR[gr % 2][:, 0:1024].rearrange("p (j q) -> p j q", q=256)[:, :, 0:128]
                second = PR[gr % 2][:, 1024:1536].rearrange("p (j q) -> p j q", q=128)
                pool.wait_ge(masked, 2 * n)
                g.tensor_tensor(NOTE[:, :], ONES[:, 0:1], ONES[:, 0:1], ALU.mult)
                for part in (first, second):
                    g.affine_select(out=part, in_=part, compare_op=ALU.is_ge, fill=0.0, base=0,
                                    pattern=[[0, 4], [1, 128]], channel_multiplier=-1).then_inc(masked, 1)

            def sequence(b, last):
                for gr in range(GROUPS):
                    if gr == 0:
                        q_k_stack(b, 3)
                    elif not last:
                        q_k_stack(b + 1, gr - 1)
                    causal_select(b, gr)

            for gr in range(3):
                q_k_stack(0, gr)
            sequence(0, False)
            with pool.Fori(0, 7) as k:
                sequence(2 * k + 1, False)
                sequence(2 * k + 2, False)
            sequence(15, True)

            def rstd_chunk(c):
                pool.wait_ge(c_var, c + 1)
                g.tensor_tensor(RSC, VAR, EPS4[:, :], ALU.add).then_inc(c_rs, 1)
                pool.wait_ge(c_rs, c + 1)
                g.tensor_tensor(RSC, RSC, EPST[:, 0:4], ALU.pow).then_inc(c_rstd, 1)

            def low_hidden(c, u):
                n = c * UNITS + u
                pool.wait_ge(e_hi, n + 1)
                g.tensor_tensor(PRL[u % 3], PRF[u % 3], PRH[u % 3], ALU.subtract).then_inc(e_lo, 1)

            rstd_chunk(0)
            for k in range(UNITS // STAGE_UNITS):
                cols = slice(k * STAGE_UNITS * 128, (k + 1) * STAGE_UNITS * 128)
                pool.wait_ge(wd_hi, k + 1)
                g.tensor_tensor(WDL[:, cols], WD[:, cols], WDH[:, cols], ALU.subtract).then_inc(wd_lo, 1)
            for u in range(4):
                low_hidden(0, u)
            with pool.Fori(0, CHUNKS - 1) as c:
                for u in range(4, UNITS):
                    low_hidden(c, u)
                    if u == PREP["rstd"]:
                        rstd_chunk(c + 1)
                for u in range(4):
                    low_hidden(c + 1, u)
            for u in range(4, UNITS):
                low_hidden(CHUNKS - 1, u)

        @block.scalar
        def _(act):
            s = nc.scalar
            act.wait_ge(ld_cf, 16)
            s.activation(IDR[:, :], ident, ACT.Copy).then_inc(ident_r, 1)
            act.wait_ge(a_mm, 1)
            s.activation(CST[1], PA[:, 0:B], ACT.Copy).then_inc(a_cp, 1)
            act.wait_ge(a_mm, 2)
            s.activation(CST[2], PB[:, 0:B], ACT.Copy).then_inc(a_cp, 1)
            split_hi(act)

            def scan_step(t, par):
                for h in range(2):
                    act.wait_ge(gates[h], t + 1)
                    for k, (f, bias) in enumerate(((ACT.Tanh, 2), (ACT.Sigmoid, 1), (ACT.Sigmoid, 0))):
                        col = (2, 1, 0)[k] * 128
                        s.activation(SG[h][:, col:col + 128], GATE[h][par][:, col:col + 128], f,
                                     bias=VEC[:, bias:bias + 1]).then_inc(acts[h], 1)

            act.wait_ge(ld_vec, 16)
            with act.Fori(0, B // 2) as k:
                scan_step(2 * k, 0)
                scan_step(2 * k + 1, 1)
            act.wait_ge(cu_mm, 1)
            s.activation(CU, PB[:, 0:256], ACT.Copy).then_inc(cu_cp, 1)
            with act.Fori(0, CHUNKS) as i:
                act.wait_ge(ro_add, i + 1)
                act.wait_ge(ro_tr, i)
                s.activation(ROT[:, 512:1024], ROT[:, 0:512], ACT.Tanh, bias=VEC[:, 3:4]).then_inc(ro_tanh, 1)

            def split_sequence(b):
                act.wait_ge(t_tr, b + 1)
                if not begins(b):
                    act.wait_ge(qk_mm, GROUPS * b)
                s.activation(TH, PAS, ACT.Copy).then_inc(t_hi, 1)

            def values(b, par):
                act.wait_ge(v_mm, b + 1)
                s.activation(VPB[par][:, :, :, 0:HD],
                             PAS.rearrange("p (t h d) -> p t h d", t=2, d=HD), ACT.Copy).then_inc(v_cp, 1)

            def hi_slots(b, gr):
                n = b * GROUPS + gr
                act.wait_ge(qk_pos, n + 1)
                s.activation(HM[gr % 2][:, 0:256], QKF[gr % 2][:, 0:256], ACT.Copy,
                             scale=CF[:, C_QLO:C_QLO + 1]).then_inc(qk_hi, 1)
                s.activation(HM[gr % 2][:, 256:512], QKF[gr % 2][:, 256:512], ACT.Copy,
                             scale=CF[:, C_KLO:C_KLO + 1]).then_inc(qk_hi, 1)

            def u_copy(b, gr):
                n = b * GROUPS + gr
                act.wait_ge(pv_mm, n + 1)
                s.activation(US[:, :], PBU, ACT.Copy).then_inc(u_cp, 1)

            def o_copy(b):
                act.wait_ge(o_tr, b + 1)
                s.activation(OT[:, :], PAS, ACT.Copy).then_inc(o_cp, 1)

            def exps(b, gr):
                n = b * GROUPS + gr
                act.wait_ge(st_mm, n + 1)
                if not begins(b) or gr >= 2:
                    act.wait_ge(pv_mm, n - 1)
                s.activation(PR[gr % 2], PT[:, :], ACT.Exp, scale=SCALE).then_inc(prob, 1)

            def sequence(b, par, first, last):
                for gr in range(GROUPS):
                    if gr >= 2:
                        u_copy(b, gr - 2)
                    elif not first:
                        u_copy(b - 1, gr + 2)
                    if gr == 0:
                        hi_slots(b, 3)
                    elif not last:
                        hi_slots(b + 1, gr - 1)
                    if gr == 0 and not last:
                        split_sequence(b + 1)
                    exps(b, gr)
                    if gr == 1 and not last:
                        values(b + 1, 1 - par)
                    if gr == 2 and not first:
                        o_copy(b - 1)

            act.wait_ge(zeroed, 8)
            split_sequence(0)
            values(0, 0)
            for gr in range(3):
                hi_slots(0, gr)
            sequence(0, 0, True, False)
            with act.Fori(0, 7) as k:
                sequence(2 * k + 1, 1, False, False)
                sequence(2 * k + 2, 0, False, False)
            sequence(15, 1, False, True)
            u_copy(15, 2)
            u_copy(15, 3)
            o_copy(15)

            def high_chunk(c):
                act.wait_ge(c_tr, c + 1)
                s.activation(YHI[:, ncols(c, CHUNK)], PA[:, :], ACT.Copy).then_inc(c_hi, 1)

            def exp_logits(c):
                act.wait_ge(g_mm, c + 1)
                s.activation(TURN, PA[:, :], ACT.Exp, scale=-1.0).then_inc(g_exp, 1)

            def routing(c):
                act.wait_ge(g_cwtr, c + 1)
                if not begins(c):
                    act.wait_ge(e_cw, PAIRS * c)
                s.activation(CWT[:, :], PAH[:, 0:CHUNK], ACT.Copy).then_inc(g_cwt, 1)

            def silu(c, u):
                n = c * UNITS + u
                act.wait_ge(e_gate, n + 1)
                if not (begins(c) and u < 2):
                    act.wait_ge(e_prod, n if u == 0 else n - 1)
                s.activation(SIL[u % 2], EG[u % 2], ACT.Silu).then_inc(e_silu, 1)

            def high_hidden(c, u):
                n = c * UNITS + u
                act.wait_ge(e_prod, n + 1)
                if not (begins(c) and u < 3):
                    act.wait_ge(e_down, n - 2)
                s.activation(PRH[u % 3], PRF[u % 3], ACT.Copy).then_inc(e_hi, 1)

            def copy_sum(c):
                act.wait_ge(e_down, (c + 1) * UNITS)
                s.activation(TURN, PB[:, :], ACT.Copy).then_inc(y_cp, 1)

            def body(c, last):
                for u in range(4, UNITS):
                    silu(c, u)
                    high_hidden(c, u - 1)
                    if not last:
                        if u == PREP["turn"]:
                            high_chunk(c + 1)
                        if u == PREP["exp"]:
                            exp_logits(c + 1)
                        if u == PREP["turn_weights"]:
                            routing(c + 1)

            high_chunk(0)
            exp_logits(0)
            act.wait_ge(ld_wd, 16)
            act.wait_ge(x3_done, B)
            for k in range(UNITS // STAGE_UNITS):
                cols = slice(k * STAGE_UNITS * 128, (k + 1) * STAGE_UNITS * 128)
                s.activation(WDH[:, cols], WD[:, cols], ACT.Copy).then_inc(wd_hi, 1)
            routing(0)
            silu(0, 0)
            for u in range(1, 4):
                silu(0, u)
                high_hidden(0, u - 1)
            with act.Fori(0, CHUNKS - 1) as c:
                body(c, False)
                silu(c + 1, 0)
                high_hidden(c, UNITS - 1)
                for u in range(1, 4):
                    silu(c + 1, u)
                    high_hidden(c + 1, u - 1)
                copy_sum(c)
            body(CHUNKS - 1, True)
            high_hidden(CHUNKS - 1, UNITS - 1)
            copy_sum(CHUNKS - 1)

        @block.tensor
        def _(pe):
            mm = nc.tensor.matmul

            def three(out_, wn_h, wn_l, y_h, y_l, start, stop=False, skip=True):
                mm(out_, wn_h, y_h, start=start, stop=False, skip_group_check=skip)
                mm(out_, wn_h, y_l, start=False, stop=False, skip_group_check=skip)
                return mm(out_, wn_l, y_h, start=False, stop=stop, skip_group_check=skip)

            pe.wait_ge(consts, 7)
            pe.wait_ge(ident_r, 1)
            pe.wait_ge(ld_w, 16)
            pe.wait_ge(a_rows, 2)
            mm(PA[:, 0:B], ONES[:, :], CST[0], start=True, stop=False, skip_group_check=True)
            for T in range(TILES):
                ins = mm(PA[:, T // 2:T // 2 + 1], X[:, T * D:(T + 1) * D], RS[:, T:T + 1], start=False,
                         stop=(T == TILES - 1), skip_group_check=True)
            ins.then_inc(a_mm, 1)
            pe.wait_ge(a_cp, 1)
            mm(PB[:, 0:B], w(WV0), CST[1], start=True, stop=True).then_inc(a_mm, 1)
            pe.wait_ge(a_cp, 2)
            for b in range(B):
                bank = PS[:, b // 4 * 512:b // 4 * 512 + 512] if b < 12 else PT[:, 0:512]
                ins = mm(bank[:, b % 4 * 128:b % 4 * 128 + 128], CST[2][:, b:b + 1].broadcast_to([P, P]), w(WO0),
                         start=True, stop=True)
                if b % 4 == 3:
                    ins.then_inc(a_mm, 1)

            transpose_tiles(pe)

            def inputs_part(t, h, par):
                bank = GATE[h][par]
                cols = bass.ds(t * S + h * 128, 128)
                for k, n in enumerate((WF, WI, WC)):
                    three(bank[:, k * 128:(k + 1) * 128], wh(n), wl(n), YHI[:, cols], YLO[:, cols], start=(k == 0))

            def cell_part(t, h, par):
                pe.wait_ge(cell[h], 3 * t)
                bank = GATE[h][par]
                for k, n in ((2, UC), (1, UI), (0, UF)):
                    ins = mm(bank[:, k * 128:(k + 1) * 128], w(n), C[h], start=False, stop=True, skip_group_check=True)
                ins.then_inc(gates[h], 1)

            def scan_step(t, par, more=True):
                for h in range(2):
                    cell_part(t, h, par)
                    if more:
                        inputs_part(t + 1, h, 1 - par)

            pe.wait_ge(small_split, 2)
            pe.wait_ge(c_init, 2)
            for p in range(2):
                pe.wait_ge(lo[p], CHUNKS // 2)
            pe.wait_ge(x1_done, 4)
            for h in range(2):
                inputs_part(0, h, 0)
            with pe.Fori(0, B // 2 - 1) as k:
                scan_step(2 * k, 0)
                scan_step(2 * k + 1, 1)
            scan_step(B - 2, 0)
            scan_step(B - 1, 1, more=False)

            for h in range(2):
                pe.wait_ge(cell[h], 3 * B)
                ins = mm(PB[:, h * 128:(h + 1) * 128], w(UO), C[h], start=(h == 0), stop=True, skip_group_check=True)
            ins.then_inc(cu_mm, 1)
            with pe.Fori(0, CHUNKS) as i:
                pe.wait_ge(ro_add, i)
                cols = ncols(i, CHUNK)
                three(PA[:, :], wh(WO), wl(WO), YHI[:, cols], YLO[:, cols], start=True, stop=True).then_inc(ro_mm, 1)
                pe.wait_ge(ro_tanh, i + 1)
                pe.wait_ge(ro_x, i)
                for t in range(4):
                    ins = nc.tensor.transpose(PS[:, t * 128:(t + 1) * 128], ROT[:, 512 + t * 128:640 + t * 128], ident)
                ins.then_inc(ro_tr, 1)

            def transpose_sequence(b):
                pe.wait_ge(t_norm, 2 * b + 2)
                if not begins(b):
                    pe.wait_ge(qk_pos, GROUPS * b)
                for t in range(2):
                    ins = nc.tensor.transpose(PAS[:, t * 128:(t + 1) * 128], OH2[:, t * 128:(t + 1) * 128], ident)
                ins.then_inc(t_tr, 1)

            def values(b):
                if begins(b):
                    pe.wait_ge(t_hi, 1)
                    pe.wait_ge(t_lo, 1)
                else:
                    pe.wait_ge(qk_pos, GROUPS * b + 1)
                for t in range(2):
                    rows = slice(t * 128, (t + 1) * 128)
                    dst = PAS[:, rows]
                    mm(dst, TH[:, rows], wh(WV1), start=True, stop=False, skip_group_check=True)
                    mm(dst, TH[:, rows], wl(WV1), start=False, stop=False, skip_group_check=True)
                    ins = mm(dst, TL[:, rows], wh(WV1), start=False, stop=True, skip_group_check=True)
                ins.then_inc(v_mm, 1)

            def q_k(b, gr):
                n = b * GROUPS + gr
                if gr == 0:
                    pe.wait_ge(v_cp if begins(b) else t_lo, b + 1)
                    if not begins(b):
                        pe.wait_ge(t_hi, b + 1)
                elif gr == 1 and not begins(b):
                    pe.wait_ge(v_cp, b + 1)
                elif gr == 2 and not (isinstance(b, int) and b <= 1):
                    pe.wait_ge(o_cp, b - 1)
                elif gr == 3 and not (isinstance(b, int) and b <= 1):
                    pe.wait_ge(x3_done, b - 1)
                if not begins(b) or gr > 0:
                    pe.wait_ge(qk_pos, n)
                cols = slice(gr * 128, (gr + 1) * 128)
                for m in range(2):
                    ins = three(PA[:, m * 256:(m + 1) * 256], WQK[m][0][:, cols], WQK[m][1][:, cols], TH, TL,
                                start=True, stop=True, skip=False)
                ins.then_inc(qk_mm, 1)

            def scores_first(b, gr):
                n = b * GROUPS + gr
                pe.wait_ge(km[gr], 64 * (b + 1))
                if not begins(b) or gr > 0:
                    pe.wait_ge(s_max, 3 * n - 2)
                keys = KM[gr].rearrange("p (j k) -> p j k", k=256)
                dst = PS[:, 0:512].rearrange("p (j k) -> p j k", k=128)
                mm(dst, QS[gr][:, 0:128], keys[:, :, 0:128], start=True, stop=True, skip_group_check=True)
                mm(dst, ident_bf, causal.unsqueeze(1).broadcast_to([P, 4, 128]), start=False, stop=True,
                   skip_group_check=True).then_inc(s_mm, 1)

            def scores_second(b, gr, j):
                n = b * GROUPS + gr
                if not begins(b) or gr > 0:
                    if j == 0:
                        pe.wait_ge(s_max, 3 * n - 1)
                    else:
                        pe.wait_ge(q_shift, n)
                dst = PS[:, 512 + j * 256:1024 + j * 256]
                mm(dst, QS[gr][:, 128:256], KM[gr][:, j * 256:(j + 2) * 256], start=True, stop=True,
                   skip_group_check=True)
                mm(dst.rearrange("p (j k) -> p j k", k=256)[:, :, 128:256], ident_bf,
                   causal.unsqueeze(1).broadcast_to([P, 2, 128]), start=False, stop=True,
                   skip_group_check=True).then_inc(s_mm, 1)

            def shift_rows(b, gr):
                n = b * GROUPS + gr
                pe.wait_ge(m_neg, n + 1)
                for t in range(2):
                    cols = slice(t * 128, (t + 1) * 128)
                    ins = mm(MTP[:, cols], M2[:, cols], IDR[:, :], start=True, stop=True)
                ins.then_inc(m_tr, 1)

            def scores_t(b, gr):
                n = b * GROUPS + gr
                pe.wait_ge(q_shift, n + 1)
                if not begins(b) or gr > 0:
                    pe.wait_ge(prob, n)
                q = Q2[gr % 2]
                for j in range(4):
                    mm(PT[:, j * 256:(j + 1) * 256], KM[gr][:, j * 256:j * 256 + 128], q, start=True, stop=True)
                for j in range(4):
                    ins = mm(PT[:, 1024 + j * 128:1152 + j * 128], KM[gr][:, j * 256 + 128:j * 256 + 256],
                             q[:, 128:256], start=True, stop=True)
                ins.then_inc(st_mm, 1)

            def probs_values(b, gr, par):
                n = b * GROUPS + gr
                if not begins(b) or gr > 0:
                    pe.wait_ge(o_norm, n)
                pe.wait_ge(masked, 2 * n + 2)
                for j in range(4):
                    h = GROUPS * gr + j
                    dst = PB[32 * j:32 * j + 32, 0:256]
                    mm(dst, VPB[par][:, 0, h, :], PR[gr % 2][:, j * 256:(j + 1) * 256], start=True, stop=True,
                       tile_position=(0, 32 * j), skip_group_check=True)
                for j in range(4):
                    h = GROUPS * gr + j
                    ins = mm(PB[32 * j:32 * j + 32, 128:256], VPB[par][:, 1, h, :],
                             PR[gr % 2][:, 1024 + j * 128:1152 + j * 128], start=False, stop=True,
                             tile_position=(0, 32 * j), skip_group_check=True)
                ins.then_inc(pv_mm, 1)

            def transpose_u(b, gr):
                n = b * GROUPS + gr
                pe.wait_ge(u_cp, n + 1)
                for t in range(2):
                    cols = slice(t * 128, (t + 1) * 128)
                    ins = nc.tensor.transpose(PBU[:, cols], US[:, cols], ident)
                ins.then_inc(u_tr, 1)

            def transpose_o(b, par):
                pe.wait_ge(o_norm, GROUPS * b + 4)
                for t in range(2):
                    cols = slice(t * 128, (t + 1) * 128)
                    ins = nc.tensor.transpose(PAS[:, cols], OH[par][:, cols], ident)
                ins.then_inc(o_tr, 1)

            def project_o(b):
                pe.wait_ge(o_cp, b + 1)
                for t in range(2):
                    cols = slice(t * 128, (t + 1) * 128)
                    ins = mm(PAS[:, cols], OT[:, cols], w(WO1), start=True, stop=True, skip_group_check=True)
                ins.then_inc(o_mm, 1)

            def sequence(b, par, first, last):
                for gr in range(GROUPS):
                    ahead = (b, gr + 1) if gr < 3 else (b + 1, 0)
                    if gr < 3 or not last:
                        scores_first(*ahead)
                        scores_second(*ahead, 0)
                    shift_rows(b, gr)
                    if gr == 0:
                        q_k(b, 3)
                    elif not last:
                        q_k(b + 1, gr - 1)
                    older = (b, gr - 2, par) if gr >= 2 else (b - 1, gr + 2, 1 - par)
                    if gr >= 2 or not first:
                        if gr == 2:
                            pe.wait_ge(v_cp, b + 1)
                        probs_values(*older)
                    if gr < 3 or not last:
                        scores_second(*ahead, 2)
                    if gr == 0 and not last:
                        transpose_sequence(b + 1)
                    scores_t(b, gr)
                    if gr >= 2 or not first:
                        transpose_u(older[0], older[1])
                    if gr == 1 and not last:
                        values(b + 1)
                    if gr >= 2 and not first:
                        if last:
                            pe.wait_ge(x3_done if gr == 2 else o_cp, b - 1 if gr == 2 else b)
                        else:
                            pe.wait_ge(qk_pos, GROUPS * (b + 1) + gr)
                        if gr == 2:
                            transpose_o(b - 1, 1 - par)
                        else:
                            project_o(b - 1)

            pe.wait_ge(ld_cb, 16)
            pe.wait_ge(zeroed, 8)
            pe.wait_ge(qk_split, 12)
            transpose_sequence(0)
            values(0)
            for gr in range(3):
                q_k(0, gr)
            scores_first(0, 0)
            scores_second(0, 0, 0)
            scores_second(0, 0, 2)
            sequence(0, 0, True, False)
            with pe.Fori(0, 7) as k:
                sequence(2 * k + 1, 1, False, False)
                sequence(2 * k + 2, 0, False, False)
            sequence(15, 1, False, True)
            for gr in (2, 3):
                probs_values(15, gr, 1)
                transpose_u(15, gr)
            pe.wait_ge(x3_done, 15)
            transpose_o(15, 1)
            project_o(15)

            def turn_chunk(c):
                pe.wait_ge(c_norm, 4 * c + 4)
                if begins(c):
                    pe.wait_ge(x3_done, B)
                elif isinstance(c, int):
                    pe.wait_ge(g_cwt, c)
                else:
                    pe.wait_ge(x4_done, c - 1)
                for t in range(4):
                    cols = slice(t * 128, (t + 1) * 128)
                    ins = nc.tensor.transpose(PA[:, cols], YNC[:, cols], ident)
                ins.then_inc(c_tr, 1)

            def gate_logits(c):
                pe.wait_ge(c_lo, c + 1)
                cols = ncols(c, CHUNK)
                three(PA[:, :], wh(GW), wl(GW), YHI[:, cols], YLO[:, cols], start=True, stop=True).then_inc(g_mm, 1)

            def turn_exp(c):
                pe.wait_ge(g_exp, c + 1)
                for t in range(4):
                    cols = slice(t * 128, (t + 1) * 128)
                    ins = nc.tensor.transpose(PA[:, cols], TURN[:, cols], ident)
                ins.then_inc(g_tr, 1)

            def turn_weights(c):
                pe.wait_ge(g_cw, c + 1)
                for t in range(4):
                    cols = slice(t * 128, (t + 1) * 128)
                    ins = nc.tensor.transpose(PAH[:, cols], CWS[:, cols], ident_h)
                ins.then_inc(g_cwtr, 1)

            def hidden(c, u):
                n = c * UNITS + u
                at = u * 256
                cols = ncols(c, CHUNK)
                if not (begins(c) and u < 2):
                    pe.wait_ge(e_silu, n if u == 0 else n - 1)
                three(EG[u % 2], GUH[:, at:at + 128], GUL[:, at:at + 128], YHI[:, cols], YLO[:, cols],
                      start=True, stop=True).then_inc(e_gate, 1)
                if u >= 2:
                    pe.wait_ge(e_act, c * PAIRS + u - 1)
                elif u == 0 and not begins(c):
                    pe.wait_ge(e_prod, n)
                three(EU[u % 2], GUH[:, at + 128:at + 256], GUL[:, at + 128:at + 256], YHI[:, cols], YLO[:, cols],
                      start=True, stop=True).then_inc(e_up, 1)
                if u < PAIRS:
                    if u == 0:
                        pe.wait_ge(g_cwt, c + 1)
                    elif u >= 2:
                        pe.wait_ge(e_prod, n - 1)
                    mm(EC[u % 2], SEL[:, u * 128:(u + 1) * 128], CWT[:, :],
                       start=True, stop=True).then_inc(e_cw, 1)

            def down(c, u):
                n = c * UNITS + u
                cols = slice(u * 128, (u + 1) * 128)
                if u == 0 and not begins(c):
                    pe.wait_ge(y_cp, c)
                pe.wait_ge(e_hi, n + 1)
                mm(PB[:, :], WDH[:, cols], PRH[u % 3], start=(u == 0), stop=False)
                mm(PB[:, :], WDL[:, cols], PRH[u % 3], start=False, stop=False)
                pe.wait_ge(e_lo, n + 1)
                mm(PB[:, :], WDH[:, cols], PRL[u % 3], start=False, stop=(u == UNITS - 1)).then_inc(e_down, 1)

            def turn_sum(c, last):
                pe.wait_ge(y_cp, c + 1)
                pe.wait_ge(g_cwt, CHUNKS if last else c + 2)
                for t in range(4):
                    cols = slice(t * 128, (t + 1) * 128)
                    ins = nc.tensor.transpose(PA[:, cols], TURN[:, cols], ident)
                ins.then_inc(y_tr, 1)

            def body(c, last):
                down(c, 0)
                for u in range(4, UNITS):
                    hidden(c, u)
                    if not last:
                        if u == PREP["turn"]:
                            turn_chunk(c + 1)
                        if u == PREP["logits"]:
                            gate_logits(c + 1)
                        if u == PREP["turn_exp"]:
                            turn_exp(c + 1)
                        if u == PREP["turn_weights"]:
                            turn_weights(c + 1)
                    down(c, u - 3)

            turn_chunk(0)
            gate_logits(0)
            turn_exp(0)
            pe.wait_ge(ld_sel, 16)
            turn_weights(0)
            pe.wait_ge(gu_split, 2 * (UNITS // STAGE_UNITS))
            for u in range(4):
                hidden(0, u)
            pe.wait_ge(wd_lo, UNITS // STAGE_UNITS)
            with pe.Fori(0, CHUNKS - 1) as c:
                body(c, False)
                for u in range(3):
                    hidden(c + 1, u)
                    down(c, UNITS - 3 + u)
                hidden(c + 1, 3)
                turn_sum(c, False)
            body(CHUNKS - 1, True)
            for u in range(3):
                down(CHUNKS - 1, UNITS - 3 + u)
            turn_sum(CHUNKS - 1, True)

        @block.vector
        def _(dve):
            v = nc.vector

            def row_stats(k):
                ch = Chain(dve, stats[k])
                with dve.Fori(0, TILES // 4) as i:
                    for t in range(4):
                        ch.did(v.bn_stats(BN[:, bass.ds((4 * i + t) * 6, 6)], X[:, bass.ds((4 * i + t) * D, D)]))
                ch.at(TILES)
                ch.settle()
                mean_e, m2_e, mean_o, m2_o = (BN[:, col:6 * TILES:6] for col in (1, 2, 4, 5))
                mean, var = MV[:, 0:2 * TILES:2], MV[:, 1:2 * TILES:2]
                ch.did(v.tensor_tensor(NMR[:, :], mean_e, mean_o, ALU.subtract))
                ch.did(v.tensor_tensor(mean, mean_e, mean_o, ALU.add))
                ch.did(v.tensor_tensor(var, m2_e, m2_o, ALU.add))
                ch.settle()
                ch.did(v.scalar_tensor_tensor(NMR[:, :], NMR[:, :], 0.25, NMR[:, :], ALU.mult, ALU.mult))
                ch.did(v.tensor_scalar(mean, mean, 0.5, None, ALU.mult))
                ch.settle()
                ch.did(v.scalar_tensor_tensor(var, var, 1.0 / D, NMR[:, :], ALU.mult, ALU.add))
                ch.settle()

            dve.wait_ge(ld_x, 16)
            row_stats(0)
            dve.wait_ge(rstd[0], 1)
            v.scalar_tensor_tensor(NMR[:, :], MV[:, 0:2 * TILES:2], -1.0, RS[:, :], ALU.mult, ALU.mult).then_inc(a_rows, 1)
            dve.wait_ge(a_rows, 1)
            v.tensor_tensor(CST[0], NMR[:, 0:TILES:2], NMR[:, 1:TILES:2], ALU.add).then_inc(a_rows, 1)
            for q in range(4):
                bank = PS[:, q * 512:(q + 1) * 512] if q < 3 else PT[:, 0:512]
                dve.wait_ge(a_mm, 3 + q)
                xs = X[:, q * 1024:(q + 1) * 1024].rearrange("p (b h d) -> p b h d", h=2, d=D)
                v.tensor_tensor(xs, xs, bank.rearrange("p (b d) -> p b d", d=D).unsqueeze(2).broadcast_to([P, 4, 2, D]),
                                ALU.add).then_inc(x1_done, 1)

            dve.wait_ge(x1_done, 4)
            row_stats(1)
            dve.wait_ge(rstd[1], 1)
            normalise_and_lo(dve)

            dve.wait_ge(ld_vec, 16)
            for h in range(2):
                v.tensor_copy(C[h], VEC[:, 4:5].broadcast_to([P, 128])).then_inc(c_init, 1)

            def scan_step(t):
                for h in range(2):
                    f, i, gg = (SG[h][:, k * 128:(k + 1) * 128] for k in range(3))
                    dve.wait_ge(acts[h], 3 * t + 2)
                    v.tensor_tensor(TMP[h], i, gg, ALU.mult).then_inc(cell[h], 1)
                    dve.wait_ge(acts[h], 3 * t + 3)
                    dve.wait_ge(c_init, 2)
                    v.tensor_tensor(C[h], f, C[h], ALU.mult).then_inc(cell[h], 1)
                    dve.wait_ge(cell[h], 3 * t + 2)
                    v.tensor_tensor(C[h], C[h], TMP[h], ALU.add).then_inc(cell[h], 1)
                    dve.wait_ge(cell[h], 3 * t + 3)

            with dve.Fori(0, B) as t:
                scan_step(t)

            dve.wait_ge(cu_cp, 1)
            with dve.Fori(0, CHUNKS) as i:
                dve.wait_ge(ro_mm, i + 1)
                dve.wait_ge(ro_tanh, i)
                v.tensor_tensor(ROT[:, 0:512].rearrange("p (b s) -> p b s", b=2),
                                PA[:, :].rearrange("p (b s) -> p b s", b=2),
                                CU.unsqueeze(1).broadcast_to([P, 2, S]), ALU.add).then_inc(ro_add, 1)
                dve.wait_ge(ro_tr, i + 1)
                v.tensor_tensor(X[:, ncols(i, CHUNK)], X[:, ncols(i, CHUNK)], PS[:, 0:512], ALU.add).then_inc(ro_x, 1)

            dve.wait_ge(ro_x, CHUNKS)
            row_stats(2)
            dve.wait_ge(rstd[2], 1)

            def norm_sequence(b):
                if not begins(b):
                    dve.wait_ge(t_tr, b)
                for t in range(2):
                    at = 2 * b + t
                    v.tensor_scalar(OH2[:, t * 128:(t + 1) * 128], X[:, bass.ds(at * D, D)], MV[:, bass.ds(at * 2, 1)],
                                    RS[:, bass.ds(at, 1)], ALU.subtract, ALU.mult).then_inc(t_norm, 1)

            def lo_sequence(b):
                dve.wait_ge(t_hi, b + 1)
                v.tensor_tensor(TL, PAS, TH, ALU.subtract).then_inc(t_lo, 1)

            def positions(b, gr):
                n = b * GROUPS + gr
                dve.wait_ge(qk_mm, n + 1)
                if not begins(b) or gr >= 2:
                    dve.wait_ge(stack, n - 1)
                v.tensor_tensor(QKF[gr % 2], PA[:, :], pos, ALU.add).then_inc(qk_pos, 1)

            def shift_q(b, gr):
                n = b * GROUPS + gr
                dve.wait_ge(m_tr, n + 1)
                if not begins(b) or gr >= 2:
                    dve.wait_ge(st_mm, n - 1)
                v.tensor_tensor(Q2[gr % 2], QS[gr], MTP, ALU.add).then_inc(q_shift, 1)

            def maxima(b, gr, bank):
                n = b * GROUPS + gr
                dve.wait_ge(s_mm, 3 * n + bank + 1)
                if bank == 0 and (not begins(b) or gr > 0):
                    dve.wait_ge(m_neg, n)
                col, k = ((0, 128), (4, 256), (6, 256))[bank]
                v.tensor_reduce(MX[:, col:col + 512 // k], PS[:, bank * 512:(bank + 1) * 512].rearrange(
                    "p (j k) -> p j k", k=k), AX.X, ALU.max).then_inc(s_max, 1)

            def negate_maxima(b, gr):
                n = b * GROUPS + gr
                dve.wait_ge(s_max, 3 * n + 3)
                if not begins(b) or gr > 0:
                    dve.wait_ge(m_tr, n)
                v.tensor_scalar(M2[:, 0:256:32], MX[:, :], -1.0, None, ALU.mult).then_inc(m_neg, 1)

            def normalise_o(b, gr, par):
                n = b * GROUPS + gr
                dve.wait_ge(u_tr, n + 1)
                if not begins(b) or gr > 0:
                    dve.wait_ge(o_norm, n)
                if not begins(b) and gr == 0:
                    dve.wait_ge(o_tr, b - 1)
                u = PBU.rearrange("p (t j c) -> p t j c", t=2, c=32)
                rd = RD[:, :].rearrange("p (t j) -> p t j", t=2)
                v.reciprocal(rd, u[:, :, :, HD]).then_inc(u_rec, 1)
                dve.wait_ge(u_rec, n + 1)
                o = OH[par].rearrange("p (t g j c) -> p t g j c", t=2, g=4, c=HD)[:, :, gr, :, :]
                v.tensor_tensor(o, u[:, :, :, 0:HD], rd.unsqueeze(3).broadcast_to([P, 2, 4, HD]), ALU.mult
                                ).then_inc(o_norm, 1)

            def add_o(b):
                dve.wait_ge(o_mm, b + 1)
                v.tensor_tensor(X[:, ncols(b, 256)], X[:, ncols(b, 256)], PAS, ALU.add).then_inc(x3_done, 1)

            def sequence(b, par, first, last):
                for gr in range(GROUPS):
                    ahead = (b, gr + 1) if gr < 3 else (b + 1, 0)
                    more = gr < 3 or not last
                    if more:
                        maxima(*ahead, 0)
                    shift_q(b, gr)
                    if gr == 0:
                        positions(b, 3)
                    elif not last:
                        positions(b + 1, gr - 1)
                    if gr == 0 and not last:
                        norm_sequence(b + 1)
                    if more:
                        maxima(*ahead, 1)
                        maxima(*ahead, 2)
                        negate_maxima(*ahead)
                    if gr == 0 and not last:
                        lo_sequence(b + 1)
                    if gr >= 2:
                        normalise_o(b, gr - 2, par)
                    elif not first:
                        normalise_o(b - 1, gr + 2, 1 - par)
                    if gr == 3 and not first:
                        add_o(b - 1)

            dve.wait_ge(zeroed, 8)
            dve.wait_ge(qk_split, 12)
            norm_sequence(0)
            lo_sequence(0)
            for gr in range(3):
                positions(0, gr)
            for bank in range(3):
                maxima(0, 0, bank)
            negate_maxima(0, 0)
            sequence(0, 0, True, False)
            with dve.Fori(0, 7) as k:
                sequence(2 * k + 1, 1, False, False)
                sequence(2 * k + 2, 0, False, False)
            sequence(15, 1, False, True)
            normalise_o(15, 2, 1)
            normalise_o(15, 3, 1)
            add_o(15)

            G4 = 4 * 8
            sig, sc, t1, t2, t3, cw = (VP[:, k * 256:(k + 1) * 256] for k in range(6))
            gsc, rank, best = VP[:, 1536:1568], VP[:, 1568:1600], VP[:, 1600:1632]
            tot, rec = VP[:, 1632:1636], VP[:, 1636:1640]
            ch = Chain(dve, g_chain)
            PER = 47

            def tiles4(ap):
                return ap.rearrange("p (t e) -> p t e", t=4)

            def op(ins):
                ch.did(ins)
                ch.settle()

            def prepare(c, step):
                if step == "stats":
                    ch.at(PER * c)
                    for t in range(4):
                        ch.did(v.bn_stats(BNC[:, t * 6:(t + 1) * 6], X[:, bass.ds((4 * c + t) * D, D)]))
                elif step == "mean":
                    ch.settle()
                    ch.did(v.tensor_tensor(SPREAD, BNC[:, 1:24:6], BNC[:, 4:24:6], ALU.subtract))
                    ch.did(v.tensor_tensor(MEAN, BNC[:, 1:24:6], BNC[:, 4:24:6], ALU.add))
                    ch.did(v.tensor_tensor(VAR, BNC[:, 2:24:6], BNC[:, 5:24:6], ALU.add))
                elif step == "variance":
                    ch.settle()
                    ch.did(v.scalar_tensor_tensor(SPREAD, SPREAD, 0.25, SPREAD, ALU.mult, ALU.mult))
                    op(v.tensor_scalar(MEAN, MEAN, 0.5, None, ALU.mult))
                    v.scalar_tensor_tensor(VAR, VAR, 1.0 / D, SPREAD, ALU.mult, ALU.add).then_inc(c_var, 1)
                elif step == "normalise":
                    dve.wait_ge(c_rstd, c + 1)
                    for t in range(4):
                        v.tensor_scalar(YNC[:, t * 128:(t + 1) * 128], X[:, bass.ds((4 * c + t) * D, D)],
                                        MEAN[:, t:t + 1], RSC[:, t:t + 1], ALU.subtract, ALU.mult).then_inc(c_norm, 1)
                elif step == "low":
                    dve.wait_ge(c_hi, c + 1)
                    v.tensor_tensor(YLO[:, ncols(c, CHUNK)], PA[:, :], YHI[:, ncols(c, CHUNK)], ALU.subtract
                                    ).then_inc(c_lo, 1)
                elif step == "sigmoid":
                    dve.wait_ge(g_tr, c + 1)
                    v.tensor_scalar(tiles4(t1), tiles4(PA[:, :])[:, :, 0:NE], 1.0, None, ALU.add).then_inc(g_use, 1)
                    dve.wait_ge(g_use, c + 1)
                    op(v.reciprocal(sig, t1))
                elif step == "pairs":
                    op(v.tensor_tensor(tiles4(sc), tiles4(sig), BIAS[:, :].unsqueeze(1).broadcast_to([P, 4, NE]),
                                       ALU.add))
                    s8 = sc.rearrange("p (g k) -> p g k", k=8)
                    h1, l1 = (t1[:, k:k + 128].rearrange("p (g k) -> p g k", k=4) for k in (0, 128))
                    ch.did(v.tensor_tensor(h1, s8[:, :, 0:4], s8[:, :, 4:8], ALU.max))
                    ch.did(v.tensor_tensor(l1, s8[:, :, 0:4], s8[:, :, 4:8], ALU.min))
                elif step == "fours":
                    ch.settle()
                    h1, l1 = (t1[:, k:k + 128].rearrange("p (g k) -> p g k", k=4) for k in (0, 128))
                    h2, a2, b2 = (t2[:, k:k + 64].rearrange("p (g k) -> p g k", k=2) for k in (0, 64, 128))
                    ch.did(v.tensor_tensor(h2, h1[:, :, 0:2], h1[:, :, 2:4], ALU.max))
                    ch.did(v.tensor_tensor(a2, h1[:, :, 0:2], h1[:, :, 2:4], ALU.min))
                    op(v.tensor_tensor(b2, l1[:, :, 0:2], l1[:, :, 2:4], ALU.max))
                    ch.did(v.tensor_tensor(a2, a2, b2, ALU.max))
                elif step == "groups":
                    ch.settle()
                    h2, a2 = (t2[:, k:k + 64].rearrange("p (g k) -> p g k", k=2) for k in (0, 64))
                    h3, a3, b3 = t3[:, 0:32], t3[:, 32:64], t3[:, 64:96]
                    ch.did(v.tensor_tensor(h3, h2[:, :, 0], h2[:, :, 1], ALU.max))
                    ch.did(v.tensor_tensor(a3, h2[:, :, 0], h2[:, :, 1], ALU.min))
                    op(v.tensor_tensor(b3, a2[:, :, 0], a2[:, :, 1], ALU.max))
                    op(v.tensor_tensor(a3, a3, b3, ALU.max))
                    ch.did(v.tensor_tensor(gsc, h3, a3, ALU.add))
                elif step == "compare":
                    ch.settle()
                    gs = gsc.rearrange("p (t g) -> p t g", t=4)
                    other = gs.unsqueeze(2).broadcast_to([P, 4, 8, 8])
                    own = gs.unsqueeze(3).broadcast_to([P, 4, 8, 8])
                    ch.did(v.tensor_tensor(t1.rearrange("p (t g k) -> p t g k", t=4, k=8), other, own, ALU.is_gt))
                    op(v.tensor_tensor(t2.rearrange("p (t g k) -> p t g k", t=4, k=8), other, own, ALU.is_equal))
                    tri = CF[:, C_TRI:C_TRI + 64].unsqueeze(1).broadcast_to([P, 4, 64])
                    ch.did(v.tensor_tensor(tiles4(t2), tiles4(t2), tri, ALU.mult))
                elif step == "rank":
                    ch.settle()
                    op(v.tensor_tensor(t1, t1, t2, ALU.add))
                    ch.did(v.tensor_reduce(rank, t1.rearrange("p (g k) -> p g k", k=8), AX.X, ALU.add))
                elif step == "reach":
                    ch.settle()
                    op(v.tensor_scalar(rank, rank, 3.5, -BIG / 2, ALU.is_gt, ALU.mult))
                    ch.did(v.tensor_tensor(t3.rearrange("p (g k) -> p g k", k=8), sc.rearrange("p (g k) -> p g k", k=8),
                                           rank.unsqueeze(2).broadcast_to([P, G4, 8]), ALU.add))
                elif step == "best":
                    ch.settle()
                    ch.did(v.tensor_copy(tot, sig[:, 0:4]))
                    for t in range(4):
                        ch.did(v.max(best[:, t * 8:t * 8 + 8], t3[:, t * 64:(t + 1) * 64]))
                elif step == "replace":
                    ch.settle()
                    ch.did(v.tensor_copy(tot, sig[:, 0:4]))
                    for t in range(4):
                        ch.did(v.match_replace(t2[:, t * 64:(t + 1) * 64], best[:, t * 8:t * 8 + 8],
                                               t3[:, t * 64:(t + 1) * 64], -BIG))
                elif step == "chosen":
                    ch.settle()
                    op(v.tensor_tensor(t1, t2, t3, ALU.not_equal))
                    ch.did(v.tensor_tensor(t1, t1, sig, ALU.mult))
                elif step == "sum":
                    ch.settle()
                    op(v.tensor_reduce(tot, tiles4(t1), AX.X, ALU.add))
                    op(v.tensor_scalar(tot, tot, 1e-20, None, ALU.add))
                    ch.did(v.reciprocal(rec, tot))
                elif step == "weights":
                    ch.settle()
                    ch.did(v.scalar_tensor_tensor(tiles4(cw), tiles4(t1), ROUTED_SCALE,
                                                  rec.unsqueeze(2).broadcast_to([P, 4, NE]), ALU.mult, ALU.mult))
                elif step == "parts":
                    parts = CWS.rearrange("p (t k e) -> p t k e", t=4, k=2)
                    ch.settle()
                    op(v.tensor_copy(parts[:, :, 0, :], tiles4(cw)))
                    op(v.tensor_tensor(tiles4(t2), tiles4(cw), parts[:, :, 0, :], ALU.subtract))
                    v.tensor_scalar(parts[:, :, 1, :], tiles4(t2), LOW, None, ALU.mult).then_inc(g_cw, 1)
                    assert ch.n == PER, ch.n

            STEPS = ("stats", "mean", "variance", "normalise", "low", "sigmoid", "pairs", "fours", "groups", "compare",
                     "rank", "reach", "best", "replace", "chosen", "sum", "weights", "parts")

            def product(c, u):
                n = c * UNITS + u
                dve.wait_ge(e_silu, n + 1)
                dve.wait_ge(e_up, n + 1)
                if u < PAIRS:
                    v.tensor_tensor(SIL[u % 2], SIL[u % 2], EU[u % 2], ALU.mult).then_inc(e_act, 1)
                    dve.wait_ge(e_act, c * PAIRS + u + 1)
                    dve.wait_ge(e_cw, c * PAIRS + u + 1)
                if not (begins(c) and u < 3):
                    dve.wait_ge(e_lo, n - 2)
                v.tensor_tensor(PRF[u % 3], SIL[u % 2], EC[u % 2] if u < PAIRS else EU[u % 2], ALU.mult
                                ).then_inc(e_prod, 1)

            def add_sum(c):
                dve.wait_ge(y_tr, c + 1)
                v.tensor_tensor(X[:, ncols(c, CHUNK)], X[:, ncols(c, CHUNK)], PA[:, :], ALU.add).then_inc(x4_done, 1)

            def body(c, last):
                for u in range(4, UNITS):
                    product(c, u)
                    if not last:
                        for step in STEPS:
                            if u == PREP[step]:
                                prepare(c + 1, step)

            dve.wait_ge(ld_bias, 16)
            dve.wait_ge(x3_done, B)
            for step in STEPS:
                prepare(0, step)
            for u in range(4):
                product(0, u)
            with dve.Fori(0, CHUNKS - 1) as c:
                body(c, False)
                for u in range(4):
                    product(c + 1, u)
                add_sum(c)
            body(CHUNKS - 1, True)
            add_sum(CHUNKS - 1)


def kernel(**inputs):
    import numpy as np
    import concourse.bacc as bacc
    from concourse.bass_utils import run_bass_kernel_spmd

    a = {k: np.ascontiguousarray(v) for k, v in inputs.items()}
    f32 = np.float32

    gate = np.zeros((D, P), f32)
    gate[:, :NE] = a["L1_ffn_gate_w"].T
    mats = {
        WF: a["L0_ffn_wf"].T, WI: a["L0_ffn_wi"].T, WC: a["L0_ffn_wc"].T, WO: a["L0_ffn_wo"].T,
        WV1: a["L1_attn_Wv"], GW: gate, WV0: a["L0_attn_w_qkv"][2 * D:].T, WO0: a["L0_attn_w_o"].T,
        UF: a["L0_ffn_uf"].T, UI: a["L0_ffn_ui"].T, UC: a["L0_ffn_uc"].T, UO: a["L0_ffn_uo"].T,
        WO1: a["L1_attn_Wo"], WQ: a["L1_attn_Wq"], WK: a["L1_attn_Wk"],
    }
    small = np.ascontiguousarray(np.stack([mats[k] for k in range(15)], axis=1))
    vec = np.ascontiguousarray(np.stack([a[f"L0_ffn_{k}"] for k in ("bf", "bi", "bc", "bo", "in_c")], axis=1))
    gu = np.zeros((D, UNITS, 2, 2, FF), f32)
    wd = np.zeros((2, FF, UNITS, D), f32)
    for k, name in enumerate(("gate", "up")):
        gu[:, :PAIRS, k] = a[f"L1_ffn_We_{name}"].reshape(PAIRS, 2, D, FF).transpose(2, 0, 1, 3)
        gu[:, PAIRS, k, 0] = a[f"L1_ffn_Ws_{name}"]
    wd[:, :, :PAIRS] = a["L1_ffn_We_down"].reshape(PAIRS, 2, FF, D).transpose(1, 2, 0, 3)
    wd[0, :, PAIRS] = a["L1_ffn_Ws_down"]
    gu, wd = gu.reshape(D, UNITS, 256), wd.reshape(P, UNITS, D)

    cf = np.zeros((P, C_END), f32)
    cf[:, C_ID:C_ID + 128] = np.eye(P, dtype=f32)
    scale = 1.0 / (np.power(f32(10000.0), np.arange(0, HD, 2, dtype=f32) / f32(HD)) + np.finfo(f32).eps)
    angle = np.arange(S, dtype=f32)[:, None] * scale.astype(f32)[None, :]
    pos = np.stack([np.sin(angle), np.cos(angle)], axis=-1).reshape(S, HD).astype(f32)
    slot = np.arange(P) % 32
    for p in range(P):
        if slot[p] >= 8:
            cf[p, C_POS:C_POS + 256] = pos[:, p % 8]
            cf[p, C_POS + 256:C_POS + 512] = pos[:, p % 8]
    cf[slot == 0, C_POS + 256:C_POS + 512] = 1.0
    cf[(slot >= 16) & (slot < 24), C_QLO] = 1.0
    cf[slot >= 24, C_KLO] = 1.0
    cf[:, C_TRI:C_TRI + 64] = np.tril(np.ones((8, 8), f32), -1).reshape(1, 64)
    cb = np.zeros((P, 256), np.dtype(mybir.dt.np(BF16)))
    cb[:, :128] = np.eye(P)
    cb[:, 128:] = np.triu(np.full((P, P), -BIG, f32), 1)
    ch = np.zeros((P, PAIRS + 1, P), np.float16)
    for u in range(PAIRS):
        for k in range(2):
            ch[2 * u + k, u, k * FF:(k + 1) * FF] = 1.0
            ch[NE + 2 * u + k, u, k * FF:(k + 1) * FF] = 1.0 / LOW
    ch[:, PAIRS] = np.eye(P)
    ch = ch.reshape(P, (PAIRS + 1) * P)

    nc = bacc.Bacc("TRN2", target_bir_lowering=False, num_devices=1)
    arrays, args = {}, []
    for name, arr in (("x", a["L0_attn_x"]), ("small", small), ("vec", vec), ("gate_bias", a["L1_ffn_gate_bias"]),
                      ("gu", gu), ("wd", wd), ("cf32", cf), ("cbf", cb), ("cf16", ch)):
        arr = np.ascontiguousarray(arr)
        arrays[name] = arr
        args.append(nc.dram_tensor(name, arr.shape, mybir.dt.from_np(arr.dtype), kind="ExternalInput").ap())
    args.append(nc.dram_tensor("out", (B, S, D), F32, kind="ExternalOutput").ap())
    two_layers(nc, *args)
    r = run_bass_kernel_spmd(nc, [arrays], core_ids=[0])
    return r.results[0]["out"]
```

```python
import concourse.bass as bass
from concourse import mybir
from concourse.alu_op_type import AluOpType as ALU
from contextlib import ExitStack

F32 = mybir.dt.float32
F32R = mybir.dt.float32r
BF16 = mybir.dt.bfloat16
F16 = mybir.dt.float16
ACT = mybir.ActivationFunctionType
AX = mybir.AxisListType

P = 128
B, S, D = 16, 256, 128
TILES = B * S // P
HEADS, HD = 16, 8
GROUPS = 4
NE, FF = 64, 64
PAIRS = NE // 2
UNITS = PAIRS + 1
STAGE_UNITS = 3
CHUNK = 512
CHUNKS = B * S // CHUNK
EPS = 1e-5
QUARTER = TILES // 4
BIG = 3e38
SCALE = float(D) ** -0.5
ROUTED_SCALE = 2.5
LOW = 4096.0

WF, WI, WC, WO, WV1, GW, WV0, WO0, UF, UI, UC, UO, WO1, WQ, WK = range(15)
SPLIT = 6
PREP = {"stats": 4, "variance": 5, "rstd": 6, "normalise": 8, "turn": 11, "low": 12, "logits": 13,
        "exp": 13, "turn_exp": 16, "sigmoid": 17, "pairs": 18, "fours": 19, "groups": 20, "compare": 21, "rank": 22,
        "reach": 23, "best": 24, "replace": 25, "chosen": 26, "sum": 27, "weights": 28, "parts": 29,
        "turn_weights": UNITS - 1}
C_ID, C_POS, C_QLO, C_KLO, C_TRI, C_SUM, C_END = 0, 128, 640, 641, 642, 706, 722


def begins(b):
    return isinstance(b, int) and b == 0


class Chain:

    def __init__(self, eng, sem):
        self.eng, self.sem, self.base, self.n = eng, sem, 0, 0

    def at(self, base):
        self.base, self.n = base, 0

    def did(self, ins):
        ins.then_inc(self.sem, 1)
        self.n += 1

    def settle(self):
        self.eng.wait_ge(self.sem, self.base + self.n)


def two_layers(nc, x, small, vec, gate_bias, gu, wd, cf32, cbf, cf16, out):
    ctx = ExitStack()
    with ctx:
        def sb(name, shape, dt=F32):
            return ctx.enter_context(nc.sbuf_tensor(name, shape, dt))

        def sem(name):
            return ctx.enter_context(nc.semaphore(name))

        X = sb("X", [P, TILES * D])
        YHI = sb("YHI", [P, B * S], F32R)
        YLO = sb("YLO", [P, B * S], F32R)
        GUH = sb("GUH", [P, UNITS * 256], F32R)
        GUL = sb("GUL", [P, UNITS * 256], F32R)
        WH = sb("WH", [P, SPLIT * 128], F32R)
        WL = sb("WL", [P, SPLIT * 128], F32R)
        VEC = sb("VEC", [P, 5])
        BIAS = sb("BIAS", [P, NE])
        CF = sb("CF", [P, C_END])
        CB = sb("CB", [P, 256], BF16)
        SEL = sb("SEL", [P, PAIRS * 128 + 128], F16)
        CWT = sb("CWT", [P, CHUNK], F16)
        IDR = sb("IDR", [P, P], F32R)
        ONES = sb("ONES", [P, P])
        EPST = sb("EPST", [P, TILES])
        EPS4 = sb("EPS4", [P, 4])
        MV = sb("MV", [P, TILES * 2])
        RS = sb("RS", [P, TILES])
        BN = sb("BN", [P, TILES * 6])
        NMR = sb("NMR", [P, TILES])
        COLS = sb("COLS", [P, 3 * B])
        BUF = sb("BUF", [P, 3072])
        ROT = sb("ROT", [P, 1024])
        VP = sb("VP", [P, 2 * 2 * HEADS * 32])
        US = sb("US", [P, S])
        RD = sb("RD", [P, 2 * 4])
        NOTE = sb("NOTE", [P, 1])
        PRX = sb("PRX", [P, 1024], F32R)
        LN3 = sb("LN3", [P, 40])

        with ExitStack() as early:
            def sb_early(name, shape, dt=F32):
                return early.enter_context(nc.sbuf_tensor(name, shape, dt))

            WD = sb_early("WD", [P, UNITS * 128])
            W = sb_early("W", [P, 15 * 128])
            WQK = [[sb_early(f"W{m}S{part}", [P, HEADS * 32], F32R) for part in "hl"] for m in "qk"]
            MAXIMA = sb_early("MAXIMA", [P, 2 * S], F32R)
            OHS, OH2, OT = sb_early("OHS", [P, 4 * D]), sb_early("OH2", [P, 2 * D]), sb_early("OT", [P, S])
        WDL = sb("WDL", [P, UNITS * 128], F32R)
        WDH = sb("WDH", [P, UNITS * 128], F32R)
        HID = sb("HID", [P, 1024], F32R)

        ident = CF[:, C_ID:C_ID + 128]
        pos = CF[:, C_POS:C_POS + 512]
        ident_bf = CB[:, 0:128]
        causal = CB[:, 128:256]
        ident_h = SEL[:, PAIRS * 128:PAIRS * 128 + 128]

        def w(n):
            return W[:, n * 128:(n + 1) * 128]

        def wh(n):
            return WH[:, n * 128:(n + 1) * 128]

        def wl(n):
            return WL[:, n * 128:(n + 1) * 128]

        PA = ctx.enter_context(nc.psum_tensor("PA", [P, 512], F32))
        PS = ctx.enter_context(nc.psum_tensor("PS", [P, 1536], F32))
        PT = ctx.enter_context(nc.psum_tensor("PT", [P, 1536], F32))
        PB = ctx.enter_context(nc.psum_tensor("PB", [P, 512], F32))

        ld_x = [sem(f"ld_x{q}") for q in range(4)]
        ld_w, ld_vec, ld_bias, ld_cf, ld_cb, ld_sel, ld_wd = (
            sem(n) for n in ("ld_w", "ld_vec", "ld_bias", "ld_cf", "ld_cb", "ld_sel", "ld_wd"))
        ld_gu = [sem(f"ld_gu{p}") for p in range(2)]
        gu_split = sem("gu_split")
        consts = sem("consts")
        ident_r = sem("ident_r")
        small_split = sem("small_split")
        qk_split = sem("qk_split")
        a_stats, a_var, a_rs, a_rstd = (sem(n) for n in ("a_stats", "a_var", "a_rs", "a_rstd"))
        t_stats, t_var, t_rs, t_rstd = (sem(n) for n in ("t_stats", "t_var", "t_rs", "t_rstd"))
        b_stats, b_var, b_rs, b_rstd = (sem(n) for n in ("b_stats", "b_var", "b_rs", "b_rstd"))
        a_rows = sem("a_rows")
        a_mm = sem("a_mm")
        a_cp = sem("a_cp")
        x1_done = sem("x1_done")
        norm, tr, hi, lo = sem("norm"), sem("tr"), sem("hi"), sem("lo")
        gates, acts, cell = sem("gates"), sem("acts"), sem("cell")
        cu_mm = sem("cu_mm")
        cu_cp = sem("cu_cp")
        ro_mm, ro_add, ro_tanh, ro_tr, ro_x = (sem(n) for n in ("ro_mm", "ro_add", "ro_tanh", "ro_tr", "ro_x"))
        t_norm, t_tr, t_hi, t_lo, v_mm, v_cp = (sem(n) for n in ("t_norm", "t_tr", "t_hi", "t_lo", "v_mm", "v_cp"))
        zeroed = sem("zeroed")
        km = [sem(f"km{g}") for g in range(GROUPS)]
        qk_mm, qk_pos, qk_hi, stack, s_mm, s_max, m_tr, q_shift = (
            sem(n) for n in ("qk_mm", "qk_pos", "qk_hi", "stack", "s_mm", "s_max", "m_tr", "q_shift"))
        st_mm, prob, masked, pv_mm, u_cp, u_tr, u_rec, o_norm = (
            sem(n) for n in ("st_mm", "prob", "masked", "pv_mm", "u_cp", "u_tr", "u_rec", "o_norm"))
        o_tr, o_cp, o_mm, x3_done = (sem(n) for n in ("o_tr", "o_cp", "o_mm", "x3_done"))
        c_var, c_rs, c_rstd, c_norm, c_tr, c_hi, c_lo = (
            sem(n) for n in ("c_var", "c_rs", "c_rstd", "c_norm", "c_tr", "c_hi", "c_lo"))
        g_mm, g_exp, g_tr, g_use, g_chain, g_cw, g_cwtr, g_cwt = (
            sem(n) for n in ("g_mm", "g_exp", "g_tr", "g_use", "g_chain", "g_cw", "g_cwtr", "g_cwt"))
        wd_hi, wd_lo = sem("wd_hi"), sem("wd_lo")
        e_gate, e_up, e_cw, e_silu, e_act, e_prod, e_hi, e_lo, e_down = (
            sem(n) for n in ("e_gate", "e_up", "e_cw", "e_silu", "e_act", "e_prod", "e_hi", "e_lo", "e_down"))
        y_cp, y_tr, x4_done, stored = (sem(n) for n in ("y_cp", "y_tr", "x4_done", "stored"))

        KM = [YLO[:, g * 1024:(g + 1) * 1024] for g in range(GROUPS)]
        QKS = [YHI[:, g * 512:(g + 1) * 512] for g in range(GROUPS)]
        QS = [QKS[g][:, 0:256] for g in range(GROUPS)]
        Q2 = [YHI[:, 2048 + p * 256:2304 + p * 256] for p in range(2)]
        HM = [YHI[:, 2560 + p * 512:3072 + p * 512] for p in range(2)]
        TH = YHI[:, 3584:3840]
        TL = YHI[:, 3840:4096]
        MTP = PS[:, 1024:1280]
        M2 = [MAXIMA[:, p * S:(p + 1) * S] for p in range(2)]
        QKF = [ROT[:, p * 512:(p + 1) * 512] for p in range(2)]
        PR = [BUF[:, p * 1536:(p + 1) * 1536] for p in range(2)]
        VPB = [VP[:, p * 1024:(p + 1) * 1024].rearrange("p (t h c) -> p t h c", t=2, c=32) for p in range(2)]
        PBU, PAS = PB[:, 0:256], PA[:, 0:256]
        PAB = [PA, PB]
        OH = [OHS[:, p * 256:(p + 1) * 256] for p in range(2)]
        RSZ = [VP[:, T * 32:(T + 1) * 32] for T in range(TILES)]
        RSM = [VP[:, 32 * t:32 * t + 65 * (B - 1) + 1:65] for t in range(2)]
        CST = [COLS[:, n * B:(n + 1) * B] for n in range(3)]

        def qk_bank(b, gr):
            return PT[:, gr * 512:(gr + 1) * 512] if begins(b) and gr < 3 else PA[:, :]

        def o_bank(b):
            return PS[:, (B - 1 - b) * 512:(B - 1 - b) * 512 + 256] if isinstance(b, int) and b >= B - 2 else PAS

        GATE = [[bank[:, k * 512:(k + 1) * 512] for k in range(3)] for bank in (PS, PT)]
        SG = [VP[:, k * 256:(k + 1) * 256] for k in range(3)]
        C, IG, CU = (VP[:, k * 256:(k + 1) * 256] for k in (3, 4, 5))
        CWS = US[:, :].bitcast(F16)
        PAH = PA[:, 0:256].bitcast(F16)
        SIL = [BUF[:, p * 512:(p + 1) * 512] for p in range(2)]
        PRF = [BUF[:, 1024 + p * 512:1536 + p * 512] for p in range(3)]
        PRH = [WH[:, 0:512], HID[:, 0:512], PRX[:, 0:512]]
        PRL = [WL[:, 0:512], HID[:, 512:1024], PRX[:, 512:1024]]
        YNC, TURN = ROT[:, 0:512], ROT[:, 512:1024]
        EG = [PS[:, 0:512], PS[:, 512:1024]]
        EU = [PS[:, 1024:1536], PT[:, 0:512]]
        EC = [PT[:, 512:1024], PT[:, 1024:1536]]
        BNC, MEAN, VAR, SPREAD, RSC = (LN3[:, a:b] for a, b in ((0, 24), (24, 28), (28, 32), (32, 36), (36, 40)))

        block = ctx.enter_context(nc.Block())

        def ncols(i, n):
            return bass.ds(i * n, n)

        def mean_variance(v, did, settle, bn, mean, var, spread):
            mean_e, m2_e, mean_o, m2_o = (bn[:, col::6] for col in (1, 2, 4, 5))
            did(v.tensor_tensor(spread, mean_e, mean_o, ALU.subtract))
            did(v.tensor_tensor(mean, mean_e, mean_o, ALU.add))
            did(v.tensor_tensor(var, m2_e, m2_o, ALU.add))
            settle()
            did(v.scalar_tensor_tensor(spread, spread, 0.25, spread, ALU.mult, ALU.mult))
            did(v.tensor_scalar(mean, mean, 0.5, None, ALU.mult))
            settle()
            return v.scalar_tensor_tensor(var, var, 1.0 / D, spread, ALU.mult, ALU.add)

        @block.sync
        def _(sp):
            for q in range(4):
                sp.dma_start(X[:, q * QUARTER * D:(q + 1) * QUARTER * D].rearrange("p (b h d) -> p b h d", h=2, d=D),
                             x[4 * q:4 * q + 4].rearrange("b (h p) d -> p b h d", p=P)).then_inc(ld_x[q], 16)
            sp.dma_start(W[:, :], small.rearrange("p k m -> p (k m)")).then_inc(ld_w, 16)
            sp.dma_start(CF[:, :], cf32).then_inc(ld_cf, 16)
            sp.dma_start(VEC[:, :], vec).then_inc(ld_vec, 16)
            sp.dma_start(BIAS[:, :], gate_bias.partition_broadcast(P)).then_inc(ld_bias, 16)
            sp.dma_start(CB[:, :], cbf).then_inc(ld_cb, 16)
            for n in range(UNITS // STAGE_UNITS):
                if n >= 2:
                    sp.wait_ge(gu_split, 2 * (n - 1))
                sp.dma_start(BUF[:, (n % 2) * 1536:(n % 2) * 1536 + STAGE_UNITS * 256],
                             gu[:, n * STAGE_UNITS:(n + 1) * STAGE_UNITS, :].rearrange("p k m -> p (k m)")
                             ).then_inc(ld_gu[n % 2], 16)
            sp.dma_start(SEL[:, :], cf16).then_inc(ld_sel, 16)
            sp.dma_start(WD[:, :], wd.rearrange("p k m -> p (k m)")).then_inc(ld_wd, 16)
            def spread_k(b, gr):
                n = b * GROUPS + gr
                sp.wait_ge(stack, 2 * n + 1)
                for j in range(4):
                    rows = slice(32 * j, 32 * j + 32)
                    sp.dma_start(KM[gr][rows, j * 256:(j + 1) * 256].bitcast(F32),
                                 QKS[gr][rows, 256:512].bitcast(F32)).then_inc(km[gr], 16)

            for gr in range(GROUPS):
                spread_k(0, gr)
            with sp.Fori(1, B) as b:
                for gr in range(GROUPS):
                    spread_k(b, gr)

            with sp.Fori(0, CHUNKS) as c:
                sp.wait_ge(x4_done, c + 2)
                sp.dma_start(out[bass.ds(c * 2, 2), :, :].rearrange("b (h p) d -> p b h d", p=P),
                             X[:, bass.ds(c * CHUNK, CHUNK)].rearrange("p (b h d) -> p b h d", h=2, d=D)
                             ).then_inc(stored, 16)
            sp.wait_ge(stored, 16 * CHUNKS)

        @block.gpsimd
        def _(pool):
            g = nc.gpsimd
            g.memset(EPST[:, :], -0.5).then_inc(consts, 1)
            g.memset(ONES[:, :], 1.0).then_inc(consts, 1)
            g.memset(EPS4[:, :], EPS).then_inc(consts, 1)
            g.memset(VP[:, 0:32 * TILES], 0.0).then_inc(consts, 1)
            for m in range(2):
                for part in range(2):
                    g.memset(WQK[m][part][:, :].bitcast(F32), 0.0).then_inc(consts, 1)
            def rstd_quarter(q):
                cols = slice(q * QUARTER, (q + 1) * QUARTER)
                pool.wait_ge(a_var, q + 1)
                g.tensor_scalar(RS[:, cols], MV[:, TILES:][:, cols], EPS, None, ALU.add).then_inc(a_rs, 1)
                pool.wait_ge(a_rs, q + 1)
                for t in range(2):
                    g.tensor_tensor(RSM[t][:, 4 * q:4 * q + 4], RS[:, cols][:, t::2], EPST[:, 0:4], ALU.pow
                                    ).then_inc(a_rstd, 1)

            def rstd_scan(c):
                pool.wait_ge(b_var, c + 1)
                g.tensor_tensor(RSC, VAR, EPS4[:, :], ALU.add).then_inc(b_rs, 1)
                pool.wait_ge(b_rs, c + 1)
                g.tensor_tensor(RSC, RSC, EPST[:, 0:4], ALU.pow).then_inc(b_rstd, 1)

            def split_experts(n):
                cols = slice(n * STAGE_UNITS * 256, (n + 1) * STAGE_UNITS * 256)
                raw = BUF[:, (n % 2) * 1536:(n % 2) * 1536 + STAGE_UNITS * 256]
                pool.wait_ge(ld_gu[n % 2], 16 * (n // 2 + 1))
                g.tensor_copy(GUH[:, cols], raw).then_inc(gu_split, 1)
                pool.wait_ge(gu_split, 2 * n + 1)
                g.tensor_tensor(GUL[:, cols], raw, GUH[:, cols], ALU.subtract).then_inc(gu_split, 1)

            pool.wait_ge(consts, 8)
            for q in range(4):
                rstd_quarter(q)
            pool.wait_ge(ld_w, 16)
            g.tensor_copy(WH[:, :], W[:, 0:SPLIT * 128]).then_inc(small_split, 1)
            pool.wait_ge(small_split, 1)
            g.tensor_tensor(WL[:, :], W[:, 0:SPLIT * 128], WH[:, :], ALU.subtract).then_inc(small_split, 1)
            rstd_scan(0)
            rstd_scan(1)
            for m, src in enumerate((WQ, WK)):
                raw = w(src).rearrange("p (h d) -> p h d", d=HD)
                wide = [WQK[m][part][:, :].rearrange("p (h s d) -> p h s d", s=4, d=HD) for part in range(2)]
                for s in (1, 2, 3):
                    g.tensor_copy(wide[0][:, :, s, :], raw).then_inc(qk_split, 1)
                pool.wait_ge(qk_split, 6 * m + 3)
                for s in (1, 2, 3):
                    g.tensor_tensor(wide[1][:, :, s, :], raw, wide[0][:, :, s, :], ALU.subtract).then_inc(qk_split, 1)
            for n in range(UNITS // STAGE_UNITS):
                if 2 + n < CHUNKS:
                    rstd_scan(2 + n)
                split_experts(n)

            pool.wait_ge(ro_mm, CHUNKS)
            for gr in range(GROUPS):
                g.memset(KM[gr].bitcast(F32), 0.0).then_inc(zeroed, 1)
            g.memset(MAXIMA[:, :].bitcast(F32), 0.0).then_inc(zeroed, 1)
            pool.wait_ge(ro_add, CHUNKS)
            g.memset(VP[:, :], 0.0).then_inc(zeroed, 1)
            pool.wait_ge(zeroed, 6)
            for p in range(2):
                g.memset(VPB[p][:, :, :, HD:HD + 1], 1.0).then_inc(zeroed, 1)
            pool.wait_ge(t_var, 1)
            g.tensor_scalar(RS[:, :], MV[:, TILES:], EPS, None, ALU.add).then_inc(t_rs, 1)
            pool.wait_ge(t_rs, 1)
            for cols in (slice(0, 4), slice(4, TILES)):
                g.tensor_tensor(RS[:, cols], RS[:, cols], EPST[:, cols], ALU.pow).then_inc(t_rstd, 1)

            def q_k_stack(b, gr):
                n = b * GROUPS + gr
                pool.wait_ge(qk_hi, 2 * n + 1)
                if not begins(b):
                    pool.wait_ge(km[gr], 64 * b)
                g.tensor_tensor(QKS[gr][:, 256:512], QKF[gr % 2][:, 256:512], HM[gr % 2][:, 256:512], ALU.subtract
                                ).then_inc(stack, 1)
                pool.wait_ge(qk_hi, 2 * n + 2)
                if not begins(b):
                    pool.wait_ge(q_shift, n - GROUPS + 1)
                g.tensor_tensor(QKS[gr][:, 0:256], QKF[gr % 2][:, 0:256], HM[gr % 2][:, 0:256], ALU.subtract
                                ).then_inc(stack, 1)

            def causal_select(b, gr):
                n = b * GROUPS + gr
                pool.wait_ge(prob, n + 1)
                first = PR[gr % 2][:, 0:1024].rearrange("p (j q) -> p j q", q=256)[:, :, 0:128]
                second = PR[gr % 2][:, 1024:1536].rearrange("p (j q) -> p j q", q=128)
                pool.wait_ge(masked, 2 * n)
                g.tensor_tensor(NOTE[:, :], ONES[:, 0:1], ONES[:, 0:1], ALU.mult)
                for part in (first, second):
                    g.affine_select(out=part, in_=part, compare_op=ALU.is_ge, fill=0.0, base=0,
                                    pattern=[[0, 4], [1, 128]], channel_multiplier=-1).then_inc(masked, 1)

            def rstd_chunk(c):
                pool.wait_ge(c_var, c + 1)
                g.tensor_tensor(RSC, VAR, EPS4[:, :], ALU.add).then_inc(c_rs, 1)
                pool.wait_ge(c_rs, c + 1)
                g.tensor_tensor(RSC, RSC, EPST[:, 0:4], ALU.pow).then_inc(c_rstd, 1)

            def sequence(b, last):
                for gr in range(GROUPS):
                    if gr == 0:
                        q_k_stack(b, 3)
                    elif not last:
                        q_k_stack(b + 1, gr - 1)
                    causal_select(b, gr)
                    if last and gr == 0:
                        rstd_chunk(0)

            for gr in range(3):
                q_k_stack(0, gr)
            sequence(0, False)
            with pool.Fori(0, 7) as k:
                sequence(2 * k + 1, False)
                sequence(2 * k + 2, False)
            sequence(15, True)

            def low_hidden(c, u):
                n = c * UNITS + u
                pool.wait_ge(e_hi, n + 1)
                g.tensor_tensor(PRL[u % 3], PRF[u % 3], PRH[u % 3], ALU.subtract).then_inc(e_lo, 1)

            for k in range(UNITS // STAGE_UNITS):
                cols = slice(k * STAGE_UNITS * 128, (k + 1) * STAGE_UNITS * 128)
                pool.wait_ge(wd_hi, k + 1)
                g.tensor_tensor(WDL[:, cols], WD[:, cols], WDH[:, cols], ALU.subtract).then_inc(wd_lo, 1)
            for u in range(4):
                low_hidden(0, u)
            with pool.Fori(0, CHUNKS - 1) as c:
                for u in range(4, UNITS):
                    low_hidden(c, u)
                    if u == PREP["rstd"]:
                        rstd_chunk(c + 1)
                for u in range(4):
                    low_hidden(c + 1, u)
            for u in range(4, UNITS):
                low_hidden(CHUNKS - 1, u)

        @block.scalar
        def _(act):
            s = nc.scalar
            act.wait_ge(ld_cf, 16)
            s.activation(IDR[:, :], ident, ACT.Copy, scale=-1.0).then_inc(ident_r, 1)
            act.sem_inc(y_cp, 1)
            act.wait_ge(a_mm, 1)
            s.activation(US[:, 0:128], PA[:, 0:128], ACT.Copy).then_inc(a_cp, 1)
            act.wait_ge(a_mm, 2)
            s.activation(CST[1], PB[:, 0:B], ACT.Copy).then_inc(a_cp, 1)
            act.wait_ge(a_mm, 3)
            s.activation(CST[2], PA[:, 0:B], ACT.Copy).then_inc(a_cp, 1)

            def high_scan(c):
                act.wait_ge(tr, c + 1)
                s.activation(YHI[:, ncols(c, CHUNK)], PA[:, :], ACT.Copy).then_inc(hi, 1)

            def scan_step(t, par, half):
                for k, f, bias in ((2, ACT.Tanh, 2), (1, ACT.Sigmoid, 1), (0, ACT.Sigmoid, 0)):
                    act.wait_ge(gates, 3 * t + 3 - k)
                    s.activation(SG[k], GATE[par][k][:, half * 256:(half + 1) * 256], f,
                                 bias=VEC[:, bias:bias + 1]).then_inc(acts, 1)

            def scan_pair(p, par, turned=True):
                scan_step(2 * p, par, 0)
                if turned:
                    high_scan(p + 1)
                scan_step(2 * p + 1, par, 1)

            high_scan(0)
            act.wait_ge(ld_vec, 16)
            with act.Fori(0, CHUNKS // 2 - 1) as k:
                scan_pair(2 * k, 0)
                scan_pair(2 * k + 1, 1)
            scan_pair(CHUNKS - 2, 0)
            scan_pair(CHUNKS - 1, 1, turned=False)
            act.wait_ge(cu_mm, 1)
            s.activation(CU, PB[:, 0:256], ACT.Copy).then_inc(cu_cp, 1)
            with act.Fori(0, CHUNKS // 2) as k:
                for p in range(2):
                    act.wait_ge(ro_add, 2 * k + p + 1)
                    h = ROT[:, p * 512:(p + 1) * 512]
                    s.activation(h, h, ACT.Tanh, bias=VEC[:, 3:4]).then_inc(ro_tanh, 1)

            def split_sequence(b):
                act.wait_ge(t_tr, b + 1)
                if not begins(b):
                    act.wait_ge(qk_mm, GROUPS * b)
                s.activation(TH, PAS, ACT.Copy).then_inc(t_hi, 1)

            def values(b, par):
                act.wait_ge(v_mm, b + 1)
                s.activation(VPB[par][:, :, :, 0:HD],
                             PAS.rearrange("p (t h d) -> p t h d", t=2, d=HD), ACT.Copy).then_inc(v_cp, 1)

            def hi_slots(b, gr):
                n = b * GROUPS + gr
                act.wait_ge(qk_pos, n + 1)
                s.activation(HM[gr % 2][:, 256:512], QKF[gr % 2][:, 256:512], ACT.Copy,
                             scale=CF[:, C_KLO:C_KLO + 1]).then_inc(qk_hi, 1)
                s.activation(HM[gr % 2][:, 0:256], QKF[gr % 2][:, 0:256], ACT.Copy,
                             scale=CF[:, C_QLO:C_QLO + 1]).then_inc(qk_hi, 1)

            def u_copy(b, gr):
                n = b * GROUPS + gr
                act.wait_ge(pv_mm, n + 1)
                s.activation(US[:, :], PBU, ACT.Copy).then_inc(u_cp, 1)

            def o_copy(b):
                act.wait_ge(o_tr, b + 1)
                s.activation(OT[:, :], o_bank(b), ACT.Copy).then_inc(o_cp, 1)

            def exps(b, gr):
                n = b * GROUPS + gr
                act.wait_ge(st_mm, n + 1)
                if not begins(b) or gr >= 2:
                    act.wait_ge(pv_mm, n - 1)
                s.activation(PR[gr % 2], PT[:, :], ACT.Exp, scale=SCALE).then_inc(prob, 1)

            def sequence(b, par, first, last):
                for gr in range(GROUPS):
                    if gr >= 2:
                        u_copy(b, gr - 2)
                    elif not first:
                        u_copy(b - 1, gr + 2)
                    if gr == 0:
                        hi_slots(b, 3)
                    elif not last:
                        hi_slots(b + 1, gr - 1)
                    if gr == 0 and not last:
                        split_sequence(b + 1)
                    if gr == 1 and not last:
                        values(b + 1, 1 - par)
                    if gr == 2 and not first and not last:
                        o_copy(b - 1)
                    if last and gr == 2:
                        high_chunk(0)
                    if last and gr == 3:
                        exp_logits(0)
                    exps(b, gr)

            def high_chunk(c):
                act.wait_ge(c_tr, c + 1)
                s.activation(YHI[:, ncols(c, CHUNK)], PA[:, :], ACT.Copy).then_inc(c_hi, 1)

            def exp_logits(c):
                act.wait_ge(g_mm, c + 1)
                if begins(c):
                    act.wait_ge(stack, 2 * 64)
                s.activation(TURN, PA[:, :], ACT.Exp, scale=-1.0).then_inc(g_exp, 1)

            act.wait_ge(zeroed, 8)
            split_sequence(0)
            hi_slots(0, 0)
            values(0, 0)
            hi_slots(0, 1)
            hi_slots(0, 2)
            sequence(0, 0, True, False)
            with act.Fori(0, 7) as k:
                sequence(2 * k + 1, 1, False, False)
                sequence(2 * k + 2, 0, False, False)
            sequence(15, 1, False, True)
            u_copy(15, 2)
            o_copy(14)
            u_copy(15, 3)
            o_copy(15)

            def routing(c):
                act.wait_ge(g_cwtr, c + 1)
                if not begins(c):
                    act.wait_ge(e_cw, PAIRS * c)
                s.activation(CWT[:, :], PAH[:, 0:CHUNK], ACT.Copy).then_inc(g_cwt, 1)

            def silu(c, u):
                n = c * UNITS + u
                act.wait_ge(e_gate, n + 1)
                if not (begins(c) and u < 2):
                    act.wait_ge(e_prod, n if u == 0 else n - 1)
                s.activation(SIL[u % 2], EG[u % 2], ACT.Silu).then_inc(e_silu, 1)

            def high_hidden(c, u):
                n = c * UNITS + u
                act.wait_ge(e_prod, n + 1)
                if not (begins(c) and u < 3):
                    act.wait_ge(e_down, n - 2)
                s.activation(PRH[u % 3], PRF[u % 3], ACT.Copy).then_inc(e_hi, 1)

            def copy_sum(c):
                act.wait_ge(e_down, (c + 1) * UNITS)
                s.activation(TURN, PB[:, :], ACT.Copy).then_inc(y_cp, 1)

            def body(c, last):
                for u in range(4, UNITS):
                    silu(c, u)
                    high_hidden(c, u - 1)
                    if not last:
                        if u == PREP["turn"]:
                            high_chunk(c + 1)
                        if u == PREP["exp"]:
                            exp_logits(c + 1)
                        if u == PREP["turn_weights"]:
                            routing(c + 1)

            act.wait_ge(ld_wd, 16)
            act.wait_ge(x3_done, B + 1)
            for k in range(UNITS // STAGE_UNITS):
                cols = slice(k * STAGE_UNITS * 128, (k + 1) * STAGE_UNITS * 128)
                s.activation(WDH[:, cols], WD[:, cols], ACT.Copy).then_inc(wd_hi, 1)
            silu(0, 0)
            silu(0, 1)
            routing(0)
            high_hidden(0, 0)
            for u in range(2, 4):
                silu(0, u)
                high_hidden(0, u - 1)
            with act.Fori(0, CHUNKS - 1) as c:
                body(c, False)
                silu(c + 1, 0)
                high_hidden(c, UNITS - 1)
                for u in range(1, 4):
                    if u == 3:
                        copy_sum(c)
                    silu(c + 1, u)
                    high_hidden(c + 1, u - 1)
            body(CHUNKS - 1, True)
            high_hidden(CHUNKS - 1, UNITS - 1)
            copy_sum(CHUNKS - 1)

        @block.tensor
        def _(pe):
            mm = nc.tensor.matmul

            def three(out_, wn_h, wn_l, y_h, y_l, start, stop=False, skip=True):
                mm(out_, wn_h, y_h, start=start, stop=False, skip_group_check=skip)
                mm(out_, wn_h, y_l, start=False, stop=False, skip_group_check=skip)
                return mm(out_, wn_l, y_h, start=False, stop=stop, skip_group_check=skip)

            pe.wait_ge(consts, 8)
            pe.sem_inc(ro_tr, 1)
            for T in range(TILES):
                if T % QUARTER == 0:
                    pe.wait_ge(a_rstd, 2 * (T // QUARTER) + 2)
                j = T % 4
                ins = mm(PA[32 * j:32 * j + 32, 0:128], RSZ[T], X[:, T * D:(T + 1) * D], start=(T < 4),
                         stop=(T >= TILES - 4), tile_position=(0, 32 * j), skip_group_check=True)
            ins.then_inc(a_mm, 1)
            pe.wait_ge(ld_cf, 16)
            pe.wait_ge(a_rows, 3)
            mm(PB[:, 0:B], ONES[:, :], CST[0], start=True, stop=False)
            pe.wait_ge(a_cp, 1)
            mm(PB[:, 0:B], US[:, 0:128], CF[:, C_SUM:C_SUM + B], start=False, stop=True).then_inc(a_mm, 1)
            pe.wait_ge(ld_w, 16)
            pe.wait_ge(a_cp, 2)
            mm(PA[:, 0:B], w(WV0), CST[1], start=True, stop=True).then_inc(a_mm, 1)
            pe.wait_ge(a_cp, 3)
            for b in range(B):
                bank = PS[:, b // 4 * 512:b // 4 * 512 + 512] if b < 12 else PT[:, 0:512]
                ins = mm(bank[:, b % 4 * 128:b % 4 * 128 + 128], CST[2][:, b:b + 1].broadcast_to([P, P]), w(WO0),
                         start=True, stop=True)
                if b % 4 == 3:
                    ins.then_inc(a_mm, 1)

            def turn_scan(c):
                pe.wait_ge(norm, 4 * c + 4)
                if not begins(c):
                    pe.wait_ge(lo, c)
                for t in range(4):
                    cols = slice(t * 128, (t + 1) * 128)
                    ins = nc.tensor.transpose(PA[:, cols], YNC[:, cols], ident)
                ins.then_inc(tr, 1)

            def inputs_part(p, par):
                pe.wait_ge(lo, p + 1)
                cols = ncols(p, CHUNK)
                for k, n in ((2, WC), (1, WI), (0, WF)):
                    three(GATE[par][k], wh(n), wl(n), YHI[:, cols], YLO[:, cols], start=True)

            def cell_part(t, par, half):
                pe.wait_ge(cell, 3 * t + 1)
                for k, n in ((2, UC), (1, UI), (0, UF)):
                    mm(GATE[par][k][:, half * 256:(half + 1) * 256], w(n), C, start=False, stop=True,
                       skip_group_check=True).then_inc(gates, 1)

            def scan_pair(p, par, more=True):
                cell_part(2 * p, par, 0)
                if more:
                    turn_scan(p + 1)
                cell_part(2 * p + 1, par, 1)
                if more:
                    inputs_part(p + 1, 1 - par)

            turn_scan(0)
            pe.wait_ge(small_split, 2)
            pe.wait_ge(x1_done, 3)
            inputs_part(0, 0)
            pe.wait_ge(x1_done, 4)
            with pe.Fori(0, CHUNKS // 2 - 1) as k:
                scan_pair(2 * k, 0)
                scan_pair(2 * k + 1, 1)
            scan_pair(CHUNKS - 2, 0)
            scan_pair(CHUNKS - 1, 1, more=False)

            pe.wait_ge(cell, 3 * B + 1)
            mm(PB[:, 0:256], w(UO), C, start=True, stop=True).then_inc(cu_mm, 1)

            def read_out(i, p):
                if isinstance(i, int) and i < 2:
                    pe.wait_ge(cu_cp, 1)
                else:
                    pe.wait_ge(ro_add, i - 1)
                cols = ncols(i, CHUNK)
                three(PAB[p][:, :], wh(WO), wl(WO), YHI[:, cols], YLO[:, cols], start=True, stop=True).then_inc(ro_mm, 1)

            def turn_out(i, p):
                pe.wait_ge(ro_tanh, i + 1)
                if not (isinstance(i, int) and i < 2):
                    pe.wait_ge(ro_x, i - 1)
                for t in range(4):
                    ins = nc.tensor.transpose(PS[:, p * 512 + t * 128:p * 512 + (t + 1) * 128],
                                              ROT[:, p * 512 + t * 128:p * 512 + (t + 1) * 128], ident)
                ins.then_inc(ro_tr, 1)

            read_out(0, 0)
            read_out(1, 1)
            turn_out(0, 0)
            read_out(2, 0)
            turn_out(1, 1)
            with pe.Fori(1, CHUNKS // 2 - 1) as k:
                read_out(2 * k + 1, 1)
                turn_out(2 * k, 0)
                read_out(2 * k + 2, 0)
                turn_out(2 * k + 1, 1)
            read_out(CHUNKS - 1, 1)
            turn_out(CHUNKS - 2, 0)
            turn_out(CHUNKS - 1, 1)

            def transpose_sequence(b):
                pe.wait_ge(t_norm, 2 * b + 2)
                if not begins(b):
                    pe.wait_ge(qk_pos, GROUPS * b)
                for t in range(2):
                    ins = nc.tensor.transpose(PAS[:, t * 128:(t + 1) * 128], OH2[:, t * 128:(t + 1) * 128], ident)
                ins.then_inc(t_tr, 1)

            def values(b):
                if begins(b):
                    pe.wait_ge(t_hi, 1)
                    pe.wait_ge(t_lo, 1)
                else:
                    pe.wait_ge(qk_pos, GROUPS * b + 1)
                for t in range(2):
                    rows = slice(t * 128, (t + 1) * 128)
                    dst = PAS[:, rows]
                    mm(dst, TH[:, rows], wh(WV1), start=True, stop=False, skip_group_check=True)
                    mm(dst, TH[:, rows], wl(WV1), start=False, stop=False, skip_group_check=True)
                    ins = mm(dst, TL[:, rows], wh(WV1), start=False, stop=True, skip_group_check=True)
                ins.then_inc(v_mm, 1)

            def q_k(b, gr):
                n = b * GROUPS + gr
                if begins(b):
                    if gr == 0:
                        pe.wait_ge(t_hi, 1)
                        pe.wait_ge(t_lo, 1)
                    if gr == 3:
                        pe.wait_ge(v_cp, 1)
                else:
                    if gr == 0:
                        pe.wait_ge(t_hi, b + 1)
                        pe.wait_ge(t_lo, b + 1)
                    elif gr == 1:
                        pe.wait_ge(v_cp, b + 1)
                    elif gr == 2 and not (isinstance(b, int) and b == 1):
                        pe.wait_ge(o_cp, b - 1)
                    elif gr == 3:
                        pe.wait_ge(x3_done, b)
                    pe.wait_ge(qk_pos, n)
                cols = slice(gr * 128, (gr + 1) * 128)
                for m in range(2):
                    ins = three(qk_bank(b, gr)[:, m * 256:(m + 1) * 256], WQK[m][0][:, cols], WQK[m][1][:, cols], TH, TL,
                                start=True, stop=True, skip=False)
                ins.then_inc(qk_mm, 1)

            def scores_first(b, gr):
                n = b * GROUPS + gr
                pe.wait_ge(stack, 2 * n + 2)
                pe.wait_ge(km[gr], 64 * (b + 1))
                if not begins(b) or gr > 0:
                    pe.wait_ge(s_max, 3 * n - 2)
                keys = KM[gr].rearrange("p (j k) -> p j k", k=256)
                dst = PS[:, 0:512].rearrange("p (j k) -> p j k", k=128)
                mm(dst, QS[gr][:, 0:128], keys[:, :, 0:128], start=True, stop=True, skip_group_check=True)
                mm(dst, ident_bf, causal.unsqueeze(1).broadcast_to([P, 4, 128]), start=False, stop=True,
                   skip_group_check=True).then_inc(s_mm, 1)

            def scores_second(b, gr, j):
                n = b * GROUPS + gr
                if not begins(b) or gr > 0:
                    if j == 0:
                        pe.wait_ge(s_max, 3 * n - 1)
                    else:
                        pe.wait_ge(q_shift, n)
                dst = PS[:, 512 + j * 256:1024 + j * 256]
                mm(dst, QS[gr][:, 128:256], KM[gr][:, j * 256:(j + 2) * 256], start=True, stop=True,
                   skip_group_check=True)
                mm(dst.rearrange("p (j k) -> p j k", k=256)[:, :, 128:256], ident_bf,
                   causal.unsqueeze(1).broadcast_to([P, 2, 128]), start=False, stop=True,
                   skip_group_check=True).then_inc(s_mm, 1)

            def shift_rows(b, gr):
                n = b * GROUPS + gr
                pe.wait_ge(s_max, 3 * n + 3)
                for t in range(2):
                    cols = slice(t * 128, (t + 1) * 128)
                    ins = mm(MTP[:, cols], M2[gr % 2][:, cols], IDR[:, :], start=True, stop=True)
                ins.then_inc(m_tr, 1)

            def scores_t(b, gr):
                n = b * GROUPS + gr
                pe.wait_ge(q_shift, n + 1)
                if not begins(b) or gr > 0:
                    pe.wait_ge(prob, n)
                q = Q2[gr % 2]
                for j in range(4):
                    mm(PT[:, j * 256:(j + 1) * 256], KM[gr][:, j * 256:j * 256 + 128], q, start=True, stop=True)
                for j in range(4):
                    ins = mm(PT[:, 1024 + j * 128:1152 + j * 128], KM[gr][:, j * 256 + 128:j * 256 + 256],
                             q[:, 128:256], start=True, stop=True)
                ins.then_inc(st_mm, 1)

            def probs_values(b, gr, par):
                n = b * GROUPS + gr
                if not begins(b) or gr > 0:
                    pe.wait_ge(o_norm, n)
                pe.wait_ge(masked, 2 * n + 2)
                for j in range(4):
                    h = GROUPS * gr + j
                    dst = PB[32 * j:32 * j + 32, 0:256]
                    mm(dst, VPB[par][:, 0, h, :], PR[gr % 2][:, j * 256:(j + 1) * 256], start=True, stop=True,
                       tile_position=(0, 32 * j), skip_group_check=True)
                for j in range(4):
                    h = GROUPS * gr + j
                    ins = mm(PB[32 * j:32 * j + 32, 128:256], VPB[par][:, 1, h, :],
                             PR[gr % 2][:, 1024 + j * 128:1152 + j * 128], start=False, stop=True,
                             tile_position=(0, 32 * j), skip_group_check=True)
                ins.then_inc(pv_mm, 1)

            def transpose_u(b, gr):
                n = b * GROUPS + gr
                pe.wait_ge(u_cp, n + 1)
                for t in range(2):
                    cols = slice(t * 128, (t + 1) * 128)
                    ins = nc.tensor.transpose(PBU[:, cols], US[:, cols], ident)
                ins.then_inc(u_tr, 1)

            def transpose_o(b, par):
                pe.wait_ge(o_norm, GROUPS * b + 4)
                for t in range(2):
                    cols = slice(t * 128, (t + 1) * 128)
                    ins = nc.tensor.transpose(o_bank(b)[:, cols], OH[par][:, cols], ident)
                ins.then_inc(o_tr, 1)

            def project_o(b):
                pe.wait_ge(o_cp, b + 1)
                for t in range(2):
                    cols = slice(t * 128, (t + 1) * 128)
                    ins = mm(o_bank(b)[:, cols], OT[:, cols], w(WO1), start=True, stop=True, skip_group_check=True)
                ins.then_inc(o_mm, 1)

            def turn_chunk(c):
                pe.wait_ge(c_norm, 4 * c + 4)
                if begins(c):
                    pe.wait_ge(qk_pos, GROUPS * B)
                else:
                    pe.wait_ge(x4_done, c)
                for t in range(4):
                    cols = slice(t * 128, (t + 1) * 128)
                    ins = nc.tensor.transpose(PA[:, cols], YNC[:, cols], ident)
                ins.then_inc(c_tr, 1)

            def gate_logits(c):
                pe.wait_ge(c_lo, c + 1)
                cols = ncols(c, CHUNK)
                three(PA[:, :], wh(GW), wl(GW), YHI[:, cols], YLO[:, cols], start=True, stop=True).then_inc(g_mm, 1)

            def turn_exp(c):
                pe.wait_ge(g_exp, c + 1)
                for t in range(4):
                    cols = slice(t * 128, (t + 1) * 128)
                    ins = nc.tensor.transpose(PA[:, cols], TURN[:, cols], ident)
                ins.then_inc(g_tr, 1)

            def sequence(b, par, first, last):
                for gr in range(GROUPS):
                    ahead = (b, gr + 1) if gr < 3 else (b + 1, 0)
                    if gr < 3 or not last:
                        scores_first(*ahead)
                        scores_second(*ahead, 0)
                    shift_rows(b, gr)
                    if gr == 0:
                        q_k(b, 3)
                    elif not last:
                        q_k(b + 1, gr - 1)
                    older = (b, gr - 2, par) if gr >= 2 else (b - 1, gr + 2, 1 - par)
                    if gr >= 2 or not first:
                        if gr == 2:
                            pe.wait_ge(v_cp, b + 1)
                        probs_values(*older)
                    if last and gr == 2:
                        turn_chunk(0)
                    if last and gr == 3:
                        gate_logits(0)
                    if gr < 3 or not last:
                        scores_second(*ahead, 2)
                    if gr == 0 and not last:
                        transpose_sequence(b + 1)
                    if gr == 1 and not last:
                        values(b + 1)
                    if gr >= 2 and not first and not last:
                        pe.wait_ge(qk_pos, GROUPS * (b + 1) + gr)
                        if gr == 2:
                            transpose_o(b - 1, 1 - par)
                        else:
                            project_o(b - 1)
                    scores_t(b, gr)
                    if gr >= 2 or not first:
                        transpose_u(older[0], older[1])
                    if last and gr == 3:
                        turn_exp(0)

            pe.wait_ge(ld_cb, 16)
            pe.wait_ge(ident_r, 1)
            pe.wait_ge(zeroed, 8)
            pe.wait_ge(qk_split, 12)
            transpose_sequence(0)
            q_k(0, 0)
            values(0)
            q_k(0, 1)
            q_k(0, 2)
            scores_first(0, 0)
            scores_second(0, 0, 0)
            scores_second(0, 0, 2)
            sequence(0, 0, True, False)
            with pe.Fori(0, 7) as k:
                sequence(2 * k + 1, 1, False, False)
                sequence(2 * k + 2, 0, False, False)
            sequence(15, 1, False, True)
            probs_values(15, 2, 1)
            transpose_u(15, 2)
            pe.wait_ge(s_max, 3 * 64)
            transpose_o(14, 0)
            probs_values(15, 3, 1)
            transpose_u(15, 3)
            project_o(14)
            transpose_o(15, 1)
            project_o(15)

            def turn_weights(c):
                pe.wait_ge(g_cw, c + 1)
                for t in range(4):
                    cols = slice(t * 128, (t + 1) * 128)
                    ins = nc.tensor.transpose(PAH[:, cols], CWS[:, cols], ident_h)
                ins.then_inc(g_cwtr, 1)

            def gate_up(c, u):
                n = c * UNITS + u
                at = u * 256
                cols = ncols(c, CHUNK)
                if not (begins(c) and u < 2):
                    pe.wait_ge(e_silu, n if u == 0 else n - 1)
                three(EG[u % 2], GUH[:, at:at + 128], GUL[:, at:at + 128], YHI[:, cols], YLO[:, cols],
                      start=True, stop=True).then_inc(e_gate, 1)
                if u >= 2:
                    pe.wait_ge(e_act, c * PAIRS + u - 1)
                elif u == 0 and not begins(c):
                    pe.wait_ge(e_prod, n)
                three(EU[u % 2], GUH[:, at + 128:at + 256], GUL[:, at + 128:at + 256], YHI[:, cols], YLO[:, cols],
                      start=True, stop=True).then_inc(e_up, 1)

            def routed(c, u):
                n = c * UNITS + u
                if u < PAIRS:
                    if u == 0:
                        pe.wait_ge(g_cwt, c + 1)
                    elif u >= 2:
                        pe.wait_ge(e_prod, n - 1)
                    mm(EC[u % 2], SEL[:, u * 128:(u + 1) * 128], CWT[:, :],
                       start=True, stop=True).then_inc(e_cw, 1)

            def hidden(c, u):
                gate_up(c, u)
                routed(c, u)

            def down(c, u):
                n = c * UNITS + u
                cols = slice(u * 128, (u + 1) * 128)
                if u == 0 and not begins(c):
                    pe.wait_ge(y_cp, c + 1)
                pe.wait_ge(e_hi, n + 1)
                mm(PB[:, :], WDH[:, cols], PRH[u % 3], start=(u == 0), stop=False)
                mm(PB[:, :], WDL[:, cols], PRH[u % 3], start=False, stop=False)
                pe.wait_ge(e_lo, n + 1)
                mm(PB[:, :], WDH[:, cols], PRL[u % 3], start=False, stop=(u == UNITS - 1)).then_inc(e_down, 1)

            def turn_sum(c, last):
                pe.wait_ge(y_cp, c + 2)
                pe.wait_ge(g_cwt, CHUNKS if last else c + 2)
                for t in range(4):
                    cols = slice(t * 128, (t + 1) * 128)
                    ins = nc.tensor.transpose(PA[:, cols], TURN[:, cols], ident)
                ins.then_inc(y_tr, 1)

            def body(c, last):
                down(c, 0)
                for u in range(4, UNITS):
                    hidden(c, u)
                    if not last:
                        if u == PREP["turn"]:
                            turn_chunk(c + 1)
                        if u == PREP["logits"]:
                            gate_logits(c + 1)
                        if u == PREP["turn_exp"]:
                            turn_exp(c + 1)
                        if u == PREP["turn_weights"]:
                            turn_weights(c + 1)
                    down(c, u - 3)

            pe.wait_ge(ld_sel, 16)
            pe.wait_ge(gu_split, 2 * (UNITS // STAGE_UNITS))
            pe.wait_ge(x3_done, B + 1)
            gate_up(0, 0)
            gate_up(0, 1)
            turn_weights(0)
            routed(0, 0)
            routed(0, 1)
            hidden(0, 2)
            hidden(0, 3)
            pe.wait_ge(wd_lo, UNITS // STAGE_UNITS)
            with pe.Fori(0, CHUNKS - 1) as c:
                body(c, False)
                for u in range(3):
                    hidden(c + 1, u)
                    down(c, UNITS - 3 + u)
                hidden(c + 1, 3)
                turn_sum(c, False)
            body(CHUNKS - 1, True)
            for u in range(3):
                down(CHUNKS - 1, UNITS - 3 + u)
            turn_sum(CHUNKS - 1, True)

        @block.vector
        def _(dve):
            v = nc.vector

            dve.sem_inc(x3_done, 1)
            dve.sem_inc(x4_done, 1)
            ch = Chain(dve, a_stats)
            for q in range(4):
                dve.wait_ge(ld_x[q], 16)
                for T in range(q * QUARTER, (q + 1) * QUARTER):
                    ch.did(v.bn_stats(BN[:, T * 6:(T + 1) * 6], X[:, T * D:(T + 1) * D]))
                ch.settle()
                cols = slice(q * QUARTER, (q + 1) * QUARTER)
                mean_variance(v, ch.did, ch.settle, BN[:, q * QUARTER * 6:(q + 1) * QUARTER * 6], MV[:, cols],
                              MV[:, TILES:][:, cols], NMR[:, cols]).then_inc(a_var, 1)
            dve.wait_ge(a_rstd, 8)
            for t in range(2):
                v.scalar_tensor_tensor(NMR[:, t * B:(t + 1) * B], MV[:, t:TILES:2], -1.0, RSM[t], ALU.mult, ALU.mult
                                       ).then_inc(a_rows, 1)
            dve.wait_ge(a_rows, 2)
            v.tensor_tensor(CST[0], NMR[:, 0:B], NMR[:, B:2 * B], ALU.add).then_inc(a_rows, 1)

            def add_values(q):
                bank = PS[:, q * 512:(q + 1) * 512] if q < 3 else PT[:, 0:512]
                dve.wait_ge(a_mm, 4 + q)
                xs = X[:, q * 1024:(q + 1) * 1024].rearrange("p (b h d) -> p b h d", h=2, d=D)
                v.tensor_tensor(xs, xs, bank.rearrange("p (b d) -> p b d", d=D).unsqueeze(2).broadcast_to([P, 4, 2, D]),
                                ALU.add).then_inc(x1_done, 1)

            chs = Chain(dve, b_stats)
            PER_SCAN = 4 + 5

            def scan_stats(c):
                chs.at(PER_SCAN * c)
                for t in range(4):
                    chs.did(v.bn_stats(BNC[:, t * 6:(t + 1) * 6], X[:, bass.ds((4 * c + t) * D, D)]))
                chs.settle()
                mean_variance(v, chs.did, chs.settle, BNC, MEAN, VAR, SPREAD).then_inc(b_var, 1)
                assert chs.n == PER_SCAN, chs.n

            def scan_norm(c):
                dve.wait_ge(b_rstd, c + 1)
                if not begins(c):
                    dve.wait_ge(tr, c)
                for t in range(4):
                    v.tensor_scalar(YNC[:, t * 128:(t + 1) * 128], X[:, bass.ds((4 * c + t) * D, D)],
                                    MEAN[:, t:t + 1], RSC[:, t:t + 1], ALU.subtract, ALU.mult).then_inc(norm, 1)

            def scan_low(c):
                dve.wait_ge(hi, c + 1)
                v.tensor_tensor(YLO[:, ncols(c, CHUNK)], PA[:, :], YHI[:, ncols(c, CHUNK)], ALU.subtract
                                ).then_inc(lo, 1)

            add_values(0)
            dve.wait_ge(x1_done, 1)
            scan_stats(0)
            add_values(1)
            scan_norm(0)
            add_values(2)
            scan_low(0)
            add_values(3)
            dve.wait_ge(ld_vec, 16)
            v.tensor_copy(C, VEC[:, 4:5].broadcast_to([P, S])).then_inc(cell, 1)
            scan_stats(1)
            scan_norm(1)

            def scan_step(t):
                dve.wait_ge(acts, 3 * t + 2)
                v.tensor_tensor(IG, SG[1], SG[2], ALU.mult).then_inc(cell, 1)
                dve.wait_ge(acts, 3 * t + 3)
                v.tensor_tensor(C, SG[0], C, ALU.mult).then_inc(cell, 1)
                dve.wait_ge(cell, 3 * t + 3)
                v.tensor_tensor(C, C, IG, ALU.add).then_inc(cell, 1)

            def scan_pair(p, ahead=2):
                scan_step(2 * p)
                if ahead > 0:
                    scan_low(p + 1)
                if ahead > 1:
                    scan_stats(p + 2)
                scan_step(2 * p + 1)
                if ahead > 1:
                    scan_norm(p + 2)

            with dve.Fori(0, CHUNKS - 2) as p:
                scan_pair(p)
            scan_pair(CHUNKS - 2, 1)
            scan_pair(CHUNKS - 1, 0)

            cht = Chain(dve, t_stats)

            def add_cell(i, p):
                dve.wait_ge(ro_mm, i + 1)
                if not (isinstance(i, int) and i < 2):
                    dve.wait_ge(ro_tr, i)
                v.tensor_tensor(ROT[:, p * 512:(p + 1) * 512].rearrange("p (b s) -> p b s", b=2),
                                PAB[p][:, :].rearrange("p (b s) -> p b s", b=2),
                                CU.unsqueeze(1).broadcast_to([P, 2, S]), ALU.add).then_inc(ro_add, 1)

            def add_out(i, p):
                dve.wait_ge(ro_tr, i + 2)
                v.tensor_tensor(X[:, ncols(i, CHUNK)], X[:, ncols(i, CHUNK)], PS[:, p * 512:(p + 1) * 512], ALU.add
                                ).then_inc(ro_x, 1)

            def out_stats(i):
                dve.wait_ge(ro_x, i + 1)
                for t in range(4):
                    cht.did(v.bn_stats(BN[:, bass.ds((4 * i + t) * 6, 6)], X[:, bass.ds((4 * i + t) * D, D)]))

            dve.wait_ge(cu_cp, 1)
            add_cell(0, 0)
            add_cell(1, 1)
            add_out(0, 0)
            with dve.Fori(0, CHUNKS // 2 - 1) as k:
                for p in range(2):
                    add_cell(2 * k + p + 2, p)
                    out_stats(2 * k + p)
                    add_out(2 * k + p + 1, 1 - p)
            out_stats(CHUNKS - 2)
            add_out(CHUNKS - 1, 1)
            out_stats(CHUNKS - 1)
            cht.at(TILES)
            cht.settle()
            mean_variance(v, cht.did, cht.settle, BN, MV[:, 0:TILES], MV[:, TILES:], NMR[:, :]).then_inc(t_var, 1)

            dve.wait_ge(t_rstd, 1)

            def norm_sequence(b):
                if not begins(b):
                    dve.wait_ge(t_tr, b)
                for t in range(2):
                    at = 2 * b + t
                    v.tensor_scalar(OH2[:, t * 128:(t + 1) * 128], X[:, bass.ds(at * D, D)], MV[:, bass.ds(at, 1)],
                                    RS[:, bass.ds(at, 1)], ALU.subtract, ALU.mult).then_inc(t_norm, 1)

            def lo_sequence(b):
                dve.wait_ge(t_hi, b + 1)
                v.tensor_tensor(TL, PAS, TH, ALU.subtract).then_inc(t_lo, 1)

            def positions(b, gr):
                n = b * GROUPS + gr
                dve.wait_ge(qk_mm, n + 1)
                if not begins(b) or gr >= 2:
                    dve.wait_ge(stack, 2 * n - 2)
                v.tensor_tensor(QKF[gr % 2], qk_bank(b, gr), pos, ALU.add).then_inc(qk_pos, 1)

            def shift_q(b, gr):
                n = b * GROUPS + gr
                dve.wait_ge(m_tr, n + 1)
                if not begins(b) or gr >= 2:
                    dve.wait_ge(st_mm, n - 1)
                v.tensor_tensor(Q2[gr % 2], QS[gr], MTP, ALU.add).then_inc(q_shift, 1)

            def maxima(b, gr, bank):
                n = b * GROUPS + gr
                dve.wait_ge(s_mm, 3 * n + bank + 1)
                if bank == 0 and (not begins(b) or gr >= 2):
                    dve.wait_ge(m_tr, n - 1)
                col, k = ((0, 128), (4, 256), (6, 256))[bank]
                v.tensor_reduce(M2[gr % 2][:, 32 * col:32 * (col + 512 // k):32], PS[:, bank * 512:(bank + 1) * 512].rearrange(
                    "p (j k) -> p j k", k=k), AX.X, ALU.max).then_inc(s_max, 1)

            def normalise_o(b, gr, par):
                n = b * GROUPS + gr
                dve.wait_ge(u_tr, n + 1)
                if not begins(b) or gr > 0:
                    dve.wait_ge(o_norm, n)
                u = PBU.rearrange("p (t j c) -> p t j c", t=2, c=32)
                rd = RD[:, :].rearrange("p (t j) -> p t j", t=2)
                v.reciprocal(rd, u[:, :, :, HD]).then_inc(u_rec, 1)
                dve.wait_ge(u_rec, n + 1)
                o = OH[par].rearrange("p (t g j c) -> p t g j c", t=2, g=4, c=HD)[:, :, gr, :, :]
                v.tensor_tensor(o, u[:, :, :, 0:HD], rd.unsqueeze(3).broadcast_to([P, 2, 4, HD]), ALU.mult
                                ).then_inc(o_norm, 1)

            def add_o(b):
                dve.wait_ge(o_mm, b + 1)
                v.tensor_tensor(X[:, ncols(b, 256)], X[:, ncols(b, 256)], o_bank(b), ALU.add).then_inc(x3_done, 1)

            G4 = 4 * 8
            sig, sc, t1, t2 = (VP[:, k * 256:(k + 1) * 256] for k in range(4))
            t3, cw = YNC[:, 0:256], YNC[:, 256:512]
            gsc, rank, best, tot, rec = (BN[:, a:b] for a, b in ((0, 32), (32, 64), (64, 96), (96, 100), (100, 104)))
            ch = Chain(dve, g_chain)
            PER = 47

            def tiles4(ap):
                return ap.rearrange("p (t e) -> p t e", t=4)

            def op(ins):
                ch.did(ins)
                ch.settle()

            def prepare(c, step):
                if step == "stats":
                    ch.at(PER * c)
                    for t in range(4):
                        ch.did(v.bn_stats(BNC[:, t * 6:(t + 1) * 6], X[:, bass.ds((4 * c + t) * D, D)]))
                elif step == "variance":
                    ch.settle()
                    mean_variance(v, ch.did, ch.settle, BNC, MEAN, VAR, SPREAD).then_inc(c_var, 1)
                elif step == "normalise":
                    dve.wait_ge(c_rstd, c + 1)
                    for t in range(4):
                        v.tensor_scalar(YNC[:, t * 128:(t + 1) * 128], X[:, bass.ds((4 * c + t) * D, D)],
                                        MEAN[:, t:t + 1], RSC[:, t:t + 1], ALU.subtract, ALU.mult).then_inc(c_norm, 1)
                elif step == "low":
                    dve.wait_ge(c_hi, c + 1)
                    v.tensor_tensor(YLO[:, ncols(c, CHUNK)], PA[:, :], YHI[:, ncols(c, CHUNK)], ALU.subtract
                                    ).then_inc(c_lo, 1)
                elif step == "sigmoid":
                    dve.wait_ge(g_tr, c + 1)
                    v.tensor_scalar(tiles4(t1), tiles4(PA[:, :])[:, :, 0:NE], 1.0, None, ALU.add).then_inc(g_use, 1)
                    dve.wait_ge(g_use, c + 1)
                    op(v.reciprocal(sig, t1))
                elif step == "pairs":
                    op(v.tensor_tensor(tiles4(sc), tiles4(sig), BIAS[:, :].unsqueeze(1).broadcast_to([P, 4, NE]),
                                       ALU.add))
                    s8 = sc.rearrange("p (g k) -> p g k", k=8)
                    h1, l1 = (t1[:, k:k + 128].rearrange("p (g k) -> p g k", k=4) for k in (0, 128))
                    ch.did(v.tensor_tensor(h1, s8[:, :, 0:4], s8[:, :, 4:8], ALU.max))
                    ch.did(v.tensor_tensor(l1, s8[:, :, 0:4], s8[:, :, 4:8], ALU.min))
                elif step == "fours":
                    ch.settle()
                    h1, l1 = (t1[:, k:k + 128].rearrange("p (g k) -> p g k", k=4) for k in (0, 128))
                    h2, a2, b2 = (t2[:, k:k + 64].rearrange("p (g k) -> p g k", k=2) for k in (0, 64, 128))
                    ch.did(v.tensor_tensor(h2, h1[:, :, 0:2], h1[:, :, 2:4], ALU.max))
                    ch.did(v.tensor_tensor(a2, h1[:, :, 0:2], h1[:, :, 2:4], ALU.min))
                    op(v.tensor_tensor(b2, l1[:, :, 0:2], l1[:, :, 2:4], ALU.max))
                    ch.did(v.tensor_tensor(a2, a2, b2, ALU.max))
                elif step == "groups":
                    ch.settle()
                    h2, a2 = (t2[:, k:k + 64].rearrange("p (g k) -> p g k", k=2) for k in (0, 64))
                    h3, a3, b3 = t3[:, 0:32], t3[:, 32:64], t3[:, 64:96]
                    ch.did(v.tensor_tensor(h3, h2[:, :, 0], h2[:, :, 1], ALU.max))
                    ch.did(v.tensor_tensor(a3, h2[:, :, 0], h2[:, :, 1], ALU.min))
                    op(v.tensor_tensor(b3, a2[:, :, 0], a2[:, :, 1], ALU.max))
                    op(v.tensor_tensor(a3, a3, b3, ALU.max))
                    ch.did(v.tensor_tensor(gsc, h3, a3, ALU.add))
                elif step == "compare":
                    ch.settle()
                    gs = gsc.rearrange("p (t g) -> p t g", t=4)
                    other = gs.unsqueeze(2).broadcast_to([P, 4, 8, 8])
                    own = gs.unsqueeze(3).broadcast_to([P, 4, 8, 8])
                    ch.did(v.tensor_tensor(t1.rearrange("p (t g k) -> p t g k", t=4, k=8), other, own, ALU.is_gt))
                    op(v.tensor_tensor(t2.rearrange("p (t g k) -> p t g k", t=4, k=8), other, own, ALU.is_equal))
                    tri = CF[:, C_TRI:C_TRI + 64].unsqueeze(1).broadcast_to([P, 4, 64])
                    ch.did(v.tensor_tensor(tiles4(t2), tiles4(t2), tri, ALU.mult))
                elif step == "rank":
                    ch.settle()
                    op(v.tensor_tensor(t1, t1, t2, ALU.add))
                    ch.did(v.tensor_reduce(rank, t1.rearrange("p (g k) -> p g k", k=8), AX.X, ALU.add))
                elif step == "reach":
                    ch.settle()
                    op(v.tensor_scalar(rank, rank, 3.5, -BIG / 2, ALU.is_gt, ALU.mult))
                    ch.did(v.tensor_tensor(t3.rearrange("p (g k) -> p g k", k=8), sc.rearrange("p (g k) -> p g k", k=8),
                                           rank.unsqueeze(2).broadcast_to([P, G4, 8]), ALU.add))
                elif step == "best":
                    ch.settle()
                    ch.did(v.tensor_copy(tot, sig[:, 0:4]))
                    for t in range(4):
                        ch.did(v.max(best[:, t * 8:t * 8 + 8], t3[:, t * 64:(t + 1) * 64]))
                elif step == "replace":
                    ch.settle()
                    ch.did(v.tensor_copy(tot, sig[:, 0:4]))
                    for t in range(4):
                        ch.did(v.match_replace(t2[:, t * 64:(t + 1) * 64], best[:, t * 8:t * 8 + 8],
                                               t3[:, t * 64:(t + 1) * 64], -BIG))
                elif step == "chosen":
                    ch.settle()
                    op(v.tensor_tensor(t1, t2, t3, ALU.not_equal))
                    ch.did(v.tensor_tensor(t1, t1, sig, ALU.mult))
                elif step == "sum":
                    ch.settle()
                    op(v.tensor_reduce(tot, tiles4(t1), AX.X, ALU.add))
                    op(v.tensor_scalar(tot, tot, 1e-20, None, ALU.add))
                    ch.did(v.reciprocal(rec, tot))
                elif step == "weights":
                    ch.settle()
                    ch.did(v.scalar_tensor_tensor(tiles4(cw), tiles4(t1), ROUTED_SCALE,
                                                  rec.unsqueeze(2).broadcast_to([P, 4, NE]), ALU.mult, ALU.mult))
                elif step == "parts":
                    parts = CWS.rearrange("p (t k e) -> p t k e", t=4, k=2)
                    ch.settle()
                    op(v.tensor_copy(parts[:, :, 0, :], tiles4(cw)))
                    op(v.tensor_tensor(tiles4(t2), tiles4(cw), parts[:, :, 0, :], ALU.subtract))
                    v.tensor_scalar(parts[:, :, 1, :], tiles4(t2), LOW, None, ALU.mult).then_inc(g_cw, 1)
                    assert ch.n == PER, ch.n

            STEPS = ("stats", "variance", "normalise", "low", "sigmoid", "pairs", "fours", "groups", "compare",
                     "rank", "reach", "best", "replace", "chosen", "sum", "weights", "parts")

            def sequence(b, par, first, last):
                for gr in range(GROUPS):
                    ahead = (b, gr + 1) if gr < 3 else (b + 1, 0)
                    more = gr < 3 or not last
                    if more:
                        maxima(*ahead, 0)
                    shift_q(b, gr)
                    if gr == 0:
                        positions(b, 3)
                    elif not last:
                        positions(b + 1, gr - 1)
                    if gr == 0 and not last:
                        norm_sequence(b + 1)
                    if more:
                        maxima(*ahead, 1)
                        maxima(*ahead, 2)
                    if gr == 0 and not last:
                        lo_sequence(b + 1)
                    if gr >= 2:
                        normalise_o(b, gr - 2, par)
                    elif not first:
                        normalise_o(b - 1, gr + 2, 1 - par)
                    if gr == 3 and not first and not last:
                        add_o(b - 1)
                    if last and gr == 0:
                        prepare(0, "stats")
                        prepare(0, "variance")
                    if last and gr == 1:
                        dve.wait_ge(stack, 2 * 64)
                        prepare(0, "normalise")
                    if last and gr == 2:
                        prepare(0, "low")

            dve.wait_ge(zeroed, 8)
            dve.wait_ge(qk_split, 12)
            norm_sequence(0)
            lo_sequence(0)
            for gr in range(3):
                positions(0, gr)
            for bank in range(3):
                maxima(0, 0, bank)
            sequence(0, 0, True, False)
            dve.wait_ge(t_rstd, 2)
            with dve.Fori(0, 7) as k:
                sequence(2 * k + 1, 1, False, False)
                sequence(2 * k + 2, 0, False, False)
            sequence(15, 1, False, True)
            dve.wait_ge(ld_bias, 16)
            for step in ("sigmoid", "pairs", "fours"):
                prepare(0, step)
            normalise_o(15, 2, 1)
            for step in ("groups", "compare"):
                prepare(0, step)
            normalise_o(15, 3, 1)
            add_o(14)
            prepare(0, "rank")
            add_o(15)

            def product(c, u):
                n = c * UNITS + u
                dve.wait_ge(e_silu, n + 1)
                dve.wait_ge(e_up, n + 1)
                if u < PAIRS:
                    v.tensor_tensor(SIL[u % 2], SIL[u % 2], EU[u % 2], ALU.mult).then_inc(e_act, 1)
                    dve.wait_ge(e_act, c * PAIRS + u + 1)
                    dve.wait_ge(e_cw, c * PAIRS + u + 1)
                if not (begins(c) and u < 3):
                    dve.wait_ge(e_lo, n - 2)
                v.tensor_tensor(PRF[u % 3], SIL[u % 2], EC[u % 2] if u < PAIRS else EU[u % 2], ALU.mult
                                ).then_inc(e_prod, 1)

            def add_sum(c):
                dve.wait_ge(y_tr, c + 1)
                v.tensor_tensor(X[:, ncols(c, CHUNK)], X[:, ncols(c, CHUNK)], PA[:, :], ALU.add).then_inc(x4_done, 1)

            def body(c, last):
                for u in range(4, UNITS):
                    product(c, u)
                    if not last:
                        for step in STEPS:
                            if u == PREP[step]:
                                prepare(c + 1, step)

            for step in STEPS[STEPS.index("reach"):]:
                prepare(0, step)
            for u in range(4):
                product(0, u)
            with dve.Fori(0, CHUNKS - 1) as c:
                body(c, False)
                for u in range(4):
                    product(c + 1, u)
                add_sum(c)
            body(CHUNKS - 1, True)
            add_sum(CHUNKS - 1)


def kernel(**inputs):
    import numpy as np
    import concourse.bacc as bacc
    from concourse.bass_utils import run_bass_kernel_spmd

    a = {k: np.ascontiguousarray(v) for k, v in inputs.items()}
    f32 = np.float32

    gate = np.zeros((D, P), f32)
    gate[:, :NE] = a["L1_ffn_gate_w"].T
    mats = {
        WF: a["L0_ffn_wf"].T, WI: a["L0_ffn_wi"].T, WC: a["L0_ffn_wc"].T, WO: a["L0_ffn_wo"].T,
        WV1: a["L1_attn_Wv"], GW: gate, WV0: a["L0_attn_w_qkv"][2 * D:].T, WO0: a["L0_attn_w_o"].T,
        UF: a["L0_ffn_uf"].T, UI: a["L0_ffn_ui"].T, UC: a["L0_ffn_uc"].T, UO: a["L0_ffn_uo"].T,
        WO1: a["L1_attn_Wo"], WQ: a["L1_attn_Wq"], WK: a["L1_attn_Wk"],
    }
    small = np.ascontiguousarray(np.stack([mats[k] for k in range(15)], axis=1))
    vec = np.ascontiguousarray(np.stack([a[f"L0_ffn_{k}"] for k in ("bf", "bi", "bc", "bo", "in_c")], axis=1))
    gu = np.zeros((D, UNITS, 2, 2, FF), f32)
    wd = np.zeros((2, FF, UNITS, D), f32)
    for k, name in enumerate(("gate", "up")):
        gu[:, :PAIRS, k] = a[f"L1_ffn_We_{name}"].reshape(PAIRS, 2, D, FF).transpose(2, 0, 1, 3)
        gu[:, PAIRS, k, 0] = a[f"L1_ffn_Ws_{name}"]
    wd[:, :, :PAIRS] = a["L1_ffn_We_down"].reshape(PAIRS, 2, FF, D).transpose(1, 2, 0, 3)
    wd[0, :, PAIRS] = a["L1_ffn_Ws_down"]
    gu, wd = gu.reshape(D, UNITS, 256), wd.reshape(P, UNITS, D)

    cf = np.zeros((P, C_END), f32)
    cf[:, C_ID:C_ID + 128] = np.eye(P, dtype=f32)
    scale = 1.0 / (np.power(f32(10000.0), np.arange(0, HD, 2, dtype=f32) / f32(HD)) + np.finfo(f32).eps)
    angle = np.arange(S, dtype=f32)[:, None] * scale.astype(f32)[None, :]
    pos = np.stack([np.sin(angle), np.cos(angle)], axis=-1).reshape(S, HD).astype(f32)
    slot = np.arange(P) % 32
    for p in range(P):
        if slot[p] >= 8:
            cf[p, C_POS:C_POS + 256] = pos[:, p % 8]
            cf[p, C_POS + 256:C_POS + 512] = pos[:, p % 8]
    cf[slot == 0, C_POS + 256:C_POS + 512] = 1.0
    cf[(slot >= 16) & (slot < 24), C_QLO] = 1.0
    cf[slot >= 24, C_KLO] = 1.0
    cf[:, C_TRI:C_TRI + 64] = np.tril(np.ones((8, 8), f32), -1).reshape(1, 64)
    cf[np.arange(P), C_SUM + slot % B] = slot < B
    cb = np.zeros((P, 256), np.dtype(mybir.dt.np(BF16)))
    cb[:, :128] = np.eye(P)
    cb[:, 128:] = np.triu(np.full((P, P), -BIG, f32), 1)
    ch = np.zeros((P, PAIRS + 1, P), np.float16)
    for u in range(PAIRS):
        for k in range(2):
            ch[2 * u + k, u, k * FF:(k + 1) * FF] = 1.0
            ch[NE + 2 * u + k, u, k * FF:(k + 1) * FF] = 1.0 / LOW
    ch[:, PAIRS] = np.eye(P)
    ch = ch.reshape(P, (PAIRS + 1) * P)

    nc = bacc.Bacc("TRN2", target_bir_lowering=False, num_devices=1)
    arrays, args = {}, []
    for name, arr in (("x", a["L0_attn_x"]), ("small", small), ("vec", vec), ("gate_bias", a["L1_ffn_gate_bias"]),
                      ("gu", gu), ("wd", wd), ("cf32", cf), ("cbf", cb), ("cf16", ch)):
        arr = np.ascontiguousarray(arr)
        arrays[name] = arr
        args.append(nc.dram_tensor(name, arr.shape, mybir.dt.from_np(arr.dtype), kind="ExternalInput").ap())
    args.append(nc.dram_tensor("out", (B, S, D), F32, kind="ExternalOutput").ap())
    two_layers(nc, *args)
    r = run_bass_kernel_spmd(nc, [arrays], core_ids=[0])
    return r.results[0]["out"]
```
